# Optimizing a Trainium2 kernel written in Bass

```python
import numpy as np
import jax
import jax.numpy as jnp

def _softmax(x, axis=-1):
    return jax.nn.softmax(x, axis=axis)

def _gelu(x):
    return jax.nn.gelu(x, approximate=True)

def _silu(x):
    return jax.nn.silu(x)

def _sigmoid(x):
    return jax.nn.sigmoid(x)

def _layernorm(x, axis=-1, eps=1e-05):
    m = jnp.mean(x, axis=axis, keepdims=True)
    v = jnp.var(x, axis=axis, keepdims=True)
    return (x - m) / jnp.sqrt(v + eps)

def _scatter_add(tgt, idx, src, axis=0):
    return tgt.at[idx].add(src)

def _segment_sum(src, seg, n):
    return jax.ops.segment_sum(src, seg, n)
kernel_name = 'mk_seq_preln_d1_jaxref_r8_05b1f2'

def setup_inputs(seed: int=0):
    np.random.seed(seed)
    _w = jnp.asarray

    def _L0_attn_setup():
        import jax, jax.numpy as jnp
        import numpy as np
        H = 16
        CHUNK = 64
        EPS = 1e-05

        def _forward(x, wq, wk, wv, wo, fq1_w, fq1_b, fq2_w, fq2_b, fk1_w, fk1_b, fk2_w, fk2_b, norm_w):
            B, L, D = x.shape
            dk = D // H

            def proj(w):
                return (x @ w.T).reshape(B, L, H, dk).transpose(0, 2, 1, 3)
            q, k, v = (proj(wq), proj(wk), proj(wv))
            q = (q @ fq1_w.T + fq1_b) * (q @ fq2_w.T + fq2_b)
            k = (k @ fk1_w.T + fk1_b) * (k @ fk2_w.T + fk2_b)
            scale = dk ** (-0.5)
            n = L // CHUNK
            qc = q.reshape(B, H, n, CHUNK, dk) * scale
            kc = k.reshape(B, H, n, CHUNK, dk)
            vc = v.reshape(B, H, n, CHUNK, dk)
            kv = jnp.einsum('bhncd,bhnce->bhnde', kc, vc)
            kv = jnp.cumsum(kv, axis=2)
            kv = jnp.concatenate([jnp.zeros_like(kv[:, :, :1]), kv[:, :, :-1]], axis=2)
            inter = jnp.einsum('bhncd,bhnde->bhnce', qc, kv)
            s = jnp.einsum('bhncd,bhnmd->bhncm', qc, kc)
            mask = jnp.tril(jnp.ones((CHUNK, CHUNK), bool))
            s = jnp.where(mask, s, 0.0)
            intra = jnp.einsum('bhncm,bhnmd->bhncd', s, vc)
            o = (inter + intra).reshape(B, H, L, dk)
            o = o * jax.lax.rsqrt(jnp.mean(o * o, axis=-1, keepdims=True) + EPS) * norm_w
            o = o.transpose(0, 2, 1, 3).reshape(B, L, D)
            return o @ wo.T
        key = jax.random.key(seed)
        ks = jax.random.split(key, 16)
        B, L, D = (2, 512, 256)
        dk = D // H
        g = 2 ** (-2.5)

        def xav(k, n):
            lim = g * np.sqrt(6.0 / (2 * n))
            return jax.random.uniform(k, (n, n), jnp.float32, -lim, lim)
        return {'x': jax.random.normal(ks[0], (B, L, D), jnp.float32), 'wq': xav(ks[1], D), 'wk': xav(ks[2], D), 'wv': xav(ks[3], D), 'wo': xav(ks[4], D), 'fq1_w': xav(ks[5], dk), 'fq1_b': jnp.zeros((dk,), jnp.float32), 'fq2_w': xav(ks[6], dk), 'fq2_b': jnp.zeros((dk,), jnp.float32), 'fk1_w': xav(ks[7], dk), 'fk1_b': jnp.zeros((dk,), jnp.float32), 'fk2_w': xav(ks[8], dk), 'fk2_b': jnp.zeros((dk,), jnp.float32), 'norm_w': jnp.ones((dk,), jnp.float32)}
    _L0_attn_in = _L0_attn_setup()

    def _L0_ffn_setup():
        import jax, jax.numpy as jnp
        import numpy as np
        H = 256
        M = 176
        E = 32
        TOPK = 6
        G = 8
        TOPK_G = 4
        SH = 2
        B, S = (1, 128)
        key = jax.random.key(seed)
        ks = jax.random.split(key, 9)
        sc = 0.02
        return {'x': jax.random.normal(ks[0], (B, S, H), dtype=jnp.float32), 'w_router': jax.random.normal(ks[1], (H, E), dtype=jnp.float32) * sc, 'corr_bias': jax.random.normal(ks[2], (E,), dtype=jnp.float32) * 0.1, 'gate_w': jax.random.normal(ks[3], (E, H, M), dtype=jnp.float32) * sc, 'up_w': jax.random.normal(ks[4], (E, H, M), dtype=jnp.float32) * sc, 'down_w': jax.random.normal(ks[5], (E, M, H), dtype=jnp.float32) * sc, 'sh_gate_w': jax.random.normal(ks[6], (H, M * SH), dtype=jnp.float32) * sc, 'sh_up_w': jax.random.normal(ks[7], (H, M * SH), dtype=jnp.float32) * sc, 'sh_down_w': jax.random.normal(ks[8], (M * SH, H), dtype=jnp.float32) * sc}
    _L0_ffn_in = _L0_ffn_setup()
    _d = {'L0_attn_x': _L0_attn_in['x'], 'L0_attn_wq': _L0_attn_in['wq'], 'L0_attn_wk': _L0_attn_in['wk'], 'L0_attn_wv': _L0_attn_in['wv'], 'L0_attn_wo': _L0_attn_in['wo'], 'L0_attn_fq1_w': _L0_attn_in['fq1_w'], 'L0_attn_fq1_b': _L0_attn_in['fq1_b'], 'L0_attn_fq2_w': _L0_attn_in['fq2_w'], 'L0_attn_fq2_b': _L0_attn_in['fq2_b'], 'L0_attn_fk1_w': _L0_attn_in['fk1_w'], 'L0_attn_fk1_b': _L0_attn_in['fk1_b'], 'L0_attn_fk2_w': _L0_attn_in['fk2_w'], 'L0_attn_fk2_b': _L0_attn_in['fk2_b'], 'L0_attn_norm_w': _L0_attn_in['norm_w'], 'L0_ffn_w_router': _L0_ffn_in['w_router'], 'L0_ffn_corr_bias': _L0_ffn_in['corr_bias'], 'L0_ffn_gate_w': _L0_ffn_in['gate_w'], 'L0_ffn_up_w': _L0_ffn_in['up_w'], 'L0_ffn_down_w': _L0_ffn_in['down_w'], 'L0_ffn_sh_gate_w': _L0_ffn_in['sh_gate_w'], 'L0_ffn_sh_up_w': _L0_ffn_in['sh_up_w'], 'L0_ffn_sh_down_w': _L0_ffn_in['sh_down_w']}
    _x0 = _d['L0_attn_x']
    _d['L0_attn_x'] = jax.random.normal(jax.random.fold_in(jax.random.key(seed), 1), (2, 2048, 256), dtype=_x0.dtype)
    del _x0
    return _d

def reference(L0_attn_x, L0_attn_wq, L0_attn_wk, L0_attn_wv, L0_attn_wo, L0_attn_fq1_w, L0_attn_fq1_b, L0_attn_fq2_w, L0_attn_fq2_b, L0_attn_fk1_w, L0_attn_fk1_b, L0_attn_fk2_w, L0_attn_fk2_b, L0_attn_norm_w, L0_ffn_w_router, L0_ffn_corr_bias, L0_ffn_gate_w, L0_ffn_up_w, L0_ffn_down_w, L0_ffn_sh_gate_w, L0_ffn_sh_up_w, L0_ffn_sh_down_w):

    def _L0_attn_ref(x, wq, wk, wv, wo, fq1_w, fq1_b, fq2_w, fq2_b, fk1_w, fk1_b, fk2_w, fk2_b, norm_w):
        import jax, jax.numpy as jnp
        import numpy as np
        H = 16
        CHUNK = 64
        EPS = 1e-05

        def _forward(x, wq, wk, wv, wo, fq1_w, fq1_b, fq2_w, fq2_b, fk1_w, fk1_b, fk2_w, fk2_b, norm_w):
            B, L, D = x.shape
            dk = D // H

            def proj(w):
                return (x @ w.T).reshape(B, L, H, dk).transpose(0, 2, 1, 3)
            q, k, v = (proj(wq), proj(wk), proj(wv))
            q = (q @ fq1_w.T + fq1_b) * (q @ fq2_w.T + fq2_b)
            k = (k @ fk1_w.T + fk1_b) * (k @ fk2_w.T + fk2_b)
            scale = dk ** (-0.5)
            n = L // CHUNK
            qc = q.reshape(B, H, n, CHUNK, dk) * scale
            kc = k.reshape(B, H, n, CHUNK, dk)
            vc = v.reshape(B, H, n, CHUNK, dk)
            kv = jnp.einsum('bhncd,bhnce->bhnde', kc, vc)
            kv = jnp.cumsum(kv, axis=2)
            kv = jnp.concatenate([jnp.zeros_like(kv[:, :, :1]), kv[:, :, :-1]], axis=2)
            inter = jnp.einsum('bhncd,bhnde->bhnce', qc, kv)
            s = jnp.einsum('bhncd,bhnmd->bhncm', qc, kc)
            mask = jnp.tril(jnp.ones((CHUNK, CHUNK), bool))
            s = jnp.where(mask, s, 0.0)
            intra = jnp.einsum('bhncm,bhnmd->bhncd', s, vc)
            o = (inter + intra).reshape(B, H, L, dk)
            o = o * jax.lax.rsqrt(jnp.mean(o * o, axis=-1, keepdims=True) + EPS) * norm_w
            o = o.transpose(0, 2, 1, 3).reshape(B, L, D)
            return o @ wo.T
        return _forward(x, wq, wk, wv, wo, fq1_w, fq1_b, fq2_w, fq2_b, fk1_w, fk1_b, fk2_w, fk2_b, norm_w)

    def _L0_ffn_ref(x, w_router, corr_bias, gate_w, up_w, down_w, sh_gate_w, sh_up_w, sh_down_w):
        import jax, jax.numpy as jnp
        import numpy as np
        H = 256
        M = 176
        E = 32
        TOPK = 6
        G = 8
        TOPK_G = 4
        SH = 2
        B, S = (1, 128)
        b, s, h = x.shape
        xf = x.reshape(-1, h)
        T = xf.shape[0]
        logits = xf @ w_router
        scores = jax.nn.sigmoid(logits)
        sfc = scores + corr_bias
        grp = sfc.reshape(T, G, E // G)
        top2, _ = jax.lax.top_k(grp, 2)
        group_scores = top2.sum(-1)
        _, gidx = jax.lax.top_k(group_scores, TOPK_G)
        group_mask = jax.nn.one_hot(gidx, G, dtype=jnp.float32).sum(axis=1) > 0
        score_mask = jnp.repeat(group_mask, E // G, axis=1)
        masked = jnp.where(score_mask, sfc, -jnp.inf)
        _, topk_idx = jax.lax.top_k(masked, TOPK)
        topk_w = jnp.take_along_axis(scores, topk_idx, axis=1)
        combine = jnp.zeros((T, E), dtype=x.dtype).at[jnp.arange(T)[:, None], topk_idx].add(topk_w)
        g = jnp.einsum('th,ehm->etm', xf, gate_w)
        u = jnp.einsum('th,ehm->etm', xf, up_w)
        eo = jnp.einsum('etm,emh->eth', jax.nn.silu(g) * u, down_w)
        routed = jnp.einsum('te,eth->th', combine, eo)
        shared = jax.nn.silu(xf @ sh_gate_w) * (xf @ sh_up_w) @ sh_down_w
        return (routed + shared).reshape(b, s, h)
    x = L0_attn_x
    x = x + _L0_attn_ref(_layernorm(x, axis=-1), L0_attn_wq, L0_attn_wk, L0_attn_wv, L0_attn_wo, L0_attn_fq1_w, L0_attn_fq1_b, L0_attn_fq2_w, L0_attn_fq2_b, L0_attn_fk1_w, L0_attn_fk1_b, L0_attn_fk2_w, L0_attn_fk2_b, L0_attn_norm_w)
    x = x + _L0_ffn_ref(_layernorm(x, axis=-1), L0_ffn_w_router, L0_ffn_corr_bias, L0_ffn_gate_w, L0_ffn_up_w, L0_ffn_down_w, L0_ffn_sh_gate_w, L0_ffn_sh_up_w, L0_ffn_sh_down_w)
    return x

_drawn_inputs = setup_inputs


def setup_inputs(seed=0):
    import zlib

    import numpy as np

    out = dict(_drawn_inputs(seed))
    spreads = {'L0_attn_fq1_b': (0.0, 0.1),
     'L0_attn_fq2_b': (0.0, 0.1),
     'L0_attn_fk1_b': (0.0, 0.1),
     'L0_attn_fk2_b': (0.0, 0.283),
     'L0_attn_norm_w': (1.0, 0.6)}
    factors = {'L0_attn_fq2_w': 3.85,
     'L0_attn_fk1_w': 3.406,
     'L0_ffn_w_router': 4.168,
     'L0_ffn_corr_bias': 3.532,
     'L0_ffn_gate_w': 2.969,
     'L0_ffn_up_w': 2.94,
     'L0_ffn_down_w': 2.942,
     'L0_ffn_sh_gate_w': 2.901,
     'L0_ffn_sh_up_w': 2.858,
     'L0_ffn_sh_down_w': 2.857}
    for name, (base, spread) in spreads.items():
        noise = np.random.default_rng([zlib.crc32(name.encode()), seed]).standard_normal(out[name].shape)
        drawn = base * np.exp(spread * noise) if base else spread * noise
        out[name] = jnp.asarray(drawn.astype(out[name].dtype))
    for name, factor in factors.items():
        out[name] = (out[name] * factor).astype(out[name].dtype)
    return out
```

```python
from contextlib import ExitStack

import numpy as np

import concourse.bass as bass
from concourse import mybir

F32 = mybir.dt.float32
BF16 = mybir.dt.bfloat16
I32 = mybir.dt.int32
U32 = mybir.dt.uint32
ALU = mybir.AluOpType
ACT = mybir.ActivationFunctionType
AX_X = mybir.AxisListType.X

P = 128
B, L, D = 2, 2048, 256
T = B * L
H, DK, CHUNK = 16, 16, 64
KD = D // P
PAIRS = H // 2
SPAN = 256
NCH = SPAN // CHUNK
ST = SPAN // P
NSPAN = L // SPAN
E, M, TOPK, G, TOPK_G = 32, 176, 6, 8, 4
EG = E // G
MH = M // 2
MS = 2 * M
EPS = 1e-5
SCALE = DK ** -0.5
REGION = T + P
ROW = D + 1
NROWS = E * REGION + P
NTILES = (T * TOPK + E * (P - 1)) // P
UNROLL = 4
NT = -(-NTILES // UNROLL) * UNROLL
WIDE = 2 * M + 1
BIG = 3.0e38
MARK = 3.3e38
SP_TOK = 512
FREE = 1
ROUTE_LINKS = 19


def moe_block_kernel(nc, x, wq, wk, wv, wo, fq1_w, fq1_b, fq2_w, fq2_b, fk1_w, fk1_b, fk2_w, fk2_b,
                     norm_w, w_router, corr_bias, gate_w, up_w, down_w, sh_gate_w, sh_up_w,
                     sh_down_w, out):
    rows_d = nc.dram_tensor("rows_d", [NROWS, ROW], F32)
    x2_d = nc.dram_tensor("x2_d", [T, D], F32)
    x2nT_d = nc.dram_tensor("x2nT_d", [P, KD, T], F32)
    acc_d = [nc.dram_tensor(f"acc{n}_d", [T + P, D], F32) for n in range(2)]

    with ExitStack() as ctx:
        def sb(name, shape, dt=F32, stack=ctx):
            return stack.enter_context(nc.sbuf_tensor(name, shape, dt))

        def sem(name):
            return ctx.enter_context(nc.semaphore(name))

        def sems(name, n=2):
            return [sem(f"{name}{k}") for k in range(n)]

        ident = sb("ident", [P, P])
        wgu = sb("wgu", [P, E, KD, WIDE])
        wr = sb("wr", [P, KD, E])
        shg = sb("shg", [P, KD, MS])
        shu = sb("shu", [P, KD, MS])
        shd = sb("shd", [P, 3, D])
        next_row = sb("next_row", [P, E])
        first_row = sb("first_row", [P, E])
        zeros = sb("zeros", [P, D])
        part_i = sb("part_i", [P, 1], I32)
        part_f = sb("part_f", [P, 1])

        scattered = sems("scattered")
        gu_loaded = sem("gu_loaded")
        sh_loaded = sem("sh_loaded")
        router_cols = sem("router_cols")
        passed = sem("passed")

        phase_a(nc, ctx, sb, sem, sems, locals())
        phase_b(nc, ctx, sb, sem, sems, locals())


def bc(ap, axis, n):
    ap = ap.unsqueeze(axis)
    shape = list(ap.shape)
    shape[axis] = n
    return ap.to_broadcast(shape)


def apart(eng, sem, value, passed):
    eng.wait_ge(sem, value)
    eng.sem_inc(passed, 1)


def phase_a(nc, ctx, sb, sem, sems, g):
    x, rows_d, x2_d, x2nT_d = g["x"], g["rows_d"], g["x2_d"], g["x2nT_d"]
    ident, wgu, wr, next_row, first_row, zeros = (
        g[k] for k in ("ident", "wgu", "wr", "next_row", "first_row", "zeros"))
    scattered, gu_loaded, sh_loaded, router_cols, passed = (
        g[k] for k in ("scattered", "gu_loaded", "sh_loaded", "router_cols", "passed"))
    with ExitStack() as own:
        def t2(name, shape, dt=F32):
            return [sb(f"{name}{b}", shape, dt, own) for b in range(2)]

        def t1(name, shape, dt=F32):
            return sb(name, shape, dt, own)

        ones128 = t1("ones128", [P, P])
        hblock = t1("hblock", [P, 8, DK])
        kvmask = t1("kvmask", [P, P])
        hmean = t1("hmean", [P, P])
        cmask = t1("cmask", [P, 2, CHUNK])
        tri = t1("tri", [P, P], BF16)
        onesb = t1("onesb", [P, P], BF16)
        even_odd = t1("even_odd", [P, 2])
        eps_col = t1("eps_col", [P, 1])
        ids = t1("ids", [P, T // P], I32)
        first_i = t1("first_i", [P, E], I32)
        cbias = t1("cbias", [P, E])
        rep16 = t1("rep16", [DK, 8, DK])
        f4 = t1("f4", [DK, 69])
        rep = t1("rep", [P, 69])
        wqk = t1("wqk", [P, 4, KD, D])
        wvT = t1("wvT", [P, KD, 2, P])
        woT = t1("woT", [P, KD, D])
        xt = t2("xt", [P, ST, D])
        bst = t2("bst", [P, ST, 6])
        mv = t2("mv", [P, ST, 2])
        std = t2("std", [P, ST])
        rstd = t2("rstd", [P, ST])
        xn = t2("xn", [P, ST, D])
        xnT = t2("xnT", [P, KD, SPAN])
        a1 = t1("a1", [P, 4, SPAN])
        ktmp = t2("ktmp", [P, 2, SPAN])
        qT = t2("qT", [P, 2, SPAN])
        kbd = t2("kbd", [P, 2, NCH, 2, CHUNK])
        vbd = t2("vbd", [P, NCH, PAIRS, 2, DK])
        ktok = t2("ktok", [P, NCH, 2, P])
        sT_all = t1("sT_all", [P, 2, 2, 4, 2, CHUNK])
        sT = [[sT_all[:, c, b, :, :, :] for b in range(2)] for c in range(2)]
        kvm = t2("kvm", [P, 2, P])
        sq = t2("sq", [P, 2, SPAN])
        ostd = t2("ostd", [P, 2, SPAN])
        nat = sT_all[:].rearrange("p c b q f m -> p (c b q f m)").rearrange(
            "p (n r d) -> p n r d", n=4, r=KD)
        gsb = sq[0][:].rearrange("p f (h c) -> p (f h) c", c=P)
        fmap = sq[1][:].rearrange("p f (h c) -> p (f h) c", c=P)
        orstd = t1("orstd", [P, 2, SPAN])
        oT = t2("oT", [P, 2, SPAN])
        x2 = t2("x2", [P, ST, D])
        bst2 = t2("bst2_", [P, ST, 6])
        mv2 = t2("mv2_", [P, ST, 2])
        std2 = t2("std2_", [P, ST])
        rstd2 = t2("rstd2_", [P, ST])
        xp = t2("xp", [P, ST, ROW])
        x2nT = t2("x2nT", [P, KD, SPAN])
        NB = 2 * ST
        score = t1("score", [P, NB, E])
        sfc = t1("sfc", [P, NB * G, EG])
        hi2 = t1("hi2", [P, NB * G, 2])
        lo2 = t1("lo2", [P, NB * G, 2])
        top1 = t1("top1", [P, NB * G])
        mid = t1("mid", [P, NB * G])
        top2 = t1("top2", [P, NB * G])
        gsc = t1("gsc", [P, NB, G])
        gtop = t1("gtop", [P, NB, 8])
        gpick = t1("gpick", [P, NB, 8])
        gmark = t1("gmark", [P, NB, G])
        gneg = t1("gneg", [P, NB * G])
        masked = t1("masked", [P, NB, E])
        etop = t1("etop", [P, NB, 8])
        epick = t1("epick", [P, NB, 8])
        emark = t1("emark", [P, NB, E])
        chosen = t1("chosen", [P, NB, E], BF16)
        slot = t1("slot", [P, NB, E])
        slotm = t1("slotm", [P, NB, E])
        stop8 = t1("stop8", [P, NB, 8])
        slots = t1("slots", [P, NB, 8], U32)

        pg = own.enter_context(nc.psum_tensor("pg", [P, 4, 512], F32))
        pkv = own.enter_context(nc.psum_tensor("pkv", [P, 2, 512], F32))
        po = own.enter_context(nc.psum_tensor("po", [P, 2, 512], F32))

        attn_loaded = sem("attn_loaded")
        const_step = sem("const_step")
        consts_made = sem("consts_made")
        setup_pe = sem("setup_pe")
        setup_dve = sem("setup_dve")
        x_loaded, x_stats, x_aggr, x_std, x_rstd, xn_made = (
            sems(n) for n in ("x_loaded", "x_stats", "x_aggr", "x_std", "x_rstd", "xn_made"))
        xt_turned, xnT_made, proj_ready, a1_made, k_made, kbd_made, q_made = (
            sems(n) for n in ("xt_turned", "xnT_made", "proj_ready", "a1_made", "k_made", "kbd_made",
                              "q_made"))
        v_ready, vbd_made, kt_ready, ktok_made = (
            sems(n) for n in ("v_ready", "vbd_made", "kt_ready", "ktok_made"))
        s_ready = sem("s_ready")
        s_masked = sem("s_masked")
        kv_ready, kvm_made, o_ready, sq_made, ms_ready, ostd_made, orstd_made, oT_made = (
            sems(n) for n in ("kv_ready", "kvm_made", "o_ready", "sq_made", "ms_ready", "ostd_made",
                              "orstd_made", "oT_made"))
        y_ready, x2_made, x2_stored, x2_stats, x2_aggr, x2_std, x2_rstd, xp_made, id_made = (
            sems(n) for n in ("y_ready", "x2_made", "x2_stored", "x2_stats", "x2_aggr", "x2_std",
                              "x2_rstd", "xp_made", "id_made"))
        x2t_turned, x2nT_made, x2nT_stored = (
            sems(n) for n in ("x2t_turned", "x2nT_made", "x2nT_stored"))
        logit_ready = sem("logit_ready")
        score_made = sem("score_made")
        route_step = sem("route_step")
        chosen_made = sem("chosen_made")
        rank_ready = sem("rank_ready")
        slots_made = sem("slots_made")
        rank_read = sem("rank_read")
        dispatched = sems("dispatched")

        block = own.enter_context(nc.Block())

        def span(ap, b, i):
            return ap[bass.ds(b * L + i * SPAN, SPAN), :].rearrange("(t p) d -> p t d", p=P)

        x_rows = x.rearrange("b l d -> (b l) d")

        @block.sync
        def _(sp):
            for n, w in enumerate((g["wq"], g["wk"], g["wv"], g["wo"])):
                sp.dma_start(nat[:, n, :, :], w.rearrange("(r p) d -> p r d", p=P)).then_inc(attn_loaded, 16)
            for n, w in enumerate((g["fq1_w"], g["fq2_w"], g["fk1_w"], g["fk2_w"])):
                sp.dma_start(f4[:, n * DK:(n + 1) * DK], w).then_inc(attn_loaded, 16)
            for n, v in enumerate((g["fq1_b"], g["fq2_b"], g["fk1_b"], g["fk2_b"], g["norm_w"])):
                sp.dma_start(f4[:, 64 + n:65 + n], v.unsqueeze(1)).then_inc(attn_loaded, 16)
            sp.dma_start(cbias[:], g["corr_bias"].partition_broadcast(P)).then_inc(attn_loaded, 16)
            sp.dma_start(wr[:], g["w_router"].rearrange("(k p) e -> p k e", p=P)).then_inc(attn_loaded, 16)
            with sp.Fori(0, NSPAN) as i:
                for b in range(B):
                    sp.wait_ge(x2_made[b], FREE + i)
                    sp.dma_start(xt[b][:], span(x_rows, b, i)).then_inc(x_loaded[b], 16)
                for b in range(B):
                    sp.wait_ge(x2_made[b], FREE + i + 1)
                    sp.dma_start(span(x2_d, b, i), x2[b][:]).then_inc(x2_stored[b], 16)
                for b in range(B):
                    apart(sp, x2nT_made[b], FREE + i + 1, passed)
                    sp.dma_start(x2nT_d[:, :, bass.ds(b * L + i * SPAN, SPAN)], x2nT[b][:])\
                      .then_inc(x2nT_stored[b], 16)
            for b in range(B):
                sp.wait_ge(x2_stored[b], FREE + 16 * NSPAN)
                sp.wait_ge(x2nT_stored[b], FREE + 16 * NSPAN)

        @block.gpsimd
        def _(pool):
            for free in (*x2_made, *x2nT_stored, *x2_stored, *dispatched, *x2nT_made, score_made, rank_read, *oT_made):
                pool.sem_inc(free, FREE)
            n = 0

            def link(ins):
                nonlocal n
                n += 1
                ins.then_inc(const_step, 1)
                pool.wait_ge(const_step, n)

            def keep(t, pattern, base, mult, op=ALU.is_ge, fill=0.0):
                link(pool.affine_select(out=t, in_=t, compare_op=op, fill=fill, base=base,
                                        pattern=pattern, channel_multiplier=mult))

            link(pool.memset(ident[:], 0.0))
            keep(ident[:], [[-1, P]], 0, 1, ALU.not_equal, 1.0)
            link(pool.memset(ones128[:], 1.0))
            link(pool.memset(hblock[:], 1.0))
            keep(hblock[:], [[-DK, 8], [0, DK]], 0, 1)
            keep(hblock[:], [[DK, 8], [0, DK]], DK - 1, -1)
            for half in range(2):
                link(pool.memset(cmask[:, half, :], SCALE))
                keep(cmask[:, half, :], [[1, CHUNK]], CHUNK * half, -1)
            keep(cmask[:, 1, :], [[0, CHUNK]], -CHUNK, 1)
            link(pool.memset(tri[:], 1.0))
            keep(tri[:], [[1, P]], -1, -1)
            link(pool.memset(onesb[:], 1.0))
            link(pool.memset(zeros[:], 0.0))
            link(pool.memset(eps_col[:], EPS))
            link(pool.iota(ids[:], pattern=[[P, T // P]], base=0, channel_multiplier=1))
            link(pool.iota(first_i[:], pattern=[[REGION, E]], base=1, channel_multiplier=0))
            link(pool.iota(g["part_i"][:], pattern=[[0, 1]], base=0, channel_multiplier=1))
            for b in range(B):
                link(pool.memset(vbd[b][:], 0.0))
                link(pool.memset(kvm[b][:], 0.0))
            link(pool.memset(gpick[:], MARK))
            link(pool.memset(epick[:], MARK))
            pool.memset(a1[:, 0, 0:1], 0.0).then_inc(consts_made, 1)
            with pool.Fori(0, NSPAN) as i:
                apart(pool, slots_made, i + 1, passed)
                for b in range(B):
                    apart(pool, id_made[b], i + 1, passed)
                    for t in range(ST):
                        for k in range(TOPK):
                            pool.indirect_dma_start(
                                rows_d[:, :],
                                bass.IndirectOffsetOnAxis(ap=slots[:, b * ST + t, k:k + 1], axis=0),
                                xp[b][:, t, :], None).then_inc(scattered[b], 16)
                for b in range(B):
                    apart(pool, scattered[b], 16 * ST * TOPK * (i + 1), dispatched[b])
            for b in range(B):
                pool.wait_ge(scattered[b], 16 * ST * TOPK * NSPAN)

        @block.scalar
        def _(act):
            for k in range(KD):
                for w, at in ((g["gate_w"], 0), (g["up_w"], M + 1)):
                    act.dma_start(wgu[:, :, k, at:at + M],
                                  w[:, k * P:(k + 1) * P, :].rearrange("e p m -> p e m")).then_inc(gu_loaded, 16)
            act.dma_start(g["shg"][:], g["sh_gate_w"].rearrange("(k p) m -> p k m", p=P)).then_inc(sh_loaded, 16)
            act.dma_start(g["shu"][:], g["sh_up_w"].rearrange("(k p) m -> p k m", p=P)).then_inc(sh_loaded, 16)
            act.dma_start(g["shd"][:, 0:2, :], g["sh_down_w"][0:2 * P, :].rearrange("(k p) d -> p k d", p=P))\
               .then_inc(sh_loaded, 16)
            act.dma_start(g["shd"][0:MS - 2 * P, 2, :], g["sh_down_w"][2 * P:MS, :]).then_inc(sh_loaded, 16)
            act.wait_ge(consts_made, 1)
            act.wait_ge(setup_dve, 1)
            with act.Fori(0, NSPAN) as i:
                for b in range(B):
                    act.wait_ge(x_aggr[b], 2 * i + 2)
                    nc.scalar.activation(std[b][:], mv[b][:, :, 1], ACT.Sqrt, bias=eps_col[:, 0:1])\
                      .then_inc(x_std[b], 1)
                for b in range(B):
                    act.wait_ge(xt_turned[b], i + 1)
                    nc.scalar.activation(xnT[b][:], pg[:, b, :].rearrange("p (k t) -> p k t", k=KD), ACT.Copy)\
                      .then_inc(xnT_made[b], 1)
                for b in range(B):
                    for r in range(4):
                        act.wait_ge(proj_ready[b], 4 * i + r + 1)
                        nc.scalar.activation(a1[:, r, :], pg[:, (r + 2) % 4, 0:SPAN], ACT.Identity,
                                             bias=rep[:, 64 + 2 * (r // 2):65 + 2 * (r // 2)])\
                          .then_inc(a1_made[b], 1)
                for b in range(B):
                    act.wait_ge(v_ready[b], i + 1)
                    for a in range(2):
                        rows = slice(a * CHUNK, (a + 1) * CHUNK)
                        nc.scalar.activation(vbd[b][rows, :, :, a, :].rearrange("p c g e -> p (c g) e"),
                                             pg[rows, 2 + b, :].rearrange("p (c e) -> p c e", e=DK), ACT.Copy)\
                          .then_inc(vbd_made[b], 1)
                for b in range(B):
                    for half in range(2):
                        act.wait_ge(kt_ready[b], 2 * i + half + 1)
                        nc.scalar.activation(ktok[b][:, 2 * half:2 * half + 2, :, :].rearrange("p c f e -> p (c f e)"),
                                             pg[:, 2 * b + half, :], ACT.Copy).then_inc(ktok_made[b], 1)
                for b in range(B):
                    act.wait_ge(o_ready[b], NCH * (i + 1))
                    nc.scalar.activation(sq[b][:].rearrange("p f t -> p (f t)"), po[:, b, :], ACT.Square)\
                      .then_inc(sq_made[b], 1)
                for b in range(B):
                    act.wait_ge(ms_ready[b], i + 1)
                    nc.scalar.activation(ostd[b][:].rearrange("p f t -> p (f t)"), pg[:, b, :], ACT.Sqrt,
                                         bias=eps_col[:, 0:1]).then_inc(ostd_made[b], 1)
                for b in range(B):
                    act.wait_ge(x2_aggr[b], 2 * i + 2)
                    nc.scalar.activation(std2[b][:], mv2[b][:, :, 1], ACT.Sqrt, bias=eps_col[:, 0:1])\
                      .then_inc(x2_std[b], 1)
                for b in range(B):
                    act.wait_ge(x2t_turned[b], i + 1)
                    act.wait_ge(x2nT_stored[b], FREE + 16 * i)
                    nc.scalar.activation(x2nT[b][:], pg[:, b, :].rearrange("p (k t) -> p k t", k=KD), ACT.Copy)\
                      .then_inc(x2nT_made[b], 1)
                act.wait_ge(logit_ready, i + 1)
                nc.scalar.activation(score[:].rearrange("p n e -> p (n e)"), pg[:, 2, 0:NB * E], ACT.Sigmoid)\
                  .then_inc(score_made, 1)

        @block.vector
        def _(dve):
            n = 0

            def link(ins):
                nonlocal n
                n += 1
                ins.then_inc(route_step, 1)
                dve.wait_ge(route_step, n)

            dve.wait_ge(consts_made, 1)
            link(nc.vector.tensor_copy(rep16[:], bc(ident[0:DK, 0:DK], 1, 8)))
            link(nc.vector.tensor_scalar(kvmask[:], hblock[:].rearrange("p h d -> p (h d)"), SCALE, None, ALU.mult))
            link(nc.vector.tensor_scalar(hmean[:], hblock[:].rearrange("p h d -> p (h d)"), 1.0 / DK, None, ALU.mult))
            link(nc.vector.tensor_reduce(even_odd[:], hblock[:, :, 0].rearrange("p (g a) -> p a g", a=2),
                                         AX_X, ALU.add))
            link(nc.vector.tensor_scalar(cmask[:, 0, :], cmask[:, 0, :], 1.0, None, ALU.mult))
            link(nc.vector.tensor_tensor(cmask[:, 0, :], cmask[:, 0, :], cmask[:, 1, :], ALU.max))
            link(nc.vector.tensor_copy(first_row[:], first_i[:]))
            link(nc.vector.tensor_copy(next_row[:], first_i[:]))
            link(nc.vector.tensor_copy(g["part_f"][:], g["part_i"][:]))
            nc.vector.memset(ktmp[0][:, 0, 0:1], 0.0).then_inc(setup_dve, 1)
            dve.wait_ge(setup_pe, 1)
            link(nc.vector.tensor_copy(rep[:], pg[:, 0, 0:69]))
            for m in range(4):
                link(nc.vector.tensor_tensor(gsb[:, m, :].rearrange("p (h d) -> p h d", d=DK),
                                             bc(rep[:, m * DK:(m + 1) * DK], 1, 8), hblock[:], ALU.mult))
            nc.vector.memset(ktmp[0][:, 0, 1:2], 0.0).then_inc(setup_dve, 1)
            dve.wait_ge(setup_pe, 2)
            link(nc.vector.tensor_copy(fmap.rearrange("p m c -> p (m c)"), pg[:, 1, :]))
            for k in range(KD):
                for a in range(2):
                    link(nc.vector.tensor_copy(
                        wvT[:, k, a, :].rearrange("p (h e) -> p h e", e=DK),
                        pg[:, 2, k * D:(k + 1) * D].rearrange("p (h a e) -> p h a e", a=2, e=DK)[:, :, a, :]))
            link(nc.vector.tensor_scalar(woT[:].rearrange("p k d -> p (k d)"), pg[:, 3, :], rep[:, 68:69], None,
                                         ALU.mult))
            nc.vector.memset(ktmp[0][:, 0, 2:3], 0.0).then_inc(setup_dve, 1)
            dve.wait_ge(setup_pe, 3)
            for m in range(4):
                link(nc.vector.tensor_copy(wqk[:, m, :, :].rearrange("p k d -> p (k d)"), pg[:, m, :]))
            nc.vector.memset(ktmp[0][:, 0, 3:4], 0.0).then_inc(setup_dve, 1)
            setup_links = n

            def layer_stats(src, ready, st, m, stats, aggr, b, i):
                for t in range(ST):
                    ready(t)
                    nc.vector.bn_stats(st[b][:, t, :], src[b][:, t, :]).then_inc(stats[b], 1)
                for t in range(ST):
                    apart(dve, stats[b], ST * i + t + 1, passed)
                    nc.vector.bn_aggr(m[b][:, t, :], st[b][:, t, :]).then_inc(aggr[b], 1)

            with dve.Fori(0, NSPAN) as i:
                for b in range(B):
                    layer_stats(xt, lambda t: dve.wait_ge(x_loaded[b], 16 * i + 16), bst, mv, x_stats, x_aggr, b, i)
                for b in range(B):
                    dve.wait_ge(x_std[b], i + 1)
                    nc.vector.reciprocal(rstd[b][:], std[b][:]).then_inc(x_rstd[b], 1)
                    dve.wait_ge(x_rstd[b], i + 1)
                    for t in range(ST):
                        nc.vector.tensor_scalar(xn[b][:, t, :], xt[b][:, t, :], mv[b][:, t, 0:1], rstd[b][:, t:t + 1],
                                                ALU.subtract, ALU.mult).then_inc(xn_made[b], 1)
                for b in range(B):
                    for r in range(4):
                        f = r % 2
                        dst = qT[b][:, f, :] if r < 2 else ktmp[b][:, f, :]
                        dve.wait_ge(a1_made[b], 4 * i + r + 1)
                        nc.vector.scalar_tensor_tensor(
                            out=dst, in0=pg[:, (r + 2) % 4, SPAN:2 * SPAN],
                            scalar=rep[:, 65 + 2 * (r // 2):66 + 2 * (r // 2)], in1=a1[:, r, :],
                            op0=ALU.add, op1=ALU.mult).then_inc(q_made[b], 1)
                        if r >= 2:
                            dve.wait_ge(q_made[b], 4 * i + r + 1)
                            for a in range(2):
                                nc.vector.tensor_scalar(
                                    kbd[b][:, f, :, a, :], ktmp[b][:, f, :].rearrange("p (c m) -> p c m", m=CHUNK),
                                    even_odd[:, a:a + 1], None, ALU.mult).then_inc(kbd_made[b], 1)

                def mask_scores(c):
                    dve.wait_ge(s_ready, NCH * i + c + 1)
                    for b in range(B):
                        nc.vector.tensor_tensor(
                            sT[c % 2][b],
                            pg[:, :, b * P:(b + 1) * P].rearrange("p g (f m) -> p g f m", f=2),
                            bc(bc(cmask[:, 0, :], 1, 2), 1, 4), ALU.mult).then_inc(s_masked, 1)

                mask_scores(0)
                for c in range(NCH):
                    if c + 1 < NCH:
                        mask_scores(c + 1)
                    for b in range(B):
                        dve.wait_ge(kv_ready[b], NCH * i + c + 1)
                        nc.vector.tensor_tensor(kvm[b][:], pkv[:, b, 0:2 * P].rearrange("p (f e) -> p f e", f=2),
                                                bc(kvmask[:], 1, 2), ALU.mult).then_inc(kvm_made[b], 1)
                for b in range(B):
                    dve.wait_ge(ostd_made[b], i + 1)
                    nc.vector.reciprocal(orstd[:], ostd[b][:]).then_inc(orstd_made[b], 1)
                    dve.wait_ge(orstd_made[b], i + 1)
                    nc.vector.tensor_tensor(oT[b][:].rearrange("p f t -> p (f t)"), po[:, b, :],
                                            orstd[:].rearrange("p f t -> p (f t)"), ALU.mult).then_inc(oT_made[b], 1)
                    dve.wait_ge(oT_made[b], FREE + i + 1)
                for b in range(B):
                    dve.wait_ge(y_ready[b], i + 1)
                    dve.wait_ge(x2_stored[b], FREE + 16 * i)
                    nc.vector.tensor_tensor(x2[b][:], pg[:, 2 + b, :].rearrange("p (t d) -> p t d", t=ST), xt[b][:],
                                            ALU.add).then_inc(x2_made[b], 1)
                    dve.wait_ge(x2_made[b], FREE + i + 1)
                    layer_stats(x2, lambda t: None, bst2, mv2, x2_stats, x2_aggr, b, i)
                for b in range(B):
                    dve.wait_ge(x2_std[b], i + 1)
                    nc.vector.reciprocal(rstd2[b][:], std2[b][:]).then_inc(x2_rstd[b], 1)
                    dve.wait_ge(x2_rstd[b], i + 1)
                    dve.wait_ge(dispatched[b], FREE + i)
                    for t in range(ST):
                        nc.vector.tensor_scalar(xp[b][:, t, 0:D], x2[b][:, t, :], mv2[b][:, t, 0:1],
                                                rstd2[b][:, t:t + 1], ALU.subtract, ALU.mult).then_inc(xp_made[b], 1)
                    nc.vector.tensor_copy(xp[b][:, :, D:ROW].bitcast(I32),
                                          ids[:, bass.ds((L // P) * b + ST * i, ST)].unsqueeze(2)).then_inc(id_made[b], 1)
                k0 = 0

                def step(ins):
                    nonlocal k0
                    k0 += 1
                    ins.then_inc(route_step, 1)
                    apart(dve, route_step, ROUTE_LINKS * i + (setup_links + k0), passed)

                dve.wait_ge(score_made, FREE + i + 1)
                step(nc.vector.tensor_tensor(sfc[:].rearrange("p (n g) e -> p n (g e)", g=G), score[:],
                                             bc(cbias[:], 1, NB), ALU.add))
                step(nc.vector.tensor_tensor(hi2[:], sfc[:, :, 0:2], sfc[:, :, 2:4], ALU.max))
                step(nc.vector.tensor_tensor(lo2[:], sfc[:, :, 0:2], sfc[:, :, 2:4], ALU.min))
                step(nc.vector.tensor_tensor(top1[:], hi2[:, :, 0], hi2[:, :, 1], ALU.max))
                step(nc.vector.tensor_tensor(mid[:], hi2[:, :, 0], hi2[:, :, 1], ALU.min))
                step(nc.vector.tensor_tensor(top2[:], lo2[:, :, 0], lo2[:, :, 1], ALU.max))
                step(nc.vector.tensor_tensor(top2[:], top2[:], mid[:], ALU.max))
                step(nc.vector.tensor_tensor(gsc[:].rearrange("p n g -> p (n g)"), top1[:], top2[:], ALU.add))
                for n in range(NB):
                    ins = nc.vector.max(gtop[:, n, :], gsc[:, n, :])
                step(ins)
                step(nc.vector.tensor_copy(gpick[:, :, 0:TOPK_G], gtop[:, :, 0:TOPK_G]))
                for n in range(NB):
                    ins = nc.vector.match_replace(gmark[:, n, :], gpick[:, n, :], gsc[:, n, :], MARK)
                step(ins)
                step(nc.vector.tensor_scalar(gneg[:], gmark[:].rearrange("p n g -> p (n g)"), BIG, -BIG,
                                             ALU.is_lt, ALU.mult))
                step(nc.vector.tensor_tensor(masked[:].rearrange("p n (g e) -> p (n g) e", g=G), sfc[:],
                                             bc(gneg[:], 2, EG), ALU.add))
                for n in range(NB):
                    ins = nc.vector.max(etop[:, n, :], masked[:, n, :])
                step(ins)
                step(nc.vector.tensor_copy(epick[:, :, 0:TOPK], etop[:, :, 0:TOPK]))
                for n in range(NB):
                    ins = nc.vector.match_replace(emark[:, n, :], epick[:, n, :], masked[:, n, :], MARK)
                step(ins)
                nc.vector.tensor_scalar(chosen[:], emark[:], BIG, None, ALU.is_gt).then_inc(chosen_made, 1)
                dve.wait_ge(rank_ready, i + 1)
                step(nc.vector.tensor_tensor(slot[:], pg[:, 3, 0:NB * E].rearrange("p (n e) -> p n e", e=E),
                                             bc(next_row[:], 1, NB), ALU.add))
                step(nc.vector.tensor_tensor(slotm[:], slot[:], chosen[:], ALU.mult))
                for n in range(NB):
                    ins = nc.vector.max(stop8[:, n, :], slotm[:, n, :])
                step(ins)
                for b in range(B):
                    dve.wait_ge(dispatched[b], FREE + i)
                nc.vector.tensor_scalar(slots[:], stop8[:], -1.0, None, ALU.add).then_inc(slots_made, 1)
                nc.vector.tensor_tensor(next_row[:], pg[:, 3, NB * E:(NB + 1) * E], next_row[:], ALU.add)\
                  .then_inc(rank_read, 1)
                dve.wait_ge(slots_made, i + 1)
                dve.wait_ge(rank_read, FREE + i + 1)
                assert k0 == ROUTE_LINKS, k0
            dve.wait_ge(attn_loaded, 16 * 15)
            nc.vector.tensor_copy(wgu[:, :, :, M].rearrange("p e k -> p k e"), wr[:]).then_inc(router_cols, 1)

        @block.tensor
        def _(pe):
            pe.wait_ge(consts_made, 1)
            pe.wait_ge(setup_dve, 1)
            pe.wait_ge(attn_loaded, 16 * 15)
            nc.tensor.matmul(pg[:, 0, 0:69], rep16[:].rearrange("p h d -> p (h d)"), f4[:], start=True, stop=True)\
              .then_inc(setup_pe, 1)
            for n, bank in ((2, 2), (3, 3)):
                for k in range(KD):
                    for r in range(KD):
                        ins = nc.tensor.transpose(pg[:, bank, (k * KD + r) * P:(k * KD + r + 1) * P],
                                                  nat[:, n, r, k * P:(k + 1) * P], ident[:])
            pe.wait_ge(setup_dve, 2)
            for m in range(4):
                ins = nc.tensor.transpose(pg[:, 1, m * P:(m + 1) * P], gsb[:, m, :], ident[:])
            ins.then_inc(setup_pe, 1)
            pe.wait_ge(setup_dve, 3)
            for m in range(4):
                for k in range(KD):
                    for f in range(2):
                        ins = nc.tensor.matmul(pg[:, m, (k * 2 + f) * P:(k * 2 + f + 1) * P],
                                               nat[:, m // 2, f, k * P:(k + 1) * P], fmap[:, m, :],
                                               start=True, stop=True)
            ins.then_inc(setup_pe, 1)
            for b in range(B):
                nc.tensor.matmul(pkv[:, b, 0:2 * P], ident[:], zeros[:, 0:2 * P], start=True, stop=True)
            pe.wait_ge(setup_dve, 4)

            def turn(src, b, bank):
                for k in range(KD):
                    for t in range(ST):
                        ins = nc.tensor.transpose(pg[:, bank, k * SPAN + t * P:k * SPAN + (t + 1) * P],
                                                  src[b][:, t, k * P:(k + 1) * P], ident[:])
                return ins

            with pe.Fori(0, NSPAN) as i:
                for b in range(B):
                    pe.wait_ge(xn_made[b], 2 * i + 2)
                    pe.wait_ge(x2nT_made[b], FREE + i)
                    turn(xn, b, b).then_inc(xt_turned[b], 1)
                pe.wait_ge(score_made, FREE + i)
                pe.wait_ge(rank_read, FREE + i)
                for b in range(B):
                    pe.wait_ge(xnT_made[b], i + 1)
                    for r in range(4):
                        if b == 0 and r == 2:
                            pe.wait_ge(xnT_made[1], i + 1)
                        if b == 1:
                            pe.wait_ge(q_made[0], 4 * i + r + 1)
                        for m in range(2):
                            for k in range(KD):
                                ins = nc.tensor.matmul(pg[:, (r + 2) % 4, m * SPAN:(m + 1) * SPAN],
                                                       wqk[:, 2 * (r // 2) + m, k, (r % 2) * P:(r % 2 + 1) * P],
                                                       xnT[b][:, k, :], start=(k == 0), stop=(k == KD - 1))
                        ins.then_inc(proj_ready[b], 1)
                for b in range(B):
                    pe.wait_ge(q_made[1], 4 * i + b + 1)
                    for c in range(NCH):
                        for a in range(2):
                            for k in range(KD):
                                ins = nc.tensor.matmul(pg[a * CHUNK:(a + 1) * CHUNK, 2 + b, c * P:(c + 1) * P],
                                                       xnT[b][:, k, c * CHUNK:(c + 1) * CHUNK], wvT[:, k, a, :],
                                                       start=(k == 0), stop=(k == KD - 1))
                    ins.then_inc(v_ready[b], 1)
                pe.wait_ge(q_made[1], 4 * i + 4)
                for b in range(B):
                    pe.wait_ge(kbd_made[b], 4 * i + 4)
                    if b == 1:
                        for bb in range(B):
                            pe.wait_ge(vbd_made[bb], 2 * i + 2)
                    for half in range(2):
                        for c in range(2):
                            for f in range(2):
                                ins = nc.tensor.transpose(pg[:, 2 * b + half, (2 * c + f) * P:(2 * c + f + 1) * P],
                                                          kbd[b][:, f, 2 * half + c, :, :].rearrange("p a m -> p (a m)"),
                                                          ident[:])
                        ins.then_inc(kt_ready[b], 1)

                def scores(c):
                    if c == 0:
                        for b in range(B):
                            pe.wait_ge(ktok_made[b], 2 * i + 2)
                    else:
                        pe.wait_ge(s_masked, 2 * NCH * i + 2 * c)
                    for b in range(B):
                        for f in range(2):
                            for q in range(4):
                                ins = nc.tensor.matmul(
                                    pg[:, q, b * P + f * CHUNK:b * P + (f + 1) * CHUNK],
                                    kbd[b][32 * q:32 * q + 32, f, c, :, :].rearrange("p a m -> p (a m)"),
                                    qT[b][32 * q:32 * q + 32, f, c * CHUNK:(c + 1) * CHUNK], start=True, stop=True)
                    ins.then_inc(s_ready, 1)

                scores(0)
                for c in range(NCH):
                    if c + 1 < NCH:
                        scores(c + 1)
                    pe.wait_ge(s_masked, 2 * NCH * i + 2 * c + 2)
                    for b in range(B):
                        if c == 0:
                            pe.wait_ge(oT_made[b], FREE + i)
                        else:
                            pe.wait_ge(kvm_made[b], NCH * i + c)
                        for f in range(2):
                            o = po[:, b, f * SPAN + c * CHUNK:f * SPAN + (c + 1) * CHUNK]
                            nc.tensor.matmul(o, kvm[b][:, f, :], qT[b][:, f, c * CHUNK:(c + 1) * CHUNK],
                                             start=True, stop=False, skip_group_check=True)
                            for q in range(4):
                                ins = nc.tensor.matmul(
                                    po[32 * q:32 * q + 32, b, f * SPAN + c * CHUNK:f * SPAN + (c + 1) * CHUNK],
                                    vbd[b][:, c, 4 * f + q, :, :].rearrange("p a e -> p (a e)"),
                                    sT[c % 2][b][:, q, f, :], start=False, stop=(q == 3), skip_group_check=True)
                        ins.then_inc(o_ready[b], 1)
                        for f in range(2):
                            ins = nc.tensor.matmul(pkv[:, b, f * P:(f + 1) * P], ktok[b][:, c, f, :],
                                                   vbd[b][:, c, 4 * f:4 * f + 4, :, :].rearrange("p g a e -> p (g a e)"),
                                                   start=False, stop=True, skip_group_check=True)
                        ins.then_inc(kv_ready[b], 1)
                for b in range(B):
                    pe.wait_ge(sq_made[b], i + 1)
                    nc.tensor.matmul(pg[:, b, :], hmean[:], sq[b][:].rearrange("p f t -> p (f t)"),
                                     start=True, stop=True).then_inc(ms_ready[b], 1)
                for b in range(B):
                    pe.wait_ge(oT_made[b], FREE + i + 1)
                    for t in range(ST):
                        for f in range(2):
                            ins = nc.tensor.matmul(pg[:, 2 + b, t * D:(t + 1) * D], oT[b][:, f, t * P:(t + 1) * P],
                                                   woT[:, f, :], start=(f == 0), stop=(f == 1))
                    ins.then_inc(y_ready[b], 1)
                for b in range(B):
                    pe.wait_ge(xp_made[b], 2 * i + 2)
                    turn(xp, b, b).then_inc(x2t_turned[b], 1)
                for b in range(B):
                    pe.wait_ge(x2nT_made[b], FREE + i + 1)
                    for t in range(ST):
                        for k in range(KD):
                            n = b * ST + t
                            ins = nc.tensor.matmul(pg[:, 2, n * E:(n + 1) * E], x2nT[b][:, k, t * P:(t + 1) * P],
                                                   wr[:, k, :], start=(k == 0), stop=(k == KD - 1))
                ins.then_inc(logit_ready, 1)
                pe.wait_ge(chosen_made, i + 1)
                for n in range(NB):
                    dst = pg[:, 3, n * E:(n + 1) * E]
                    nc.tensor.matmul(dst, tri[:], chosen[:, n, :], start=True, stop=(n == 0))
                    for before in range(n):
                        nc.tensor.matmul(dst, onesb[:], chosen[:, before, :], start=False, stop=(before == n - 1))
                for n in range(NB):
                    ins = nc.tensor.matmul(pg[:, 3, NB * E:(NB + 1) * E], onesb[:], chosen[:, n, :],
                                           start=(n == 0), stop=(n == NB - 1))
                ins.then_inc(rank_ready, 1)


def phase_b(nc, ctx, sb, sem, sems, g):
    rows_d, x2_d, x2nT_d, acc_d, out = (g[k] for k in ("rows_d", "x2_d", "x2nT_d", "acc_d", "out"))
    ident, wgu, shg, shu, shd, next_row, first_row, zeros, part_f = (
        g[k] for k in ("ident", "wgu", "shg", "shu", "shd", "next_row", "first_row", "zeros", "part_f"))
    with ExitStack() as own:
        def t1(name, shape, dt=F32):
            return sb(name, shape, dt, own)

        wd = t1("wd", [P, E, 2, D])
        pad_row = t1("pad_row", [P, ROW])
        pad_slots = t1("pad_slots", [P, E + 1], U32)
        pad_f = t1("pad_f", [P, E + 1])
        jj_i = t1("jj_i", [P, 2], I32)
        jj = t1("jj", [P, 2])
        cnt = t1("cnt", [P, E])
        cnt_i = t1("cnt_i", [P, E], I32)
        tiles_of = t1("tiles_of", [P, E])
        tile_end = t1("tile_end", [P, E])
        onesE = t1("onesE", [P, E])
        before = t1("before", [P, 2, E])
        started = t1("started", [P, 2, E])
        expert = t1("expert", [P, 2])
        tile_at = t1("tile_at", [P, 2])
        inside = t1("inside", [P, 2])
        table = t1("table", [P, 4])
        table_i = t1("table_i", [1, 4, P], I32)
        shared = ExitStack()

        def t3(name, shape):
            return sb(name, shape, F32, shared)

        xs = [t3(f"xs{s}", [P, KD, SP_TOK]) for s in range(2)]
        x2s = [t3(f"x2s{s}", [P, 4, D]) for s in range(2)]
        sig = [t3(f"sig{s}", [P, SP_TOK]) for s in range(2)]
        sgu = [t3(f"sgu{s}", [P, SP_TOK]) for s in range(2)]
        hs = [t3(f"hs{s}", [P, SP_TOK]) for s in range(3)]
        ys = [t3(f"ys{s}", [P, 4, D]) for s in range(2)]

        pb = own.enter_context(nc.psum_tensor("pb", [P, 8, 512], F32))

        down_loaded = sem("down_loaded")
        pool_step = sem("pool_step")
        pad_made = sem("pad_made")
        padded = sem("padded")
        table_step = sem("table_step")
        table_made = sem("table_made")
        table_turned = sem("table_turned")
        table_ready = sem("table_ready")
        zeroed = sem("zeroed")
        xs_loaded, x2s_loaded, sh_stored = (sems(n) for n in ("xs_loaded", "x2s_loaded", "sh_stored"))
        gate_ready, sig_made, sgu_made, hs_made, sh_y_ready, ys_made = (
            sems(n) for n in ("gate_ready", "sig_made", "sgu_made", "hs_made", "sh_y_ready", "ys_made"))

        FT = [(0, P), (P, P), (2 * P, MS - 2 * P)]
        NSH = T // SP_TOK

        block = shared.enter_context(nc.Block())

        @block.sync
        def _(sp):
            with sp.Fori(0, NSH // 2) as i:
                for s in range(2):
                    at = (2 * i + s) * SP_TOK
                    sp.wait_ge(sh_stored[s], FREE + 16 * i)
                    sp.dma_start(xs[s][:], x2nT_d[:, :, bass.ds(at, SP_TOK)]).then_inc(xs_loaded[s], 16)
                    sp.dma_start(x2s[s][:], x2_d[bass.ds(at, SP_TOK), :].rearrange("(t p) d -> p t d", p=P))\
                      .then_inc(x2s_loaded[s], 16)
                for s in range(2):
                    at = (2 * i + s) * SP_TOK
                    sp.wait_ge(ys_made[s], FREE + 2 * i + 2)
                    sp.dma_start(acc_d[0][bass.ds(at, SP_TOK), :].rearrange("(t p) d -> p t d", p=P), ys[s][:])\
                      .then_inc(sh_stored[s], 16)
            for s in range(2):
                sp.wait_ge(sh_stored[s], FREE + 16 * (NSH // 2))

        @block.scalar
        def _(act):
            for h in range(2):
                act.dma_start(wd[0:MH, :, h, :],
                              g["down_w"][:, h * MH:(h + 1) * MH, :].rearrange("e p d -> p e d")).then_inc(down_loaded, 16)
            for n in range(T // P + 1):
                act.dma_start(acc_d[1][n * P:(n + 1) * P, :], zeros[:]).then_inc(zeroed, 16)
            act.dma_start(acc_d[0][T:T + P, :], zeros[:]).then_inc(zeroed, 16)
            act.wait_ge(g["sh_loaded"], 64)
            with act.Fori(0, NSH // 2) as i:
                for s in range(2):
                    for n, (f0, fn) in enumerate(FT):
                        p = n % 2
                        u = (3 * s + n) // 2
                        q = (3 * s + n) % 2
                        act.wait_ge(gate_ready[q], 3 * i + u + 1)
                        nc.scalar.activation(sig[q][0:fn, :], pb[0:fn, 2 * q, :], ACT.Sigmoid).then_inc(sig_made[q], 1)
            act.wait_ge(zeroed, 16 * (T // P + 2))
            act.wait_ge(down_loaded, 32)

        @block.gpsimd
        def _(pool):
            for free in (*sh_stored, *hs_made, *sh_y_ready, *ys_made):
                pool.sem_inc(free, FREE)
            n = 0

            def link(ins):
                nonlocal n
                n += 1
                ins.then_inc(pool_step, 1)
                pool.wait_ge(pool_step, n)

            link(pool.memset(pad_row[:], 0.0))
            link(pool.iota(pad_row[:, D:ROW].bitcast(I32), pattern=[[0, 1]], base=T, channel_multiplier=1))
            link(pool.iota(jj_i[:], pattern=[[P, 2]], base=0, channel_multiplier=1))
            link(pool.memset(onesE[:], 1.0))
            pool.wait_ge(pad_made, 1)
            for e in range(E + 1):
                pool.indirect_dma_start(rows_d[:, :], bass.IndirectOffsetOnAxis(ap=pad_slots[:, e:e + 1], axis=0),
                                        pad_row[:], None).then_inc(padded, 16)
            pool.wait_ge(padded, 16 * (E + 1))

        @block.vector
        def _(dve):
            n = 0

            def link(ins):
                nonlocal n
                n += 1
                ins.then_inc(table_step, 1)
                dve.wait_ge(table_step, n)

            link(nc.vector.tensor_scalar(pad_f[:, 0:E], next_row[:], part_f[:, 0:1], -1.0, ALU.add, ALU.add))
            link(nc.vector.tensor_scalar(pad_f[:, E:E + 1], part_f[:], float(E * REGION), None, ALU.add))
            nc.vector.tensor_copy(pad_slots[:], pad_f[:]).then_inc(pad_made, 1)
            dve.wait_ge(pool_step, 4)
            link(nc.vector.tensor_tensor(cnt[:], next_row[:], first_row[:], ALU.subtract))
            link(nc.vector.tensor_scalar(cnt_i[:], cnt[:], float(P - 1), None, ALU.add))
            link(nc.vector.tensor_scalar(cnt_i[:], cnt_i[:], 7, None, ALU.logical_shift_right))
            link(nc.vector.tensor_copy(tiles_of[:], cnt_i[:]))
            link(nc.vector.tensor_tensor_scan(tile_end[:], onesE[:], tiles_of[:], 0.0, ALU.mult, ALU.add))
            link(nc.vector.tensor_copy(jj[:], jj_i[:]))
            link(nc.vector.tensor_tensor(before[:], bc(tile_end[:], 1, 2), bc(jj[:], 2, E), ALU.is_le))
            link(nc.vector.tensor_reduce(expert[:], before[:], AX_X, ALU.add))
            link(nc.vector.tensor_tensor(started[:], before[:], bc(tiles_of[:], 1, 2), ALU.mult))
            link(nc.vector.tensor_reduce(tile_at[:], started[:], AX_X, ALU.add))
            link(nc.vector.tensor_tensor(tile_at[:], jj[:], tile_at[:], ALU.subtract))
            link(nc.vector.tensor_scalar(inside[:], expert[:], float(E) - 0.5, float(P), ALU.is_lt, ALU.mult))
            link(nc.vector.tensor_tensor(tile_at[:], tile_at[:], inside[:], ALU.mult))
            link(nc.vector.scalar_tensor_tensor(out=table[:, 0:2], in0=expert[:], scalar=float(REGION), in1=tile_at[:],
                                                op0=ALU.mult, op1=ALU.add))
            link(nc.vector.tensor_scalar(table[:, 2:4], expert[:], float(E - 1), None, ALU.min))
            nc.vector.memset(cnt[:, 0:1], 0.0).then_inc(table_made, 1)
            dve.wait_ge(table_turned, 1)
            nc.vector.tensor_copy(table_i[:].rearrange("p n t -> p (n t)"), pb[0:1, 7, :]).then_inc(table_ready, 1)
            with dve.Fori(0, NSH // 2) as i:
                for s in range(2):
                    for n, (f0, fn) in enumerate(FT):
                        u = (3 * s + n) // 2
                        q = (3 * s + n) % 2
                        dve.wait_ge(sig_made[q], 3 * i + u + 1)
                        nc.vector.tensor_tensor(sgu[q][0:fn, :], pb[0:fn, 2 * q, :], sig[q][0:fn, :], ALU.mult)\
                          .then_inc(sgu_made[q], 1)
                        dve.wait_ge(sgu_made[q], 3 * i + u + 1)
                        if s == 0:
                            dve.wait_ge(sh_y_ready[1], FREE + i)
                        else:
                            dve.wait_ge(sh_y_ready[0], FREE + i + 1)
                        nc.vector.tensor_tensor(hs[n][0:fn, :], pb[0:fn, 2 * q + 1, :], sgu[q][0:fn, :], ALU.mult)\
                          .then_inc(hs_made[q], 1)
                    dve.wait_ge(x2s_loaded[s], 16 * i + 16)
                    dve.wait_ge(sh_y_ready[s], FREE + i + 1)
                    dve.wait_ge(sh_stored[s], FREE + 16 * i)
                    for half in range(2):
                        nc.vector.tensor_tensor(ys[s][:, 2 * half:2 * half + 2, :],
                                                pb[:, 4 + half, :].rearrange("p (t d) -> p t d", t=2),
                                                x2s[s][:, 2 * half:2 * half + 2, :], ALU.add).then_inc(ys_made[s], 1)

        @block.tensor
        def _(pe):
            pe.wait_ge(table_made, 1)
            for n in range(4):
                ins = nc.tensor.transpose(pb[0:1, 7, n * P:(n + 1) * P], table[:, n:n + 1], ident[:])
            ins.then_inc(table_turned, 1)
            pe.wait_ge(g["sh_loaded"], 64)
            with pe.Fori(0, NSH // 2) as i:
                for s in range(2):
                    pe.wait_ge(xs_loaded[s], 16 * i + 16)
                    for n, (f0, fn) in enumerate(FT):
                        u = (3 * s + n) // 2
                        q = (3 * s + n) % 2
                        pe.wait_ge(hs_made[q], FREE + 3 * i + u)
                        for w, bank in ((shg, 2 * q), (shu, 2 * q + 1)):
                            for k in range(KD):
                                ins = nc.tensor.matmul(pb[0:fn, bank, :], w[:, k, f0:f0 + fn], xs[s][:, k, :],
                                                       start=(k == 0), stop=(k == KD - 1))
                        ins.then_inc(gate_ready[q], 1)
                    for q in range(2):
                        pe.wait_ge(hs_made[q], FREE + 3 * i + (3 * s + 3 + 1 - q) // 2)
                    if s == 0:
                        pe.wait_ge(ys_made[1], FREE + 2 * i)
                    else:
                        pe.wait_ge(ys_made[0], FREE + 2 * i + 2)
                    for t in range(4):
                        for n, (f0, fn) in enumerate(FT):
                            ins = nc.tensor.matmul(pb[:, 4 + t // 2, (t % 2) * D:(t % 2 + 1) * D],
                                                   hs[n][0:fn, t * P:(t + 1) * P], shd[0:fn, n, :],
                                                   start=(n == 0), stop=(n == 2))
                    ins.then_inc(sh_y_ready[s], 1)

        shared.close()
        phase_c(nc, sb, sem, sems, g, wd, table_i, table_ready, pb)


def phase_c(nc, sb, sem, sems, g, wd, table_i, table_ready, pb):
    rows_d, acc_d, ident, wgu = (g[k] for k in ("rows_d", "acc_d", "ident", "wgu"))
    passed = g["passed"]
    out = g["out"].rearrange("b l d -> (b l) d")
    with ExitStack() as own:
        def ring(name, n, shape):
            return [sb(f"{name}{s}", shape, F32, own) for s in range(n)]

        xe = ring("xe", UNROLL, [P, ROW])
        xeT = ring("xeT", 2, [P, KD, P])
        sg = ring("sg", 2, [P, M + 1])
        hg = ring("hg", 2, [P, M])
        h = ring("h", 2, [P, M])
        hT = ring("hT", 2, [MH, 2, P])
        ye = ring("ye", UNROLL, [P, D])
        token = [sb(f"token{s}", [P, 1], U32, own) for s in range(UNROLL)]
        s0 = ring("s0_", 2, [P, 4, D])
        s1 = ring("s1_", 2, [P, 4, D])

        row_loaded = sems("row_loaded", UNROLL)
        added = sems("added", UNROLL)
        x_turned, xeT_made, gu_ready, sg_made, hg_made, h_made, h_turned, hT_made, ye_ready, ye_made = (
            sems(n) for n in ("e_x_turned", "xeT_made", "gu_ready", "sg_made", "hg_made", "h_made", "h_turned",
                              "hT_made", "ye_ready", "ye_made"))
        sums_loaded, so_made, so_stored = (sems(n) for n in ("sums_loaded", "so_made", "so_stored"))

        ROUNDS = NT // UNROLL
        flat = table_i[:].rearrange("o n t -> o (n t)")

        def use(r, s):
            return (UNROLL // 2) * r + s // 2

        def off(r, s, n):
            return r + (s + n) // UNROLL, (s + n) % UNROLL

        with nc.Block() as block:

            @block.sync
            def _(sp):
                def one_round(r, first):
                    for s in range(UNROLL):
                        row = sp.value_load(flat[0:1, bass.ds(UNROLL * r + s, 1)], min_val=0, max_val=NROWS - P)
                        if not first:
                            apart(sp, h_made[s % 2], use(r - 1, s) + 1, passed)
                        sp.dma_start(xe[s][:], rows_d[bass.ds(row, P), :]).then_inc(row_loaded[s], 16)

                one_round(0, True)
                with sp.Fori(1, ROUNDS) as r:
                    one_round(r, False)
                for s in range(UNROLL):
                    sp.wait_ge(added[s], 16 * ROUNDS)
                with sp.Fori(0, T // SP_TOK // 2) as i:
                    for s in range(2):
                        at = (2 * i + s) * SP_TOK
                        sp.wait_ge(so_stored[s], FREE + 16 * i)
                        for n, dst in enumerate((s0, s1)):
                            sp.dma_start(dst[s][:], acc_d[n][bass.ds(at, SP_TOK), :].rearrange("(t p) d -> p t d", p=P))\
                              .then_inc(sums_loaded[s], 16)
                    for s in range(2):
                        at = (2 * i + s) * SP_TOK
                        sp.wait_ge(so_made[s], i + 1)
                        sp.dma_start(out[bass.ds(at, SP_TOK), :].rearrange("(t p) d -> p t d", p=P), s0[s][:])\
                          .then_inc(so_stored[s], 16)
                for s in range(2):
                    sp.wait_ge(so_stored[s], FREE + 16 * (T // SP_TOK // 2))

            @block.gpsimd
            def _(pool):
                for free in so_stored:
                    pool.sem_inc(free, FREE)
                def one_round(r, first):
                    for s in range(UNROLL):
                        if s >= 2:
                            apart(pool, added[s - 2], 16 * r + 16, passed)
                        elif not first:
                            apart(pool, added[s + 2], 16 * r, passed)
                        apart(pool, ye_made[s % 2], use(r, s) + 1, passed)
                        pool.indirect_dma_start(
                            acc_d[s % 2][:, :],
                            bass.IndirectOffsetOnAxis(ap=token[s][:], axis=0),
                            ye[s][:], None, compute_op=ALU.add).then_inc(added[s], 16)

                one_round(0, True)
                with pool.Fori(1, ROUNDS) as r:
                    one_round(r, False)

            @block.scalar
            def _(act):
                def turned_in(r, s):
                    p = s % 2
                    act.wait_ge(x_turned[p], use(r, s) + 1)
                    nc.scalar.activation(xeT[p][:].rearrange("p k t -> p (k t)"), pb[:, p, 0:2 * P], ACT.Copy)\
                      .then_inc(xeT_made[p], 1)

                def hidden_turned(r, s):
                    p = s % 2
                    act.wait_ge(h_turned[p], use(r, s) + 1)
                    nc.scalar.activation(hT[p][:].rearrange("p k t -> p (k t)"), pb[0:MH, 4 + p, 0:2 * P], ACT.Copy)\
                      .then_inc(hT_made[p], 1)

                def one_round(r, first, last):
                    for s in range(UNROLL):
                        p = s % 2
                        act.wait_ge(gu_ready[p], use(r, s) + 1)
                        nc.scalar.activation(sg[p][:], pb[:, 2 + p, 0:M + 1], ACT.Sigmoid).then_inc(sg_made[p], 1)
                        if not (last and s == UNROLL - 1):
                            turned_in(*off(r, s, 1))
                        if not (first and s == 0):
                            hidden_turned(*off(r, s, -1))

                turned_in(0, 0)
                one_round(0, True, False)
                with act.Fori(1, ROUNDS - 1) as r:
                    one_round(r, False, False)
                one_round(ROUNDS - 1, False, True)
                hidden_turned(ROUNDS - 1, UNROLL - 1)

            @block.vector
            def _(dve):
                def taken(r, s):
                    dve.wait_ge(ye_ready[s % 2], use(r, s) + 1)
                    dve.wait_ge(added[s], 16 * r)
                    nc.vector.tensor_copy(ye[s][:], pb[:, 6 + s % 2, 0:D]).then_inc(ye_made[s % 2], 1)

                def one_round(r, first):
                    for s in range(UNROLL):
                        p = s % 2
                        dve.wait_ge(sg_made[p], use(r, s) + 1)
                        dve.wait_ge(row_loaded[s], 16 * r + 16)
                        dve.wait_ge(added[s], 16 * r)
                        nc.vector.tensor_copy(token[s][:], xe[s][:, D:ROW].bitcast(U32))
                        nc.vector.tensor_tensor(hg[p][:], pb[:, 2 + p, 0:M], sg[p][:, 0:M], ALU.mult)\
                          .then_inc(hg_made[p], 1)
                        dve.wait_ge(hg_made[p], use(r, s) + 1)
                        nc.vector.scalar_tensor_tensor(out=h[p][:], in0=hg[p][:], scalar=sg[p][:, M:M + 1],
                                                       in1=pb[:, 2 + p, M + 1:WIDE], op0=ALU.mult, op1=ALU.mult)\
                          .then_inc(h_made[p], 1)
                        if not (first and s < 2):
                            taken(*off(r, s, -2))

                one_round(0, True)
                with dve.Fori(1, ROUNDS) as r:
                    one_round(r, False)
                for s in range(UNROLL - 2, UNROLL):
                    taken(ROUNDS - 1, s)
                with dve.Fori(0, T // SP_TOK // 2) as i:
                    for s in range(2):
                        dve.wait_ge(sums_loaded[s], 32 * i + 32)
                        nc.vector.tensor_tensor(s0[s][:], s0[s][:], s1[s][:], ALU.add).then_inc(so_made[s], 1)

            @block.tensor
            def _(pe):
                def turn_rows(r, s):
                    p = s % 2
                    pe.wait_ge(row_loaded[s], 16 * r + 16)
                    pe.wait_ge(xeT_made[p], use(r, s))
                    for k in range(KD):
                        ins = nc.tensor.transpose(pb[:, p, k * P:(k + 1) * P], xe[s][:, k * P:(k + 1) * P], ident[:])
                    ins.then_inc(x_turned[p], 1)

                def expert_of(r, s):
                    return pe.value_load(flat[0:1, bass.ds(2 * P + UNROLL * r + s, 1)], min_val=0, max_val=E - 1)

                def gate_up(r, s, e):
                    p = s % 2
                    pe.wait_ge(xeT_made[p], use(r, s) + 1)
                    pe.wait_ge(h_made[p], use(r, s))
                    for k in range(KD):
                        ins = nc.tensor.matmul(pb[:, 2 + p, 0:WIDE], xeT[p][:, k, :],
                                               wgu[:, bass.ds(e, 1), k, :].rearrange("p o c -> p (o c)"),
                                               start=(k == 0), stop=(k == KD - 1))
                    ins.then_inc(gu_ready[p], 1)

                def down(r, s, e):
                    p = s % 2
                    pe.wait_ge(hT_made[p], use(r, s) + 1)
                    pe.wait_ge(ye_made[p], use(r, s))
                    for k in range(2):
                        ins = nc.tensor.matmul(pb[:, 6 + p, 0:D], hT[p][:, k, :],
                                               wd[0:MH, bass.ds(e, 1), k, :].rearrange("p o d -> p (o d)"),
                                               start=(k == 0), stop=(k == 1))
                    ins.then_inc(ye_ready[p], 1)

                def turn_hidden(r, s):
                    p = s % 2
                    pe.wait_ge(h_made[p], use(r, s) + 1)
                    pe.wait_ge(hT_made[p], use(r, s))
                    for k in range(2):
                        ins = nc.tensor.transpose(pb[0:MH, 4 + p, k * P:(k + 1) * P],
                                                  h[p][:, k * MH:(k + 1) * MH], ident[:])
                    ins.then_inc(h_turned[p], 1)

                def step(r, s, before, after):
                    if before >= 2:
                        e = expert_of(*off(r, s, -2))
                    if after:
                        turn_rows(*off(r, s, 1))
                    if before >= 1:
                        turn_hidden(*off(r, s, -1))
                    if before >= 2:
                        down(*off(r, s, -2), e)
                    if after:
                        gate_up(*off(r, s, 1), expert_of(*off(r, s, 1)))

                turn_rows(0, 0)
                gate_up(0, 0, expert_of(0, 0))
                for s in range(UNROLL):
                    step(0, s, s, True)
                with pe.Fori(1, ROUNDS - 1) as r:
                    for s in range(UNROLL):
                        step(r, s, 2, True)
                for s in range(UNROLL + 2):
                    if s <= UNROLL:
                        step(ROUNDS - 1, s, 2, s < UNROLL - 1)
                    else:
                        down(*off(ROUNDS - 1, s, -2), expert_of(*off(ROUNDS - 1, s, -2)))


_INS = ['L0_attn_x', 'L0_attn_wq', 'L0_attn_wk', 'L0_attn_wv', 'L0_attn_wo', 'L0_attn_fq1_w', 'L0_attn_fq1_b',
        'L0_attn_fq2_w', 'L0_attn_fq2_b', 'L0_attn_fk1_w', 'L0_attn_fk1_b', 'L0_attn_fk2_w', 'L0_attn_fk2_b',
        'L0_attn_norm_w', 'L0_ffn_w_router', 'L0_ffn_corr_bias', 'L0_ffn_gate_w', 'L0_ffn_up_w', 'L0_ffn_down_w',
        'L0_ffn_sh_gate_w', 'L0_ffn_sh_up_w', 'L0_ffn_sh_down_w']


def kernel(**inputs):
    import concourse.bacc as bacc
    from concourse.bass_utils import run_bass_kernel_spmd

    nc = bacc.Bacc("TRN2", target_bir_lowering=False, num_devices=1)
    arrays, args = {}, []
    for name in _INS:
        a = np.ascontiguousarray(inputs[name])
        arrays[f"in_{name}"] = a
        args.append(nc.dram_tensor(f"in_{name}", a.shape, mybir.dt.from_np(a.dtype), kind="ExternalInput").ap())
    out = nc.dram_tensor("out_0", (B, L, D), F32, kind="ExternalOutput").ap()
    moe_block_kernel(nc, *args, out)
    r = run_bass_kernel_spmd(nc, [arrays], core_ids=[0])
    return r.results[0]["out_0"]
```

```python
from contextlib import ExitStack

import numpy as np

import concourse.bass as bass
from concourse import mybir

F32 = mybir.dt.float32
BF16 = mybir.dt.bfloat16
I32 = mybir.dt.int32
U32 = mybir.dt.uint32
ALU = mybir.AluOpType
ACT = mybir.ActivationFunctionType
AX_X = mybir.AxisListType.X

P = 128
B, L, D = 2, 2048, 256
T = B * L
H, DK = 16, 16
KD = D // P
PAIRS = H // 2
SPAN = 256
ST = SPAN // P
QK_ORDER = (2, 3, 0, 1)
NSPAN = L // SPAN
E, M, TOPK, G, TOPK_G = 32, 176, 6, 8, 4
EG = E // G
MH = M // 2
MS = 2 * M
EPS = 1e-5
SCALE = DK ** -0.5
REGION = T + P
ROW = D + 1
NROWS = E * REGION + P
NTILES = (T * TOPK + E * (P - 1)) // P
UNROLL = 4
NT = -(-NTILES // UNROLL) * UNROLL
WIDE = 2 * M + 1
BIG = 3.0e38
MARK = 3.3e38
SP_TOK = 512
FREE = 1
ROUTE_LINKS = 19


def moe_block_kernel(nc, x, wq, wk, wv, wo, fq1_w, fq1_b, fq2_w, fq2_b, fk1_w, fk1_b, fk2_w, fk2_b,
                     norm_w, w_router, corr_bias, gate_w, up_w, down_w, sh_gate_w, sh_up_w,
                     sh_down_w, out):
    rows_d = nc.dram_tensor("rows_d", [NROWS, ROW], F32)
    x2_d = nc.dram_tensor("x2_d", [T, D], F32)
    x2nT_d = nc.dram_tensor("x2nT_d", [P, KD, T], F32)
    acc_d = [nc.dram_tensor(f"acc{n}_d", [T + P, D], F32) for n in range(2)]

    with ExitStack() as ctx:
        def sb(name, shape, dt=F32, stack=ctx):
            return stack.enter_context(nc.sbuf_tensor(name, shape, dt))

        def sem(name):
            return ctx.enter_context(nc.semaphore(name))

        def sems(name, n=2):
            return [sem(f"{name}{k}") for k in range(n)]

        ident = sb("ident", [P, P])
        wgu = sb("wgu", [P, E, KD, WIDE])
        wr = sb("wr", [P, KD, E])
        shg = sb("shg", [P, KD, MS])
        shu = sb("shu", [P, KD, MS])
        shd = sb("shd", [P, 3, D])
        next_row = sb("next_row", [P, E])
        first_row = sb("first_row", [P, E])
        zeros = sb("zeros", [P, D])
        part_i = sb("part_i", [P, 1], I32)
        part_f = sb("part_f", [P, 1])

        scattered = sems("scattered")
        gu_loaded = sem("gu_loaded")
        sh_loaded = sem("sh_loaded")
        router_cols = sem("router_cols")
        passed = sem("passed")

        phase_a(nc, ctx, sb, sem, sems, locals())
        phase_b(nc, ctx, sb, sem, sems, locals())


def bc(ap, axis, n):
    ap = ap.unsqueeze(axis)
    shape = list(ap.shape)
    shape[axis] = n
    return ap.to_broadcast(shape)


def apart(eng, sem, value, passed):
    eng.wait_ge(sem, value)
    eng.sem_inc(passed, 1)


def phase_a(nc, ctx, sb, sem, sems, g):
    x, rows_d, x2_d, x2nT_d = g["x"], g["rows_d"], g["x2_d"], g["x2nT_d"]
    ident, wgu, wr, next_row, first_row, zeros = (
        g[k] for k in ("ident", "wgu", "wr", "next_row", "first_row", "zeros"))
    scattered, gu_loaded, sh_loaded, router_cols, passed = (
        g[k] for k in ("scattered", "gu_loaded", "sh_loaded", "router_cols", "passed"))
    with ExitStack() as own:
        def t2(name, shape, dt=F32):
            return [sb(f"{name}{b}", shape, dt, own) for b in range(2)]

        def t1(name, shape, dt=F32):
            return sb(name, shape, dt, own)

        ones128 = t1("ones128", [P, P])
        hblock = t1("hblock", [P, 8, DK])
        kvmask = t1("kvmask", [P, P])
        hmean = t1("hmean", [P, P])
        cmask = t1("cmask", [P, P])
        tri = t1("tri", [P, P], BF16)
        onesb = t1("onesb", [P, P], BF16)
        head_on = t1("head_on", [P, 8])
        eps_col = t1("eps_col", [P, 1])
        ids = t1("ids", [P, T // P], I32)
        first_i = t1("first_i", [P, E], I32)
        cbias = t1("cbias", [P, E])
        rep16 = t1("rep16", [DK, 8, DK])
        f4 = t1("f4", [DK, 69])
        rep = t1("rep", [P, 69])
        wqk = t1("wqk", [P, 4, KD, D])
        wvT = t1("wvT", [P, KD, D])
        woT = t1("woT", [P, KD, D])
        xt = t2("xt", [P, ST, D])
        xr = t2("xr", [P, ST, D])
        bst = t2("bst", [P, ST, 6])
        mv = t2("mv", [P, ST, 2])
        std = t2("std", [P, ST])
        rstd = t2("rstd", [P, ST])
        xn = xt
        xnT = t2("xnT", [P, KD, SPAN])
        a1 = t1("a1", [P, 2, SPAN])
        kT = t2("kT", [P, 2, SPAN])
        qT = t2("qT", [P, 2, SPAN])
        qz = t2("qz", [P, 2, 8, P])
        vz = t2("vz", [P, ST, PAIRS, 3, DK])
        ktok = t2("ktok", [P, ST, 2, P])
        sT = t2("sT", [P, 4, 4, P])
        kvm = t2("kvm", [P, 2, P])
        sq = t2("sq", [P, 2, SPAN])
        ostd = sq
        nat = sT[0][:].rearrange("p n h m -> p (n h m)").rearrange("p (n r d) -> p n r d", n=4, r=KD)
        gsb = sq[0][:].rearrange("p f (h c) -> p (f h) c", c=P)
        fmap = sq[1][:].rearrange("p f (h c) -> p (f h) c", c=P)
        orstd = t1("orstd", [P, 2, SPAN])
        oT = t2("oT", [P, 2, SPAN])
        x2 = t2("x2", [P, ST, D])
        bst2 = t2("bst2_", [P, ST, 6])
        mv2 = t2("mv2_", [P, ST, 2])
        std2 = t2("std2_", [P, ST])
        rstd2 = t2("rstd2_", [P, ST])
        xp = t2("xp", [P, ST, ROW])
        x2nT = sq
        NB = 2 * ST
        score = t1("score", [P, NB, E])
        sfc = t1("sfc", [P, NB * G, EG])
        hi2 = t1("hi2", [P, NB * G, 2])
        lo2 = t1("lo2", [P, NB * G, 2])
        top1 = t1("top1", [P, NB * G])
        mid = t1("mid", [P, NB * G])
        top2 = t1("top2", [P, NB * G])
        gsc = t1("gsc", [P, NB, G])
        gtop = t1("gtop", [P, NB, 8])
        gpick = t1("gpick", [P, NB, 8])
        gmark = t1("gmark", [P, NB, G])
        gneg = t1("gneg", [P, NB * G])
        masked = t1("masked", [P, NB, E])
        etop = t1("etop", [P, NB, 8])
        epick = t1("epick", [P, NB, 8])
        emark = t1("emark", [P, NB, E])
        chosen = t1("chosen", [P, NB, E], BF16)
        slot = t1("slot", [P, NB, E])
        slotm = t1("slotm", [P, NB, E])
        stop8 = t1("stop8", [P, NB, 8])
        slots = t1("slots", [P, NB, 8], U32)

        pg = own.enter_context(nc.psum_tensor("pg", [P, 4, 512], F32))
        pkv = own.enter_context(nc.psum_tensor("pkv", [P, 2, 2 * P], F32))
        pr = own.enter_context(nc.psum_tensor("pr", [P, 512], F32))
        po = own.enter_context(nc.psum_tensor("po", [P, 2, 512], F32))

        attn_loaded = sem("attn_loaded")
        const_step = sem("const_step")
        consts_made = sem("consts_made")
        setup_pe = sem("setup_pe")
        setup_dve = sem("setup_dve")
        xr_loaded = sems("xr_loaded")
        x_loaded, x_stats, x_aggr, x_std, xn_made = (
            sems(n) for n in ("x_loaded", "x_stats", "x_aggr", "x_std", "xn_made"))
        x_rstd, x2_rstd, orstd_made = (sem(n) for n in ("x_rstd", "x2_rstd", "orstd_made"))
        xt_turned, xnT_made, proj_ready, a1_made, q_made = (
            sems(n) for n in ("xt_turned", "xnT_made", "proj_ready", "a1_made", "q_made"))
        qz_made = sem("qz_made")
        v_ready, vz_made, kt_ready, ktok_made = (
            sems(n) for n in ("v_ready", "vz_made", "kt_ready", "ktok_made"))
        s_ready = sem("s_ready")
        s_masked = sem("s_masked")
        kv_ready, kvm_made, o_ready, sq_made, ms_ready, ostd_made, oT_made = (
            sems(n) for n in ("kv_ready", "kvm_made", "o_ready", "sq_made", "ms_ready", "ostd_made",
                              "oT_made"))
        y_ready, x2_made, x2_stored, x2_stats, x2_aggr, x2_std, xp_made, id_made = (
            sems(n) for n in ("y_ready", "x2_made", "x2_stored", "x2_stats", "x2_aggr", "x2_std",
                              "xp_made", "id_made"))
        x2t_turned, x2nT_made, x2nT_stored = (
            sems(n) for n in ("x2t_turned", "x2nT_made", "x2nT_stored"))
        logit_ready = sem("logit_ready")
        score_made = sem("score_made")
        route_step = sem("route_step")
        chosen_made = sem("chosen_made")
        rank_ready = sem("rank_ready")
        slots_made = sem("slots_made")
        rank_read = sem("rank_read")
        dispatched = sems("dispatched")

        block = own.enter_context(nc.Block())

        def span(ap, b, i):
            return ap[bass.ds(b * L + i * SPAN, SPAN), :].rearrange("(t p) d -> p t d", p=P)

        x_rows = x.rearrange("b l d -> (b l) d")
        UNITS = ST * B

        @block.sync
        def _(sp):
            for n, w in enumerate((g["wq"], g["wk"], g["wv"], g["wo"])):
                sp.dma_start(nat[:, n, :, :], w.rearrange("(r p) d -> p r d", p=P)).then_inc(attn_loaded, 16)
            for n, w in enumerate((g["fq1_w"], g["fq2_w"], g["fk1_w"], g["fk2_w"])):
                sp.dma_start(f4[:, n * DK:(n + 1) * DK], w).then_inc(attn_loaded, 16)
            for n, v in enumerate((g["fq1_b"], g["fq2_b"], g["fk1_b"], g["fk2_b"], g["norm_w"])):
                sp.dma_start(f4[:, 64 + n:65 + n], v.unsqueeze(1)).then_inc(attn_loaded, 16)
            sp.dma_start(cbias[:], g["corr_bias"].partition_broadcast(P)).then_inc(attn_loaded, 16)
            sp.dma_start(wr[:], g["w_router"].rearrange("(k p) e -> p k e", p=P)).then_inc(attn_loaded, 16)

            def next_input(j):
                for b in range(B):
                    sp.wait_ge(xt_turned[b], FREE + j)
                    sp.dma_start(xt[b][:], span(x_rows, b, j)).then_inc(x_loaded[b], 16)

            def one_span(i, last):
                for b in range(B):
                    sp.wait_ge(x2_made[b], FREE + i)
                    sp.dma_start(xr[b][:], span(x_rows, b, i)).then_inc(xr_loaded[b], 16)
                if not last:
                    next_input(i + 1)
                for b in range(B):
                    sp.wait_ge(x2_made[b], FREE + i + 1)
                    sp.dma_start(span(x2_d, b, i), x2[b][:]).then_inc(x2_stored[b], 16)
                for b in range(B):
                    apart(sp, x2nT_made[b], FREE + i + 1, passed)
                    sp.dma_start(x2nT_d[:, :, bass.ds(b * L + i * SPAN, SPAN)], x2nT[b][:])\
                      .then_inc(x2nT_stored[b], 16)

            next_input(0)
            with sp.Fori(0, NSPAN - 1) as i:
                one_span(i, False)
            one_span(NSPAN - 1, True)
            for b in range(B):
                sp.wait_ge(x2_stored[b], FREE + 16 * NSPAN)
                sp.wait_ge(x2nT_stored[b], FREE + 16 * NSPAN)

        @block.gpsimd
        def _(pool):
            for free in (*xt_turned, *x2_made, *x2nT_stored, *x2_stored, *dispatched, *x2nT_made, score_made, rank_read, *oT_made):
                pool.sem_inc(free, FREE)
            n = 0

            def link(ins):
                nonlocal n
                n += 1
                ins.then_inc(const_step, 1)
                pool.wait_ge(const_step, n)

            def keep(t, pattern, base, mult, op=ALU.is_ge, fill=0.0):
                link(pool.affine_select(out=t, in_=t, compare_op=op, fill=fill, base=base,
                                        pattern=pattern, channel_multiplier=mult))

            link(pool.memset(ident[:], 0.0))
            keep(ident[:], [[-1, P]], 0, 1, ALU.not_equal, 1.0)
            link(pool.memset(ones128[:], 1.0))
            link(pool.memset(hblock[:], 1.0))
            keep(hblock[:], [[-DK, 8], [0, DK]], 0, 1)
            keep(hblock[:], [[DK, 8], [0, DK]], DK - 1, -1)
            link(pool.memset(cmask[:], SCALE))
            keep(cmask[:], [[1, P]], 0, -1)
            link(pool.memset(tri[:], 1.0))
            keep(tri[:], [[1, P]], -1, -1)
            link(pool.memset(onesb[:], 1.0))
            link(pool.memset(zeros[:], 0.0))
            link(pool.memset(eps_col[:], EPS))
            link(pool.iota(ids[:], pattern=[[P, T // P]], base=0, channel_multiplier=1))
            link(pool.iota(first_i[:], pattern=[[REGION, E]], base=1, channel_multiplier=0))
            link(pool.iota(g["part_i"][:], pattern=[[0, 1]], base=0, channel_multiplier=1))
            for b in range(B):
                link(pool.memset(vz[b][:], 0.0))
                link(pool.memset(kvm[b][:], 0.0))
            link(pool.memset(gpick[:], MARK))
            link(pool.memset(epick[:], MARK))
            pool.memset(a1[:, 0, 0:1], 0.0).then_inc(consts_made, 1)
            with pool.Fori(0, NSPAN) as i:
                apart(pool, slots_made, i + 1, passed)
                for b in range(B):
                    apart(pool, id_made[b], i + 1, passed)
                    for t in range(ST):
                        for k in range(TOPK):
                            pool.indirect_dma_start(
                                rows_d[:, :],
                                bass.IndirectOffsetOnAxis(ap=slots[:, b * ST + t, k:k + 1], axis=0),
                                xp[b][:, t, :], None).then_inc(scattered[b], 16)
                for b in range(B):
                    apart(pool, scattered[b], 16 * ST * TOPK * (i + 1), dispatched[b])
            for b in range(B):
                pool.wait_ge(scattered[b], 16 * ST * TOPK * NSPAN)

        @block.scalar
        def _(act):
            for k in range(KD):
                for w, at in ((g["gate_w"], 0), (g["up_w"], M + 1)):
                    act.dma_start(wgu[:, :, k, at:at + M],
                                  w[:, k * P:(k + 1) * P, :].rearrange("e p m -> p e m")).then_inc(gu_loaded, 16)
            act.dma_start(g["shg"][:], g["sh_gate_w"].rearrange("(k p) m -> p k m", p=P)).then_inc(sh_loaded, 16)
            act.dma_start(g["shu"][:], g["sh_up_w"].rearrange("(k p) m -> p k m", p=P)).then_inc(sh_loaded, 16)
            act.dma_start(g["shd"][:, 0:2, :], g["sh_down_w"][0:2 * P, :].rearrange("(k p) d -> p k d", p=P))\
               .then_inc(sh_loaded, 16)
            act.dma_start(g["shd"][0:MS - 2 * P, 2, :], g["sh_down_w"][2 * P:MS, :]).then_inc(sh_loaded, 16)
            act.wait_ge(consts_made, 1)
            act.wait_ge(setup_dve, 1)

            def input_std(j):
                for b in range(B):
                    act.wait_ge(x_aggr[b], ST * j + ST)
                    nc.scalar.activation(std[b][:], mv[b][:, :, 1], ACT.Sqrt, bias=eps_col[:, 0:1])\
                      .then_inc(x_std[b], 1)

            def input_turned(j):
                for b in range(B):
                    act.wait_ge(xt_turned[b], FREE + j + 1)
                    nc.scalar.activation(xnT[b][:], pg[:, 2 + b, :].rearrange("p (k t) -> p k t", k=KD), ACT.Copy)\
                      .then_inc(xnT_made[b], 1)

            def first_factor(j, b, o):
                r = QK_ORDER[o]
                act.wait_ge(proj_ready[b], 4 * j + o + 1)
                if o >= 2:
                    act.wait_ge(q_made[b], 4 * j + o - 1)
                elif b == 1:
                    act.wait_ge(q_made[0], 4 * j + o + 3)
                nc.scalar.activation(a1[:, o % 2, :], pg[:, (r + 2) % 4, 0:SPAN], ACT.Identity,
                                     bias=rep[:, 64 + 2 * (r // 2):65 + 2 * (r // 2)]).then_inc(a1_made[b], 1)

            def spread_q(i, u, heads):
                b, t = u % 2, u // 2
                act.wait_ge(q_made[b], 4 * i + 4)
                if u >= 2:
                    act.wait_ge(s_ready, 2 * UNITS * i + 2 * (u - 1))
                for h in heads:
                    ins = nc.scalar.activation(qz[u % 2][:, :, h, :], qT[b][:, :, t * P:(t + 1) * P], ACT.Copy,
                                               scale=head_on[:, h:h + 1])
                    ins.then_inc(qz_made, 1)

            def one_span(i, last):
                for o in range(2, 4):
                    first_factor(i, 0, o)
                for o in range(4):
                    first_factor(i, 1, o)
                    spread_q(i, 0, range(2 * o, 2 * o + 2))
                for b in range(B):
                    act.wait_ge(v_ready[b], i + 1)
                    nc.scalar.activation(vz[b][:, :, :, 0:3:2, :].rearrange("p t g a e -> p (t g) a e"),
                                         pg[:, b, :].rearrange("p (g a e) -> p g a e", a=2, e=DK), ACT.Copy)\
                      .then_inc(vz_made[b], 1)
                for b in range(B):
                    act.wait_ge(kt_ready[b], i + 1)
                    nc.scalar.activation(ktok[b][:].rearrange("p t f e -> p (t f e)"), pg[:, 2 + b, :], ACT.Copy)\
                      .then_inc(ktok_made[b], 1)
                for u in range(1, UNITS):
                    spread_q(i, u, range(8))
                if not last:
                    input_std(i + 1)
                for b in range(B):
                    act.wait_ge(o_ready[b], ST * (i + 1))
                    act.wait_ge(x2nT_stored[b], FREE + 16 * i)
                    nc.scalar.activation(sq[b][:].rearrange("p f t -> p (f t)"), po[:, b, :], ACT.Square)\
                      .then_inc(sq_made[b], 1)
                if not last:
                    input_turned(i + 1)
                for b in range(B):
                    act.wait_ge(ms_ready[b], i + 1)
                    nc.scalar.activation(ostd[b][:].rearrange("p f t -> p (f t)"), pg[:, b, :], ACT.Sqrt,
                                         bias=eps_col[:, 0:1]).then_inc(ostd_made[b], 1)
                for b in range(B):
                    act.wait_ge(x2_aggr[b], ST * i + ST)
                    nc.scalar.activation(std2[b][:], mv2[b][:, :, 1], ACT.Sqrt, bias=eps_col[:, 0:1])\
                      .then_inc(x2_std[b], 1)
                    if not last:
                        first_factor(i + 1, 0, b)
                for b in range(B):
                    act.wait_ge(x2t_turned[b], i + 1)
                    act.wait_ge(oT_made[b], FREE + i + 1)
                    nc.scalar.activation(x2nT[b][:], pg[:, 2 + b, :].rearrange("p (k t) -> p k t", k=KD), ACT.Copy)\
                      .then_inc(x2nT_made[b], 1)
                act.wait_ge(logit_ready, i + 1)
                nc.scalar.activation(score[:].rearrange("p n e -> p (n e)"), pr[:, 2 * P:2 * P + NB * E],
                                     ACT.Sigmoid).then_inc(score_made, 1)

            input_std(0)
            input_turned(0)
            for o in range(2):
                first_factor(0, 0, o)
            with act.Fori(0, NSPAN - 1) as i:
                one_span(i, False)
            one_span(NSPAN - 1, True)

        @block.vector
        def _(dve):
            n = 0

            def link(ins):
                nonlocal n
                n += 1
                ins.then_inc(route_step, 1)
                dve.wait_ge(route_step, n)

            dve.wait_ge(consts_made, 1)
            link(nc.vector.tensor_copy(rep16[:], bc(ident[0:DK, 0:DK], 1, 8)))
            link(nc.vector.tensor_scalar(kvmask[:], hblock[:].rearrange("p h d -> p (h d)"), SCALE, None, ALU.mult))
            link(nc.vector.tensor_scalar(hmean[:], hblock[:].rearrange("p h d -> p (h d)"), 1.0 / DK, None, ALU.mult))
            link(nc.vector.tensor_copy(head_on[:], hblock[:, :, 0]))
            link(nc.vector.tensor_copy(first_row[:], first_i[:]))
            link(nc.vector.tensor_copy(next_row[:], first_i[:]))
            link(nc.vector.tensor_copy(g["part_f"][:], g["part_i"][:]))
            nc.vector.memset(kT[0][:, 0, 0:1], 0.0).then_inc(setup_dve, 1)
            dve.wait_ge(setup_pe, 1)
            link(nc.vector.tensor_copy(rep[:], pg[:, 0, 0:69]))
            for m in range(4):
                link(nc.vector.tensor_tensor(gsb[:, m, :].rearrange("p (h d) -> p h d", d=DK),
                                             bc(rep[:, m * DK:(m + 1) * DK], 1, 8), hblock[:], ALU.mult))
            nc.vector.memset(kT[0][:, 0, 1:2], 0.0).then_inc(setup_dve, 1)
            dve.wait_ge(setup_pe, 2)
            link(nc.vector.tensor_copy(fmap.rearrange("p m c -> p (m c)"), pg[:, 1, :]))
            link(nc.vector.tensor_copy(wvT[:].rearrange("p k d -> p (k d)"), pg[:, 2, :]))
            link(nc.vector.tensor_scalar(woT[:].rearrange("p k d -> p (k d)"), pg[:, 3, :], rep[:, 68:69], None,
                                         ALU.mult))
            nc.vector.memset(kT[0][:, 0, 2:3], 0.0).then_inc(setup_dve, 1)
            dve.wait_ge(setup_pe, 3)
            for m in range(4):
                link(nc.vector.tensor_copy(wqk[:, m, :, :].rearrange("p k d -> p (k d)"), pg[:, m, :]))
            nc.vector.memset(kT[0][:, 0, 3:4], 0.0).then_inc(setup_dve, 1)
            setup_links = n

            def layer_stats(src, ready, st, m, stats, aggr, b, i):
                for t in range(ST):
                    ready(t)
                    nc.vector.bn_stats(st[b][:, t, :], src[b][:, t, :]).then_inc(stats[b], 1)
                for t in range(ST):
                    apart(dve, stats[b], ST * i + t + 1, passed)
                    nc.vector.bn_aggr(m[b][:, t, :], st[b][:, t, :]).then_inc(aggr[b], 1)

            def input_stats(j):
                for b in range(B):
                    layer_stats(xt, lambda t: dve.wait_ge(x_loaded[b], 16 * j + 16), bst, mv, x_stats, x_aggr, b, j)

            def input_normal(j):
                for b in range(B):
                    dve.wait_ge(x_std[b], j + 1)
                    nc.vector.reciprocal(rstd[b][:], std[b][:]).then_inc(x_rstd, 1)
                    dve.wait_ge(x_rstd, B * j + (b + 1))
                    for t in range(ST):
                        nc.vector.tensor_scalar(xn[b][:, t, :], xt[b][:, t, :], mv[b][:, t, 0:1], rstd[b][:, t:t + 1],
                                                ALU.subtract, ALU.mult).then_inc(xn_made[b], 1)

            def second_factor(i, b, o):
                r = QK_ORDER[o]
                f = r % 2
                dst = qT[b][:, f, :] if r < 2 else kT[b][:, f, :]
                dve.wait_ge(a1_made[b], 4 * i + o + 1)
                nc.vector.scalar_tensor_tensor(
                    out=dst, in0=pg[:, (r + 2) % 4, SPAN:2 * SPAN],
                    scalar=rep[:, 65 + 2 * (r // 2):66 + 2 * (r // 2)], in1=a1[:, o % 2, :],
                    op0=ALU.add, op1=ALU.mult).then_inc(q_made[b], 1)

            def mask_scores(i, u):
                for g in range(2):
                    dve.wait_ge(s_ready, 2 * UNITS * i + 2 * u + g + 1)
                    nc.vector.tensor_tensor(
                        sT[u % 2][:, 2 * g:2 * g + 2, :, :].rearrange("p n h m -> p (n h) m"),
                        pg[:, 2 * g:2 * g + 2, :].rearrange("p n (h m) -> p (n h) m", m=P),
                        bc(cmask[:], 1, 8), ALU.mult).then_inc(s_masked, 1)

            def mask_state(i, u):
                b = u % 2
                dve.wait_ge(kv_ready[b], ST * i + u // 2 + 1)
                nc.vector.tensor_tensor(kvm[b][:], pkv[:, b, 0:2 * P].rearrange("p (f e) -> p f e", f=2),
                                        bc(kvmask[:], 1, 2), ALU.mult).then_inc(kvm_made[b], 1)

            def routing(j):
                k0 = 0

                def step(ins):
                    nonlocal k0
                    k0 += 1
                    ins.then_inc(route_step, 1)
                    apart(dve, route_step, ROUTE_LINKS * j + (setup_links + k0), passed)

                def group_scores():
                    dve.wait_ge(score_made, FREE + j + 1)
                    step(nc.vector.tensor_tensor(sfc[:].rearrange("p (n g) e -> p n (g e)", g=G), score[:],
                                                 bc(cbias[:], 1, NB), ALU.add))
                    step(nc.vector.tensor_tensor(hi2[:], sfc[:, :, 0:2], sfc[:, :, 2:4], ALU.max))
                    step(nc.vector.tensor_tensor(lo2[:], sfc[:, :, 0:2], sfc[:, :, 2:4], ALU.min))
                    step(nc.vector.tensor_tensor(top1[:], hi2[:, :, 0], hi2[:, :, 1], ALU.max))
                    step(nc.vector.tensor_tensor(mid[:], hi2[:, :, 0], hi2[:, :, 1], ALU.min))
                    step(nc.vector.tensor_tensor(top2[:], lo2[:, :, 0], lo2[:, :, 1], ALU.max))
                    step(nc.vector.tensor_tensor(top2[:], top2[:], mid[:], ALU.max))
                    step(nc.vector.tensor_tensor(gsc[:].rearrange("p n g -> p (n g)"), top1[:], top2[:], ALU.add))

                def pick_groups():
                    for n in range(NB):
                        ins = nc.vector.max(gtop[:, n, :], gsc[:, n, :])
                    step(ins)
                    step(nc.vector.tensor_copy(gpick[:, :, 0:TOPK_G], gtop[:, :, 0:TOPK_G]))
                    for n in range(NB):
                        ins = nc.vector.match_replace(gmark[:, n, :], gpick[:, n, :], gsc[:, n, :], MARK)
                    step(ins)
                    step(nc.vector.tensor_scalar(gneg[:], gmark[:].rearrange("p n g -> p (n g)"), BIG, -BIG,
                                                 ALU.is_lt, ALU.mult))
                    step(nc.vector.tensor_tensor(masked[:].rearrange("p n (g e) -> p (n g) e", g=G), sfc[:],
                                                 bc(gneg[:], 2, EG), ALU.add))

                def pick_experts():
                    for n in range(NB):
                        ins = nc.vector.max(etop[:, n, :], masked[:, n, :])
                    step(ins)
                    step(nc.vector.tensor_copy(epick[:, :, 0:TOPK], etop[:, :, 0:TOPK]))
                    for n in range(NB):
                        ins = nc.vector.match_replace(emark[:, n, :], epick[:, n, :], masked[:, n, :], MARK)
                    step(ins)
                    nc.vector.tensor_scalar(chosen[:], emark[:], BIG, None, ALU.is_gt).then_inc(chosen_made, 1)

                def find_rows():
                    dve.wait_ge(rank_ready, j + 1)
                    step(nc.vector.tensor_tensor(slot[:], pr[:, 0:NB * E].rearrange("p (n e) -> p n e", e=E),
                                                 bc(next_row[:], 1, NB), ALU.add))
                    step(nc.vector.tensor_tensor(slotm[:], slot[:], chosen[:], ALU.mult))
                    for n in range(NB):
                        ins = nc.vector.max(stop8[:, n, :], slotm[:, n, :])
                    step(ins)
                    for b in range(B):
                        dve.wait_ge(dispatched[b], FREE + j)
                    nc.vector.tensor_scalar(slots[:], stop8[:], -1.0, None, ALU.add).then_inc(slots_made, 1)
                    nc.vector.tensor_tensor(next_row[:], pr[:, NB * E:(NB + 1) * E], next_row[:], ALU.add)\
                      .then_inc(rank_read, 1)
                    dve.wait_ge(slots_made, j + 1)
                    dve.wait_ge(rank_read, FREE + j + 1)
                    assert k0 == ROUTE_LINKS, k0

                return group_scores, pick_groups, pick_experts, find_rows

            def one_span(i, first, last):
                parts = [lambda: None] * 4 if first else routing(i - 1)
                for b in range(B):
                    for o in range(2):
                        second_factor(i, b, o)
                    parts[2 * b]()
                    for o in range(2, 4):
                        second_factor(i, b, o)
                    if b == 0:
                        parts[1]()
                if not last:
                    input_stats(i + 1)
                parts[3]()
                mask_scores(i, 0)
                mask_scores(i, 1)
                for u in range(UNITS):
                    mask_state(i, u)
                    if u + 2 < UNITS:
                        mask_scores(i, u + 2)
                    elif u + 2 == UNITS and not last:
                        input_normal(i + 1)
                for b in range(B):
                    dve.wait_ge(ostd_made[b], i + 1)
                    nc.vector.reciprocal(orstd[:], ostd[b][:]).then_inc(orstd_made, 1)
                    dve.wait_ge(orstd_made, B * i + (b + 1))
                    nc.vector.tensor_tensor(oT[b][:].rearrange("p f t -> p (f t)"), po[:, b, :],
                                            orstd[:].rearrange("p f t -> p (f t)"), ALU.mult).then_inc(oT_made[b], 1)
                    dve.wait_ge(oT_made[b], FREE + i + 1)
                for b in range(B):
                    dve.wait_ge(y_ready[b], i + 1)
                    dve.wait_ge(xr_loaded[b], 16 * i + 16)
                    dve.wait_ge(x2_stored[b], FREE + 16 * i)
                    nc.vector.tensor_tensor(x2[b][:], pg[:, 2 + b, :].rearrange("p (t d) -> p t d", t=ST), xr[b][:],
                                            ALU.add).then_inc(x2_made[b], 1)
                    dve.wait_ge(x2_made[b], FREE + i + 1)
                    layer_stats(x2, lambda t: None, bst2, mv2, x2_stats, x2_aggr, b, i)
                for b in range(B):
                    dve.wait_ge(x2_std[b], i + 1)
                    nc.vector.reciprocal(rstd2[b][:], std2[b][:]).then_inc(x2_rstd, 1)
                    dve.wait_ge(x2_rstd, B * i + (b + 1))
                    dve.wait_ge(dispatched[b], FREE + i)
                    for t in range(ST):
                        nc.vector.tensor_scalar(xp[b][:, t, 0:D], x2[b][:, t, :], mv2[b][:, t, 0:1],
                                                rstd2[b][:, t:t + 1], ALU.subtract, ALU.mult).then_inc(xp_made[b], 1)
                    nc.vector.tensor_copy(xp[b][:, :, D:ROW].bitcast(I32),
                                          ids[:, bass.ds((L // P) * b + ST * i, ST)].unsqueeze(2)).then_inc(id_made[b], 1)

            input_stats(0)
            input_normal(0)
            one_span(0, True, False)
            with dve.Fori(1, NSPAN - 1) as i:
                one_span(i, False, False)
            one_span(NSPAN - 1, False, True)
            for part in routing(NSPAN - 1):
                part()
            dve.wait_ge(attn_loaded, 16 * 15)
            nc.vector.tensor_copy(wgu[:, :, :, M].rearrange("p e k -> p k e"), wr[:]).then_inc(router_cols, 1)

        @block.tensor
        def _(pe):
            pe.wait_ge(consts_made, 1)
            pe.wait_ge(setup_dve, 1)
            pe.wait_ge(attn_loaded, 16 * 15)
            nc.tensor.matmul(pg[:, 0, 0:69], rep16[:].rearrange("p h d -> p (h d)"), f4[:], start=True, stop=True)\
              .then_inc(setup_pe, 1)
            for n, bank in ((2, 2), (3, 3)):
                for k in range(KD):
                    for r in range(KD):
                        ins = nc.tensor.transpose(pg[:, bank, (k * KD + r) * P:(k * KD + r + 1) * P],
                                                  nat[:, n, r, k * P:(k + 1) * P], ident[:])
            pe.wait_ge(setup_dve, 2)
            for m in range(4):
                ins = nc.tensor.transpose(pg[:, 1, m * P:(m + 1) * P], gsb[:, m, :], ident[:])
            ins.then_inc(setup_pe, 1)
            pe.wait_ge(setup_dve, 3)
            for m in range(4):
                for k in range(KD):
                    for f in range(2):
                        ins = nc.tensor.matmul(pg[:, m, (k * 2 + f) * P:(k * 2 + f + 1) * P],
                                               nat[:, m // 2, f, k * P:(k + 1) * P], fmap[:, m, :],
                                               start=True, stop=True)
            ins.then_inc(setup_pe, 1)
            for b in range(B):
                nc.tensor.matmul(pkv[:, b, 0:2 * P], ident[:], zeros[:, 0:2 * P], start=True, stop=True)
            pe.wait_ge(setup_dve, 4)

            def turn(src, b, bank):
                for k in range(KD):
                    for t in range(ST):
                        ins = nc.tensor.transpose(pg[:, bank, k * SPAN + t * P:k * SPAN + (t + 1) * P],
                                                  src[b][:, t, k * P:(k + 1) * P], ident[:])
                return ins

            def turn_input(j):
                for b in range(B):
                    pe.wait_ge(xn_made[b], ST * j + ST)
                    turn(xn, b, 2 + b).then_inc(xt_turned[b], 1)

            def project(j, b, o):
                r = QK_ORDER[o]
                for m in range(2):
                    for k in range(KD):
                        ins = nc.tensor.matmul(pg[:, (r + 2) % 4, m * SPAN:(m + 1) * SPAN],
                                               wqk[:, 2 * (r // 2) + m, k, (r % 2) * P:(r % 2 + 1) * P],
                                               xnT[b][:, k, :], start=(k == 0), stop=(k == KD - 1))
                ins.then_inc(proj_ready[b], 1)

            def project_ahead(j):
                for b in range(B):
                    pe.wait_ge(xnT_made[b], j + 1)
                for o in range(2):
                    project(j, 0, o)

            def scores(i, u):
                b, t = u % 2, u // 2
                pe.wait_ge(qz_made, 8 * UNITS * i + 8 * u + 8)
                for f in range(2):
                    if u == 0:
                        for bb in range(B):
                            pe.wait_ge((vz_made, ktok_made)[f][bb], i + 1)
                    else:
                        pe.wait_ge(s_masked, 2 * UNITS * i + 2 * (u - 1) + f + 1)
                    for half in range(2):
                        ins = nc.tensor.matmul(pg[:, 2 * f + half, :], kT[b][:, f, t * P:(t + 1) * P],
                                               qz[u % 2][:, f, 4 * half:4 * half + 4, :].rearrange("p h m -> p (h m)"),
                                               start=True, stop=True)
                    ins.then_inc(s_ready, 1)

            def outputs(i, u):
                b, t = u % 2, u // 2
                if t == 0:
                    pe.wait_ge(oT_made[b], FREE + i)
                else:
                    pe.wait_ge(kvm_made[b], ST * i + t)
                pe.wait_ge(s_masked, 2 * UNITS * i + 2 * u + 2)
                for f in range(2):
                    cols = slice(f * SPAN + t * P, f * SPAN + (t + 1) * P)
                    nc.tensor.matmul(po[:, b, cols], kvm[b][:, f, :], qT[b][:, f, t * P:(t + 1) * P],
                                     start=True, stop=False, skip_group_check=True)
                    for a in range(2):
                        for q in range(4):
                            ins = nc.tensor.matmul(
                                po[32 * q:32 * q + 32, b, cols],
                                vz[b][:, t, 4 * f + q, a:a + 2, :].rearrange("p a e -> p (a e)"),
                                sT[u % 2][:, 2 * f + q // 2, 2 * (q % 2) + a, :], start=False, stop=(a == 1 and q == 3),
                                skip_group_check=True)
                ins.then_inc(o_ready[b], 1)

            def add_state(i, u):
                b, t = u % 2, u // 2
                if u:
                    pe.wait_ge(kvm_made[1 - b], ST * i + (t + b))
                for f in range(2):
                    ins = nc.tensor.matmul(pkv[:, b, f * P:(f + 1) * P], ktok[b][:, t, f, :],
                                           vz[b][:, t, 4 * f:4 * f + 4, 0:3:2, :],
                                           start=False, stop=True, skip_group_check=True)
                ins.then_inc(kv_ready[b], 1)

            def rank(j):
                pe.wait_ge(chosen_made, j + 1)
                for n in range(NB):
                    dst = pr[:, n * E:(n + 1) * E]
                    nc.tensor.matmul(dst, tri[:], chosen[:, n, :], start=True, stop=(n == 0))
                    for before in range(n):
                        nc.tensor.matmul(dst, onesb[:], chosen[:, before, :], start=False, stop=(before == n - 1))
                for n in range(NB):
                    ins = nc.tensor.matmul(pr[:, NB * E:(NB + 1) * E], onesb[:], chosen[:, n, :],
                                           start=(n == 0), stop=(n == NB - 1))
                ins.then_inc(rank_ready, 1)

            def one_span(i, first, last):
                for b in range(B):
                    pe.wait_ge(x2nT_made[b], FREE + i)
                for o in range(2, 4):
                    project(i, 0, o)
                for o in range(4):
                    pe.wait_ge(q_made[0], 4 * i + o + 1)
                    project(i, 1, o)
                if not first:
                    rank(i - 1)
                for b in range(B):
                    pe.wait_ge(q_made[1], 4 * i + b + 1)
                    for t in range(ST):
                        for k in range(KD):
                            ins = nc.tensor.matmul(pg[:, b, t * D:(t + 1) * D], xnT[b][:, k, t * P:(t + 1) * P],
                                                   wvT[:, k, :], start=(k == 0), stop=(k == KD - 1))
                    ins.then_inc(v_ready[b], 1)
                for b in range(B):
                    pe.wait_ge(q_made[1], 4 * i + b + 3)
                    for t in range(ST):
                        for f in range(2):
                            ins = nc.tensor.transpose(pg[:, 2 + b, (2 * t + f) * P:(2 * t + f + 1) * P],
                                                      kT[b][:, f, t * P:(t + 1) * P], ident[:])
                    ins.then_inc(kt_ready[b], 1)
                scores(i, 0)
                for u in range(UNITS):
                    if u + 1 < UNITS:
                        scores(i, u + 1)
                    outputs(i, u)
                    add_state(i, u)
                if not last:
                    turn_input(i + 1)
                for b in range(B):
                    pe.wait_ge(sq_made[b], i + 1)
                    nc.tensor.matmul(pg[:, b, :], hmean[:], sq[b][:].rearrange("p f t -> p (f t)"),
                                     start=True, stop=True).then_inc(ms_ready[b], 1)
                for b in range(B):
                    pe.wait_ge(oT_made[b], FREE + i + 1)
                    if not last:
                        pe.wait_ge(xnT_made[b], i + 2)
                    for t in range(ST):
                        for f in range(2):
                            ins = nc.tensor.matmul(pg[:, 2 + b, t * D:(t + 1) * D], oT[b][:, f, t * P:(t + 1) * P],
                                                   woT[:, f, :], start=(f == 0), stop=(f == 1))
                    ins.then_inc(y_ready[b], 1)
                if not last:
                    project_ahead(i + 1)
                for b in range(B):
                    pe.wait_ge(xp_made[b], ST * i + ST)
                    turn(xp, b, 2 + b).then_inc(x2t_turned[b], 1)
                for b in range(B):
                    pe.wait_ge(x2nT_made[b], FREE + i + 1)
                    for t in range(ST):
                        for k in range(KD):
                            n = b * ST + t
                            ins = nc.tensor.matmul(pr[:, 2 * P + n * E:2 * P + (n + 1) * E],
                                                   x2nT[b][:, k, t * P:(t + 1) * P],
                                                   wr[:, k, :], start=(k == 0), stop=(k == KD - 1))
                ins.then_inc(logit_ready, 1)

            turn_input(0)
            project_ahead(0)
            one_span(0, True, False)
            with pe.Fori(1, NSPAN - 1) as i:
                one_span(i, False, False)
            one_span(NSPAN - 1, False, True)
            rank(NSPAN - 1)


def phase_b(nc, ctx, sb, sem, sems, g):
    rows_d, x2_d, x2nT_d, acc_d, out = (g[k] for k in ("rows_d", "x2_d", "x2nT_d", "acc_d", "out"))
    ident, wgu, shg, shu, shd, next_row, first_row, zeros, part_f = (
        g[k] for k in ("ident", "wgu", "shg", "shu", "shd", "next_row", "first_row", "zeros", "part_f"))
    with ExitStack() as own:
        def t1(name, shape, dt=F32):
            return sb(name, shape, dt, own)

        wd = t1("wd", [P, E, 2, D])
        pad_row = t1("pad_row", [P, ROW])
        pad_slots = t1("pad_slots", [P, E + 1], U32)
        pad_f = t1("pad_f", [P, E + 1])
        jj_i = t1("jj_i", [P, 2], I32)
        jj = t1("jj", [P, 2])
        cnt = t1("cnt", [P, E])
        cnt_i = t1("cnt_i", [P, E], I32)
        tiles_of = t1("tiles_of", [P, E])
        tile_end = t1("tile_end", [P, E])
        onesE = t1("onesE", [P, E])
        before = t1("before", [P, 2, E])
        started = t1("started", [P, 2, E])
        expert = t1("expert", [P, 2])
        tile_at = t1("tile_at", [P, 2])
        inside = t1("inside", [P, 2])
        table = t1("table", [P, 4])
        table_i = t1("table_i", [1, 4, P], I32)
        shared = ExitStack()

        def t3(name, shape):
            return sb(name, shape, F32, shared)

        xs = [t3(f"xs{s}", [P, KD, SP_TOK]) for s in range(2)]
        x2s = [t3(f"x2s{s}", [P, 4, D]) for s in range(2)]
        sig = [t3(f"sig{s}", [P, SP_TOK]) for s in range(2)]
        sgu = [t3(f"sgu{s}", [P, SP_TOK]) for s in range(2)]
        hs = [t3(f"hs{s}", [P, SP_TOK]) for s in range(3)]
        ys = [t3(f"ys{s}", [P, 4, D]) for s in range(2)]

        pb = own.enter_context(nc.psum_tensor("pb", [P, 8, 512], F32))

        down_loaded = sem("down_loaded")
        pool_step = sem("pool_step")
        pad_made = sem("pad_made")
        padded = sem("padded")
        table_step = sem("table_step")
        table_made = sem("table_made")
        table_turned = sem("table_turned")
        table_ready = sem("table_ready")
        zeroed = sem("zeroed")
        xs_loaded, x2s_loaded, sh_stored = (sems(n) for n in ("xs_loaded", "x2s_loaded", "sh_stored"))
        gate_ready, sig_made, sgu_made, hs_made, sh_y_ready, ys_made = (
            sems(n) for n in ("gate_ready", "sig_made", "sgu_made", "hs_made", "sh_y_ready", "ys_made"))

        FT = [(0, P), (P, P), (2 * P, MS - 2 * P)]
        NSH = T // SP_TOK

        block = shared.enter_context(nc.Block())

        @block.sync
        def _(sp):
            with sp.Fori(0, NSH // 2) as i:
                for s in range(2):
                    at = (2 * i + s) * SP_TOK
                    sp.wait_ge(sh_stored[s], FREE + 16 * i)
                    sp.dma_start(xs[s][:], x2nT_d[:, :, bass.ds(at, SP_TOK)]).then_inc(xs_loaded[s], 16)
                    sp.dma_start(x2s[s][:], x2_d[bass.ds(at, SP_TOK), :].rearrange("(t p) d -> p t d", p=P))\
                      .then_inc(x2s_loaded[s], 16)
                for s in range(2):
                    at = (2 * i + s) * SP_TOK
                    sp.wait_ge(ys_made[s], FREE + 2 * i + 2)
                    sp.dma_start(acc_d[0][bass.ds(at, SP_TOK), :].rearrange("(t p) d -> p t d", p=P), ys[s][:])\
                      .then_inc(sh_stored[s], 16)
            for s in range(2):
                sp.wait_ge(sh_stored[s], FREE + 16 * (NSH // 2))

        @block.scalar
        def _(act):
            for h in range(2):
                act.dma_start(wd[0:MH, :, h, :],
                              g["down_w"][:, h * MH:(h + 1) * MH, :].rearrange("e p d -> p e d")).then_inc(down_loaded, 16)
            for n in range(T // P + 1):
                act.dma_start(acc_d[1][n * P:(n + 1) * P, :], zeros[:]).then_inc(zeroed, 16)
            act.dma_start(acc_d[0][T:T + P, :], zeros[:]).then_inc(zeroed, 16)
            act.wait_ge(g["sh_loaded"], 64)
            with act.Fori(0, NSH // 2) as i:
                for s in range(2):
                    for n, (f0, fn) in enumerate(FT):
                        p = n % 2
                        u = (3 * s + n) // 2
                        q = (3 * s + n) % 2
                        act.wait_ge(gate_ready[q], 3 * i + u + 1)
                        nc.scalar.activation(sig[q][0:fn, :], pb[0:fn, 2 * q, :], ACT.Sigmoid).then_inc(sig_made[q], 1)
            act.wait_ge(zeroed, 16 * (T // P + 2))
            act.wait_ge(down_loaded, 32)

        @block.gpsimd
        def _(pool):
            for free in (*sh_stored, *hs_made, *sh_y_ready, *ys_made):
                pool.sem_inc(free, FREE)
            n = 0

            def link(ins):
                nonlocal n
                n += 1
                ins.then_inc(pool_step, 1)
                pool.wait_ge(pool_step, n)

            link(pool.memset(pad_row[:], 0.0))
            link(pool.iota(pad_row[:, D:ROW].bitcast(I32), pattern=[[0, 1]], base=T, channel_multiplier=1))
            link(pool.iota(jj_i[:], pattern=[[P, 2]], base=0, channel_multiplier=1))
            link(pool.memset(onesE[:], 1.0))
            pool.wait_ge(pad_made, 1)
            for e in range(E + 1):
                pool.indirect_dma_start(rows_d[:, :], bass.IndirectOffsetOnAxis(ap=pad_slots[:, e:e + 1], axis=0),
                                        pad_row[:], None).then_inc(padded, 16)
            pool.wait_ge(padded, 16 * (E + 1))

        @block.vector
        def _(dve):
            n = 0

            def link(ins):
                nonlocal n
                n += 1
                ins.then_inc(table_step, 1)
                dve.wait_ge(table_step, n)

            link(nc.vector.tensor_scalar(pad_f[:, 0:E], next_row[:], part_f[:, 0:1], -1.0, ALU.add, ALU.add))
            link(nc.vector.tensor_scalar(pad_f[:, E:E + 1], part_f[:], float(E * REGION), None, ALU.add))
            nc.vector.tensor_copy(pad_slots[:], pad_f[:]).then_inc(pad_made, 1)
            dve.wait_ge(pool_step, 4)
            link(nc.vector.tensor_tensor(cnt[:], next_row[:], first_row[:], ALU.subtract))
            link(nc.vector.tensor_scalar(cnt_i[:], cnt[:], float(P - 1), None, ALU.add))
            link(nc.vector.tensor_scalar(cnt_i[:], cnt_i[:], 7, None, ALU.logical_shift_right))
            link(nc.vector.tensor_copy(tiles_of[:], cnt_i[:]))
            link(nc.vector.tensor_tensor_scan(tile_end[:], onesE[:], tiles_of[:], 0.0, ALU.mult, ALU.add))
            link(nc.vector.tensor_copy(jj[:], jj_i[:]))
            link(nc.vector.tensor_tensor(before[:], bc(tile_end[:], 1, 2), bc(jj[:], 2, E), ALU.is_le))
            link(nc.vector.tensor_reduce(expert[:], before[:], AX_X, ALU.add))
            link(nc.vector.tensor_tensor(started[:], before[:], bc(tiles_of[:], 1, 2), ALU.mult))
            link(nc.vector.tensor_reduce(tile_at[:], started[:], AX_X, ALU.add))
            link(nc.vector.tensor_tensor(tile_at[:], jj[:], tile_at[:], ALU.subtract))
            link(nc.vector.tensor_scalar(inside[:], expert[:], float(E) - 0.5, float(P), ALU.is_lt, ALU.mult))
            link(nc.vector.tensor_tensor(tile_at[:], tile_at[:], inside[:], ALU.mult))
            link(nc.vector.scalar_tensor_tensor(out=table[:, 0:2], in0=expert[:], scalar=float(REGION), in1=tile_at[:],
                                                op0=ALU.mult, op1=ALU.add))
            link(nc.vector.tensor_scalar(table[:, 2:4], expert[:], float(E - 1), None, ALU.min))
            nc.vector.memset(cnt[:, 0:1], 0.0).then_inc(table_made, 1)
            dve.wait_ge(table_turned, 1)
            nc.vector.tensor_copy(table_i[:].rearrange("p n t -> p (n t)"), pb[0:1, 7, :]).then_inc(table_ready, 1)
            with dve.Fori(0, NSH // 2) as i:
                for s in range(2):
                    for n, (f0, fn) in enumerate(FT):
                        u = (3 * s + n) // 2
                        q = (3 * s + n) % 2
                        dve.wait_ge(sig_made[q], 3 * i + u + 1)
                        nc.vector.tensor_tensor(sgu[q][0:fn, :], pb[0:fn, 2 * q, :], sig[q][0:fn, :], ALU.mult)\
                          .then_inc(sgu_made[q], 1)
                        dve.wait_ge(sgu_made[q], 3 * i + u + 1)
                        if s == 0:
                            dve.wait_ge(sh_y_ready[1], FREE + i)
                        else:
                            dve.wait_ge(sh_y_ready[0], FREE + i + 1)
                        nc.vector.tensor_tensor(hs[n][0:fn, :], pb[0:fn, 2 * q + 1, :], sgu[q][0:fn, :], ALU.mult)\
                          .then_inc(hs_made[q], 1)
                    dve.wait_ge(x2s_loaded[s], 16 * i + 16)
                    dve.wait_ge(sh_y_ready[s], FREE + i + 1)
                    dve.wait_ge(sh_stored[s], FREE + 16 * i)
                    for half in range(2):
                        nc.vector.tensor_tensor(ys[s][:, 2 * half:2 * half + 2, :],
                                                pb[:, 4 + half, :].rearrange("p (t d) -> p t d", t=2),
                                                x2s[s][:, 2 * half:2 * half + 2, :], ALU.add).then_inc(ys_made[s], 1)

        @block.tensor
        def _(pe):
            pe.wait_ge(table_made, 1)
            for n in range(4):
                ins = nc.tensor.transpose(pb[0:1, 7, n * P:(n + 1) * P], table[:, n:n + 1], ident[:])
            ins.then_inc(table_turned, 1)
            pe.wait_ge(g["sh_loaded"], 64)
            with pe.Fori(0, NSH // 2) as i:
                for s in range(2):
                    pe.wait_ge(xs_loaded[s], 16 * i + 16)
                    for n, (f0, fn) in enumerate(FT):
                        u = (3 * s + n) // 2
                        q = (3 * s + n) % 2
                        pe.wait_ge(hs_made[q], FREE + 3 * i + u)
                        for w, bank in ((shg, 2 * q), (shu, 2 * q + 1)):
                            for k in range(KD):
                                ins = nc.tensor.matmul(pb[0:fn, bank, :], w[:, k, f0:f0 + fn], xs[s][:, k, :],
                                                       start=(k == 0), stop=(k == KD - 1))
                        ins.then_inc(gate_ready[q], 1)
                    for q in range(2):
                        pe.wait_ge(hs_made[q], FREE + 3 * i + (3 * s + 3 + 1 - q) // 2)
                    if s == 0:
                        pe.wait_ge(ys_made[1], FREE + 2 * i)
                    else:
                        pe.wait_ge(ys_made[0], FREE + 2 * i + 2)
                    for t in range(4):
                        for n, (f0, fn) in enumerate(FT):
                            ins = nc.tensor.matmul(pb[:, 4 + t // 2, (t % 2) * D:(t % 2 + 1) * D],
                                                   hs[n][0:fn, t * P:(t + 1) * P], shd[0:fn, n, :],
                                                   start=(n == 0), stop=(n == 2))
                    ins.then_inc(sh_y_ready[s], 1)

        shared.close()
        phase_c(nc, sb, sem, sems, g, wd, table_i, table_ready, pb)


def phase_c(nc, sb, sem, sems, g, wd, table_i, table_ready, pb):
    rows_d, acc_d, ident, wgu = (g[k] for k in ("rows_d", "acc_d", "ident", "wgu"))
    passed = g["passed"]
    out = g["out"].rearrange("b l d -> (b l) d")
    with ExitStack() as own:
        def ring(name, n, shape):
            return [sb(f"{name}{s}", shape, F32, own) for s in range(n)]

        xe = ring("xe", UNROLL, [P, ROW])
        xeT = ring("xeT", 2, [P, KD, P])
        sg = ring("sg", 2, [P, M + 1])
        hg = ring("hg", 2, [P, M])
        h = ring("h", 2, [P, M])
        hT = ring("hT", 2, [MH, 2, P])
        ye = ring("ye", UNROLL, [P, D])
        token = [sb(f"token{s}", [P, 1], U32, own) for s in range(UNROLL)]
        s0 = ring("s0_", 2, [P, 4, D])
        s1 = ring("s1_", 2, [P, 4, D])

        row_loaded = sems("row_loaded", UNROLL)
        added = sems("added", UNROLL)
        x_turned, xeT_made, gu_ready, sg_made, hg_made, h_made, h_turned, hT_made, ye_ready, ye_made = (
            sems(n) for n in ("e_x_turned", "xeT_made", "gu_ready", "sg_made", "hg_made", "h_made", "h_turned",
                              "hT_made", "ye_ready", "ye_made"))
        sums_loaded, so_made, so_stored = (sems(n) for n in ("sums_loaded", "so_made", "so_stored"))

        ROUNDS = NT // UNROLL
        flat = table_i[:].rearrange("o n t -> o (n t)")

        def use(r, s):
            return (UNROLL // 2) * r + s // 2

        def off(r, s, n):
            return r + (s + n) // UNROLL, (s + n) % UNROLL

        with nc.Block() as block:

            @block.sync
            def _(sp):
                def one_round(r, first):
                    for s in range(UNROLL):
                        row = sp.value_load(flat[0:1, bass.ds(UNROLL * r + s, 1)], min_val=0, max_val=NROWS - P)
                        if not first:
                            apart(sp, h_made[s % 2], use(r - 1, s) + 1, passed)
                        sp.dma_start(xe[s][:], rows_d[bass.ds(row, P), :]).then_inc(row_loaded[s], 16)

                one_round(0, True)
                with sp.Fori(1, ROUNDS) as r:
                    one_round(r, False)
                for s in range(UNROLL):
                    sp.wait_ge(added[s], 16 * ROUNDS)
                with sp.Fori(0, T // SP_TOK // 2) as i:
                    for s in range(2):
                        at = (2 * i + s) * SP_TOK
                        sp.wait_ge(so_stored[s], FREE + 16 * i)
                        for n, dst in enumerate((s0, s1)):
                            sp.dma_start(dst[s][:], acc_d[n][bass.ds(at, SP_TOK), :].rearrange("(t p) d -> p t d", p=P))\
                              .then_inc(sums_loaded[s], 16)
                    for s in range(2):
                        at = (2 * i + s) * SP_TOK
                        sp.wait_ge(so_made[s], i + 1)
                        sp.dma_start(out[bass.ds(at, SP_TOK), :].rearrange("(t p) d -> p t d", p=P), s0[s][:])\
                          .then_inc(so_stored[s], 16)
                for s in range(2):
                    sp.wait_ge(so_stored[s], FREE + 16 * (T // SP_TOK // 2))

            @block.gpsimd
            def _(pool):
                for free in so_stored:
                    pool.sem_inc(free, FREE)
                def one_round(r, first):
                    for s in range(UNROLL):
                        if s >= 2:
                            apart(pool, added[s - 2], 16 * r + 16, passed)
                        elif not first:
                            apart(pool, added[s + 2], 16 * r, passed)
                        apart(pool, ye_made[s % 2], use(r, s) + 1, passed)
                        pool.indirect_dma_start(
                            acc_d[s % 2][:, :],
                            bass.IndirectOffsetOnAxis(ap=token[s][:], axis=0),
                            ye[s][:], None, compute_op=ALU.add).then_inc(added[s], 16)

                one_round(0, True)
                with pool.Fori(1, ROUNDS) as r:
                    one_round(r, False)

            @block.scalar
            def _(act):
                def turned_in(r, s):
                    p = s % 2
                    act.wait_ge(x_turned[p], use(r, s) + 1)
                    nc.scalar.activation(xeT[p][:].rearrange("p k t -> p (k t)"), pb[:, p, 0:2 * P], ACT.Copy)\
                      .then_inc(xeT_made[p], 1)

                def hidden_turned(r, s):
                    p = s % 2
                    act.wait_ge(h_turned[p], use(r, s) + 1)
                    nc.scalar.activation(hT[p][:].rearrange("p k t -> p (k t)"), pb[0:MH, 4 + p, 0:2 * P], ACT.Copy)\
                      .then_inc(hT_made[p], 1)

                def one_round(r, first, last):
                    for s in range(UNROLL):
                        p = s % 2
                        act.wait_ge(gu_ready[p], use(r, s) + 1)
                        nc.scalar.activation(sg[p][:], pb[:, 2 + p, 0:M + 1], ACT.Sigmoid).then_inc(sg_made[p], 1)
                        if not (last and s == UNROLL - 1):
                            turned_in(*off(r, s, 1))
                        if not (first and s == 0):
                            hidden_turned(*off(r, s, -1))

                turned_in(0, 0)
                one_round(0, True, False)
                with act.Fori(1, ROUNDS - 1) as r:
                    one_round(r, False, False)
                one_round(ROUNDS - 1, False, True)
                hidden_turned(ROUNDS - 1, UNROLL - 1)

            @block.vector
            def _(dve):
                def taken(r, s):
                    dve.wait_ge(ye_ready[s % 2], use(r, s) + 1)
                    dve.wait_ge(added[s], 16 * r)
                    nc.vector.tensor_copy(ye[s][:], pb[:, 6 + s % 2, 0:D]).then_inc(ye_made[s % 2], 1)

                def one_round(r, first):
                    for s in range(UNROLL):
                        p = s % 2
                        dve.wait_ge(sg_made[p], use(r, s) + 1)
                        dve.wait_ge(row_loaded[s], 16 * r + 16)
                        dve.wait_ge(added[s], 16 * r)
                        nc.vector.tensor_copy(token[s][:], xe[s][:, D:ROW].bitcast(U32))
                        nc.vector.tensor_tensor(hg[p][:], pb[:, 2 + p, 0:M], sg[p][:, 0:M], ALU.mult)\
                          .then_inc(hg_made[p], 1)
                        dve.wait_ge(hg_made[p], use(r, s) + 1)
                        nc.vector.scalar_tensor_tensor(out=h[p][:], in0=hg[p][:], scalar=sg[p][:, M:M + 1],
                                                       in1=pb[:, 2 + p, M + 1:WIDE], op0=ALU.mult, op1=ALU.mult)\
                          .then_inc(h_made[p], 1)
                        if not (first and s < 2):
                            taken(*off(r, s, -2))

                one_round(0, True)
                with dve.Fori(1, ROUNDS) as r:
                    one_round(r, False)
                for s in range(UNROLL - 2, UNROLL):
                    taken(ROUNDS - 1, s)
                with dve.Fori(0, T // SP_TOK // 2) as i:
                    for s in range(2):
                        dve.wait_ge(sums_loaded[s], 32 * i + 32)
                        nc.vector.tensor_tensor(s0[s][:], s0[s][:], s1[s][:], ALU.add).then_inc(so_made[s], 1)

            @block.tensor
            def _(pe):
                def turn_rows(r, s):
                    p = s % 2
                    pe.wait_ge(row_loaded[s], 16 * r + 16)
                    pe.wait_ge(xeT_made[p], use(r, s))
                    for k in range(KD):
                        ins = nc.tensor.transpose(pb[:, p, k * P:(k + 1) * P], xe[s][:, k * P:(k + 1) * P], ident[:])
                    ins.then_inc(x_turned[p], 1)

                def expert_of(r, s):
                    return pe.value_load(flat[0:1, bass.ds(2 * P + UNROLL * r + s, 1)], min_val=0, max_val=E - 1)

                def gate_up(r, s, e):
                    p = s % 2
                    pe.wait_ge(xeT_made[p], use(r, s) + 1)
                    pe.wait_ge(h_made[p], use(r, s))
                    for k in range(KD):
                        ins = nc.tensor.matmul(pb[:, 2 + p, 0:WIDE], xeT[p][:, k, :],
                                               wgu[:, bass.ds(e, 1), k, :].rearrange("p o c -> p (o c)"),
                                               start=(k == 0), stop=(k == KD - 1))
                    ins.then_inc(gu_ready[p], 1)

                def down(r, s, e):
                    p = s % 2
                    pe.wait_ge(hT_made[p], use(r, s) + 1)
                    pe.wait_ge(ye_made[p], use(r, s))
                    for k in range(2):
                        ins = nc.tensor.matmul(pb[:, 6 + p, 0:D], hT[p][:, k, :],
                                               wd[0:MH, bass.ds(e, 1), k, :].rearrange("p o d -> p (o d)"),
                                               start=(k == 0), stop=(k == 1))
                    ins.then_inc(ye_ready[p], 1)

                def turn_hidden(r, s):
                    p = s % 2
                    pe.wait_ge(h_made[p], use(r, s) + 1)
                    pe.wait_ge(hT_made[p], use(r, s))
                    for k in range(2):
                        ins = nc.tensor.transpose(pb[0:MH, 4 + p, k * P:(k + 1) * P],
                                                  h[p][:, k * MH:(k + 1) * MH], ident[:])
                    ins.then_inc(h_turned[p], 1)

                def step(r, s, before, after):
                    if before >= 2:
                        e = expert_of(*off(r, s, -2))
                    if after:
                        turn_rows(*off(r, s, 1))
                    if before >= 1:
                        turn_hidden(*off(r, s, -1))
                    if before >= 2:
                        down(*off(r, s, -2), e)
                    if after:
                        gate_up(*off(r, s, 1), expert_of(*off(r, s, 1)))

                turn_rows(0, 0)
                gate_up(0, 0, expert_of(0, 0))
                for s in range(UNROLL):
                    step(0, s, s, True)
                with pe.Fori(1, ROUNDS - 1) as r:
                    for s in range(UNROLL):
                        step(r, s, 2, True)
                for s in range(UNROLL + 2):
                    if s <= UNROLL:
                        step(ROUNDS - 1, s, 2, s < UNROLL - 1)
                    else:
                        down(*off(ROUNDS - 1, s, -2), expert_of(*off(ROUNDS - 1, s, -2)))


_INS = ['L0_attn_x', 'L0_attn_wq', 'L0_attn_wk', 'L0_attn_wv', 'L0_attn_wo', 'L0_attn_fq1_w', 'L0_attn_fq1_b',
        'L0_attn_fq2_w', 'L0_attn_fq2_b', 'L0_attn_fk1_w', 'L0_attn_fk1_b', 'L0_attn_fk2_w', 'L0_attn_fk2_b',
        'L0_attn_norm_w', 'L0_ffn_w_router', 'L0_ffn_corr_bias', 'L0_ffn_gate_w', 'L0_ffn_up_w', 'L0_ffn_down_w',
        'L0_ffn_sh_gate_w', 'L0_ffn_sh_up_w', 'L0_ffn_sh_down_w']


def kernel(**inputs):
    import concourse.bacc as bacc
    from concourse.bass_utils import run_bass_kernel_spmd

    nc = bacc.Bacc("TRN2", target_bir_lowering=False, num_devices=1)
    arrays, args = {}, []
    for name in _INS:
        a = np.ascontiguousarray(inputs[name])
        arrays[f"in_{name}"] = a
        args.append(nc.dram_tensor(f"in_{name}", a.shape, mybir.dt.from_np(a.dtype), kind="ExternalInput").ap())
    out = nc.dram_tensor("out_0", (B, L, D), F32, kind="ExternalOutput").ap()
    moe_block_kernel(nc, *args, out)
    r = run_bass_kernel_spmd(nc, [arrays], core_ids=[0])
    return r.results[0]["out_0"]
```

```python
from contextlib import ExitStack

import numpy as np

import concourse.bass as bass
from concourse import mybir

F32 = mybir.dt.float32
BF16 = mybir.dt.bfloat16
I32 = mybir.dt.int32
U32 = mybir.dt.uint32
ALU = mybir.AluOpType
ACT = mybir.ActivationFunctionType
AX_X = mybir.AxisListType.X

P = 128
B, L, D = 2, 2048, 256
T = B * L
H, DK = 16, 16
KD = D // P
PAIRS = H // 2
SPAN = 256
ST = SPAN // P
QK_ORDER = (2, 3, 0, 1)
NSPAN = L // SPAN
E, M, TOPK, G, TOPK_G = 32, 176, 6, 8, 4
EG = E // G
MH = M // 2
MS = 2 * M
EPS = 1e-5
SCALE = DK ** -0.5
REGION = T + P
ROW = D + 1
NROWS = E * REGION + P
NTILES = (T * TOPK + E * (P - 1)) // P
UNROLL = 8
SLOTS = 4
NT = -(-NTILES // UNROLL) * UNROLL
WIDE = 2 * M + 1
BIG = 3.0e38
MARK = 3.3e38
SP_TOK = 512
SUMS = 4
FREE = 1
ROUTE_LINKS = 19
SETUP_LINKS = 19
NB = B * ST
ROUTE_NAMES = ("next_row", "cbias", "rows_d", "scattered", "passed",
               "score", "sfc", "hi2", "lo2", "top1", "mid", "top2",
               "gsc", "gtop", "gpick", "gmark", "gneg", "masked", "etop",
               "epick", "emark", "chosen", "slot", "slotm", "stop8", "slots",
               "tri", "onesb", "ids", "xp", "score_made", "route_step", "chosen_made",
               "rank_ready", "slots_made", "rank_read", "dispatched", "id_made", "zeroed")


def moe_block_kernel(nc, x, wq, wk, wv, wo, fq1_w, fq1_b, fq2_w, fq2_b, fk1_w, fk1_b, fk2_w, fk2_b,
                     norm_w, w_router, corr_bias, gate_w, up_w, down_w, sh_gate_w, sh_up_w,
                     sh_down_w, out):
    rows_d = nc.dram_tensor("rows_d", [NROWS, ROW], F32)
    x2nT_d = nc.dram_tensor("x2nT_d", [P, KD, T], F32)
    acc_d = [nc.dram_tensor(f"acc{n}_d", [T + P, D], F32) for n in range(2)]

    with ExitStack() as ctx:
        def sb(name, shape, dt=F32, stack=ctx):
            return stack.enter_context(nc.sbuf_tensor(name, shape, dt))

        def sem(name):
            return ctx.enter_context(nc.semaphore(name))

        def sems(name, n=2):
            return [sem(f"{name}{k}") for k in range(n)]

        ident = sb("ident", [P, P])
        wgu = sb("wgu", [P, E, KD, WIDE])
        wr = sb("wr", [P, KD, E])
        shg = sb("shg", [P, KD, MS])
        shu = sb("shu", [P, KD, MS])
        shd = sb("shd", [P, 3, D])
        next_row = sb("next_row", [P, E])
        first_row = sb("first_row", [P, E])
        zeros = sb("zeros", [P, D])
        xs0 = sb("xs0", [P, KD, SP_TOK])
        part_i = sb("part_i", [P, 1], I32)
        part_f = sb("part_f", [P, 1])

        scattered = sems("scattered")
        gu_loaded = sem("gu_loaded")
        sh_loaded = sem("sh_loaded")
        xs_loaded = sems("xs_loaded")
        router_cols = sem("router_cols")
        passed = sem("passed")

        score = sb("score", [P, NB, E])
        sfc = sb("sfc", [P, NB * G, EG])
        hi2 = sb("hi2", [P, NB * G, 2])
        lo2 = sb("lo2", [P, NB * G, 2])
        top1 = sb("top1", [P, NB * G])
        mid = sb("mid", [P, NB * G])
        top2 = sb("top2", [P, NB * G])
        gsc = sb("gsc", [P, NB, G])
        gtop = sb("gtop", [P, NB, 8])
        gpick = sb("gpick", [P, NB, 8])
        gmark = sb("gmark", [P, NB, G])
        gneg = sb("gneg", [P, NB * G])
        masked = sb("masked", [P, NB, E])
        etop = sb("etop", [P, NB, 8])
        epick = sb("epick", [P, NB, 8])
        emark = sb("emark", [P, NB, E])
        chosen = sb("chosen", [P, NB, E], BF16)
        slot = sb("slot", [P, NB, E])
        slotm = sb("slotm", [P, NB, E])
        stop8 = sb("stop8", [P, NB, 8])
        slots = sb("slots", [P, NB, 8], U32)

        tri = sb("tri", [P, P], BF16)
        onesb = sb("onesb", [P, P], BF16)
        ids = sb("ids", [P, T // P], I32)
        cbias = sb("cbias", [P, E])
        xp = [sb(f"xp{b}", [P, ST, ROW]) for b in range(B)]
        score_made = sem("score_made")
        route_step = sem("route_step")
        chosen_made = sem("chosen_made")
        rank_ready = sem("rank_ready")
        slots_made = sem("slots_made")
        rank_read = sem("rank_read")
        dispatched = sems("dispatched")
        id_made = sems("id_made")
        zeroed = sem("zeroed")
        have = locals()
        route = {name: have[name] for name in ROUTE_NAMES}

        phase_a(nc, ctx, sb, sem, sems, locals())
        phase_b(nc, ctx, sb, sem, sems, locals())


def bc(ap, axis, n):
    ap = ap.unsqueeze(axis)
    shape = list(ap.shape)
    shape[axis] = n
    return ap.to_broadcast(shape)


def apart(eng, sem, value, passed):
    eng.wait_ge(sem, value)
    eng.sem_inc(passed, 1)


def routing(nc, dve, R, pr, j):
    k0 = 0

    def step(ins):
        nonlocal k0
        k0 += 1
        ins.then_inc(R["route_step"], 1)
        apart(dve, R["route_step"], ROUTE_LINKS * j + (SETUP_LINKS + k0), R["passed"])

    def group_scores():
        dve.wait_ge(R["score_made"], FREE + j + 1)
        step(nc.vector.tensor_tensor(R["sfc"][:].rearrange("p (n g) e -> p n (g e)", g=G), R["score"][:],
                                     bc(R["cbias"][:], 1, NB), ALU.add))
        step(nc.vector.tensor_tensor(R["hi2"][:], R["sfc"][:, :, 0:2], R["sfc"][:, :, 2:4], ALU.max))
        step(nc.vector.tensor_tensor(R["lo2"][:], R["sfc"][:, :, 0:2], R["sfc"][:, :, 2:4], ALU.min))
        step(nc.vector.tensor_tensor(R["top1"][:], R["hi2"][:, :, 0], R["hi2"][:, :, 1], ALU.max))
        step(nc.vector.tensor_tensor(R["mid"][:], R["hi2"][:, :, 0], R["hi2"][:, :, 1], ALU.min))
        step(nc.vector.tensor_tensor(R["top2"][:], R["lo2"][:, :, 0], R["lo2"][:, :, 1], ALU.max))
        step(nc.vector.tensor_tensor(R["top2"][:], R["top2"][:], R["mid"][:], ALU.max))
        step(nc.vector.tensor_tensor(R["gsc"][:].rearrange("p n g -> p (n g)"), R["top1"][:], R["top2"][:], ALU.add))

    def pick_groups():
        for n in range(NB):
            ins = nc.vector.max(R["gtop"][:, n, :], R["gsc"][:, n, :])
        step(ins)
        step(nc.vector.tensor_copy(R["gpick"][:, :, 0:TOPK_G], R["gtop"][:, :, 0:TOPK_G]))
        for n in range(NB):
            ins = nc.vector.match_replace(R["gmark"][:, n, :], R["gpick"][:, n, :], R["gsc"][:, n, :], MARK)
        step(ins)
        step(nc.vector.tensor_scalar(R["gneg"][:], R["gmark"][:].rearrange("p n g -> p (n g)"), BIG, -BIG,
                                     ALU.is_lt, ALU.mult))
        step(nc.vector.tensor_tensor(R["masked"][:].rearrange("p n (g e) -> p (n g) e", g=G), R["sfc"][:],
                                     bc(R["gneg"][:], 2, EG), ALU.add))

    def pick_experts():
        for n in range(NB):
            ins = nc.vector.max(R["etop"][:, n, :], R["masked"][:, n, :])
        step(ins)
        step(nc.vector.tensor_copy(R["epick"][:, :, 0:TOPK], R["etop"][:, :, 0:TOPK]))
        for n in range(NB):
            ins = nc.vector.match_replace(R["emark"][:, n, :], R["epick"][:, n, :], R["masked"][:, n, :], MARK)
        step(ins)
        nc.vector.tensor_scalar(R["chosen"][:], R["emark"][:], BIG, None, ALU.is_gt).then_inc(R["chosen_made"], 1)

    def find_rows():
        dve.wait_ge(R["rank_ready"], j + 1)
        step(nc.vector.tensor_tensor(R["slot"][:], pr[:, 0:NB * E].rearrange("p (n e) -> p n e", e=E),
                                     bc(R["next_row"][:], 1, NB), ALU.add))
        step(nc.vector.tensor_tensor(R["slotm"][:], R["slot"][:], R["chosen"][:], ALU.mult))
        for n in range(NB):
            ins = nc.vector.max(R["stop8"][:, n, :], R["slotm"][:, n, :])
        step(ins)
        for b in range(B):
            dve.wait_ge(R["dispatched"][b], FREE + j)
        nc.vector.tensor_scalar(R["slots"][:], R["stop8"][:], -1.0, None, ALU.add).then_inc(R["slots_made"], 1)
        nc.vector.tensor_tensor(R["next_row"][:], pr[:, NB * E:(NB + 1) * E], R["next_row"][:], ALU.add)\
          .then_inc(R["rank_read"], 1)
        dve.wait_ge(R["slots_made"], j + 1)
        dve.wait_ge(R["rank_read"], FREE + j + 1)
        assert k0 == ROUTE_LINKS, k0

    return group_scores, pick_groups, pick_experts, find_rows


def rank(nc, pe, R, pr, j):
    pe.wait_ge(R["chosen_made"], j + 1)
    for n in range(NB):
        dst = pr[:, n * E:(n + 1) * E]
        nc.tensor.matmul(dst, R["tri"][:], R["chosen"][:, n, :], start=True, stop=(n == 0))
        for before in range(n):
            nc.tensor.matmul(dst, R["onesb"][:], R["chosen"][:, before, :], start=False, stop=(before == n - 1))
    for n in range(NB):
        ins = nc.tensor.matmul(pr[:, NB * E:(NB + 1) * E], R["onesb"][:], R["chosen"][:, n, :],
                               start=(n == 0), stop=(n == NB - 1))
    ins.then_inc(R["rank_ready"], 1)


def dispatch(pool, R, j):
    apart(pool, R["slots_made"], j + 1, R["passed"])
    for b in range(B):
        apart(pool, R["id_made"][b], j + 1, R["passed"])
        for t in range(ST):
            for k in range(TOPK):
                pool.indirect_dma_start(
                    R["rows_d"][:, :],
                    bass.IndirectOffsetOnAxis(ap=R["slots"][:, b * ST + t, k:k + 1], axis=0),
                    R["xp"][b][:, t, :], None).then_inc(R["scattered"][b], 16)
    for b in range(B):
        apart(pool, R["scattered"][b], 16 * ST * TOPK * (j + 1), R["dispatched"][b])


def phase_a(nc, ctx, sb, sem, sems, g):
    x, acc_d, x2nT_d = g["x"], g["acc_d"], g["x2nT_d"]
    ident, wgu, wr, next_row, first_row, zeros = (
        g[k] for k in ("ident", "wgu", "wr", "next_row", "first_row", "zeros"))
    gu_loaded, sh_loaded, router_cols, passed = (
        g[k] for k in ("gu_loaded", "sh_loaded", "router_cols", "passed"))
    R, zeroed = g["route"], g["zeroed"]
    tri, onesb, ids, xp, id_made, score, score_made, rank_read, dispatched = (
        R[k] for k in ("tri", "onesb", "ids", "xp", "id_made", "score", "score_made", "rank_read", "dispatched"))
    with ExitStack() as own:
        def t2(name, shape, dt=F32):
            return [sb(f"{name}{b}", shape, dt, own) for b in range(2)]

        def t1(name, shape, dt=F32):
            return sb(name, shape, dt, own)

        ones128 = t1("ones128", [P, P])
        hblock = t1("hblock", [P, 8, DK])
        kvmask = t1("kvmask", [P, P])
        hmean = t1("hmean", [P, P])
        cmask = t1("cmask", [P, P])
        head_on = t1("head_on", [P, 8])
        eps_col = t1("eps_col", [P, 1])
        first_i = t1("first_i", [P, E], I32)
        rep16 = t1("rep16", [DK, 8, DK])
        f4 = t1("f4", [DK, 69])
        rep = t1("rep", [P, 69])
        wqk = t1("wqk", [P, 4, KD, D])
        wvT = t1("wvT", [P, KD, D])
        woT = t1("woT", [P, KD, D])
        xt = t2("xt", [P, ST, D])
        xr = t2("xr", [P, ST, D])
        bst = t2("bst", [P, ST, 6])
        mv = t2("mv", [P, ST, 2])
        std = t2("std", [P, ST])
        rstd = t2("rstd", [P, ST])
        xn = xt
        xnT = t2("xnT", [P, KD, SPAN])
        spare = t1("spare", [P, 1])
        a1 = t1("a1", [P, 2, SPAN])
        kT = t2("kT", [P, 2, SPAN])
        qT = t2("qT", [P, 2, SPAN])
        qz = t2("qz", [P, 2, 8, P])
        vz = t2("vz", [P, ST, PAIRS, 3, DK])
        ktok = t2("ktok", [P, ST, 2, P])
        sT = t2("sT", [P, 4, 4, P])
        kvm = t2("kvm", [P, 2, P])
        sq = t2("sq", [P, 2, SPAN])
        ostd = sq
        nat = sT[0][:].rearrange("p n h m -> p (n h m)").rearrange(
            "p (n r d) -> p n r d", n=4, r=KD)
        gsb = sq[0][:].rearrange("p f (h c) -> p (f h) c", c=P)
        fmap = sq[1][:].rearrange("p f (h c) -> p (f h) c", c=P)
        orstd = ostd
        oT = t2("oT", [P, 2, SPAN])
        x2 = t2("x2", [P, ST, D])
        bst2 = t2("bst2_", [P, ST, 6])
        mv2 = t2("mv2_", [P, ST, 2])
        std2 = t2("std2_", [P, ST])
        rstd2 = t2("rstd2_", [P, ST])
        x2nT = sq
        pg = own.enter_context(nc.psum_tensor("pg", [P, 4, 512], F32))
        pkv = own.enter_context(nc.psum_tensor("pkv", [P, 2, 2 * P], F32))
        pr = own.enter_context(nc.psum_tensor("pr", [P, 512], F32))
        po = own.enter_context(nc.psum_tensor("po", [P, 2, 512], F32))

        attn_loaded = sem("attn_loaded")
        const_step = sem("const_step")
        consts_made = sem("consts_made")
        setup_pe = sem("setup_pe")
        setup_dve = sem("setup_dve")
        xr_loaded = sems("xr_loaded")
        x_loaded, x_stats, x_aggr, x_std, xn_made = (
            sems(n) for n in ("x_loaded", "x_stats", "x_aggr", "x_std", "xn_made"))
        x_rstd, x2_rstd = (sem(n) for n in ("x_rstd", "x2_rstd"))
        sq_made, ms_ready, ostd_made, orstd_made = (sem(n) for n in ("sq_made", "ms_ready", "ostd_made", "orstd_made"))
        xt_turned, xnT_made, proj_ready, a1_made, q_made = (
            sems(n) for n in ("xt_turned", "xnT_made", "proj_ready", "a1_made", "q_made"))
        qz_made = sems("qz_made")
        v_ready, vz_made, kt_ready, ktok_made = (
            sems(n) for n in ("v_ready", "vz_made", "kt_ready", "ktok_made"))
        s_ready = sem("s_ready")
        s_masked = sem("s_masked")
        kv_ready, kvm_made, o_ready, oT_made = (sems(n) for n in ("kv_ready", "kvm_made", "o_ready", "oT_made"))
        y_ready, x2_made, x2_stored, x2_stats, x2_aggr, x2_std, xp_made = (
            sems(n) for n in ("y_ready", "x2_made", "x2_stored", "x2_stats", "x2_aggr", "x2_std",
                              "xp_made"))
        x2t_turned, x2nT_made, x2nT_stored = (
            sems(n) for n in ("x2t_turned", "x2nT_made", "x2nT_stored"))
        logit_ready = sem("logit_ready")

        block = own.enter_context(nc.Block())

        def span(ap, b, i):
            return ap[bass.ds(b * L + i * SPAN, SPAN), :].rearrange("(t p) d -> p t d", p=P)

        x_rows = x.rearrange("b l d -> (b l) d")
        UNITS = ST * B

        @block.sync
        def _(sp):
            for n, w in enumerate((g["wq"], g["wk"], g["wv"], g["wo"])):
                sp.dma_start(nat[:, n, :, :], w.rearrange("(r p) d -> p r d", p=P)).then_inc(attn_loaded, 16)
            for n, w in enumerate((g["fq1_w"], g["fq2_w"], g["fk1_w"], g["fk2_w"])):
                sp.dma_start(f4[:, n * DK:(n + 1) * DK], w).then_inc(attn_loaded, 16)
            for n, v in enumerate((g["fq1_b"], g["fq2_b"], g["fk1_b"], g["fk2_b"], g["norm_w"])):
                sp.dma_start(f4[:, 64 + n:65 + n], v.unsqueeze(1)).then_inc(attn_loaded, 16)
            sp.dma_start(R["cbias"][:], g["corr_bias"].partition_broadcast(P)).then_inc(attn_loaded, 16)
            sp.dma_start(wr[:], g["w_router"].rearrange("(k p) e -> p k e", p=P)).then_inc(attn_loaded, 16)

            def load_experts(i):
                for k in range(KD):
                    for w, at in ((g["gate_w"], 0), (g["up_w"], M + 1)):
                        sp.dma_start(wgu[:, bass.ds(i * (E // NSPAN), E // NSPAN), k, at:at + M],
                                     w[bass.ds(i * (E // NSPAN), E // NSPAN), k * P:(k + 1) * P, :].rearrange(
                                          "e p m -> p e m")).then_inc(gu_loaded, 16)

            def next_input(j):
                for b in range(B):
                    sp.wait_ge(xt_turned[b], FREE + j)
                    sp.dma_start(xt[b][:], span(x_rows, b, j)).then_inc(x_loaded[b], 16)

            def one_span(i, last):
                load_experts(i)
                for b in range(B):
                    sp.wait_ge(x2_made[b], FREE + i)
                    sp.dma_start(xr[b][:], span(x_rows, b, i)).then_inc(xr_loaded[b], 16)
                if not last:
                    next_input(i + 1)
                for b in range(B):
                    sp.wait_ge(x2_made[b], FREE + i + 1)
                    sp.dma_start(span(acc_d[1], b, i), x2[b][:]).then_inc(x2_stored[b], 16)
                for b in range(B):
                    apart(sp, x2nT_made[b], FREE + i + 1, passed)
                    sp.dma_start(x2nT_d[:, :, bass.ds(b * L + i * SPAN, SPAN)], x2nT[b][:])\
                      .then_inc(x2nT_stored[b], 16)

            next_input(0)
            sp.wait_ge(consts_made, 1)
            for n in range(2):
                sp.dma_start(acc_d[n][T:T + P, :], zeros[:]).then_inc(zeroed, 16)
            with sp.Fori(0, NSPAN - 1) as i:
                one_span(i, False)
            for b in range(B):
                sp.wait_ge(x2nT_stored[b], FREE + 16 * (NSPAN - 1))
            sp.dma_start(g["xs0"][:], x2nT_d[:, :, 0:SP_TOK]).then_inc(g["xs_loaded"][0], 16)
            one_span(NSPAN - 1, True)
            sp.wait_ge(gu_loaded, 16 * 4 * NSPAN)
            sp.wait_ge(zeroed, 32)
            for b in range(B):
                sp.wait_ge(x2_stored[b], FREE + 16 * NSPAN)
                sp.wait_ge(x2nT_stored[b], FREE + 16 * NSPAN)

        @block.gpsimd
        def _(pool):
            for free in (*xt_turned, *x2_made, *x2nT_stored, *x2_stored, *dispatched, *x2nT_made, score_made,
                         rank_read, *oT_made):
                pool.sem_inc(free, FREE)
            n = 0

            def link(ins):
                nonlocal n
                n += 1
                ins.then_inc(const_step, 1)
                pool.wait_ge(const_step, n)

            def keep(t, pattern, base, mult, op=ALU.is_ge, fill=0.0):
                link(pool.affine_select(out=t, in_=t, compare_op=op, fill=fill, base=base,
                                        pattern=pattern, channel_multiplier=mult))

            link(pool.memset(ident[:], 0.0))
            keep(ident[:], [[-1, P]], 0, 1, ALU.not_equal, 1.0)
            link(pool.memset(ones128[:], 1.0))
            link(pool.memset(hblock[:], 1.0))
            keep(hblock[:], [[-DK, 8], [0, DK]], 0, 1)
            keep(hblock[:], [[DK, 8], [0, DK]], DK - 1, -1)
            link(pool.memset(cmask[:], SCALE))
            keep(cmask[:], [[1, P]], 0, -1)
            link(pool.memset(tri[:], 1.0))
            keep(tri[:], [[1, P]], -1, -1)
            link(pool.memset(onesb[:], 1.0))
            link(pool.memset(zeros[:], 0.0))
            link(pool.memset(eps_col[:], EPS))
            link(pool.iota(ids[:], pattern=[[P, T // P]], base=0, channel_multiplier=1))
            link(pool.iota(first_i[:], pattern=[[REGION, E]], base=1, channel_multiplier=0))
            link(pool.iota(g["part_i"][:], pattern=[[0, 1]], base=0, channel_multiplier=1))
            for b in range(B):
                link(pool.memset(vz[b][:], 0.0))
                link(pool.memset(kvm[b][:], 0.0))
            link(pool.memset(R["gpick"][:], MARK))
            link(pool.memset(R["epick"][:], MARK))
            pool.memset(a1[:, 0, 0:1], 0.0).then_inc(consts_made, 1)

            def spread_q(i):
                pool.wait_ge(q_made[1], 4 * i + 4)
                for f in range(2):
                    pool.tensor_tensor(qz[1][:, f, :, :], bc(qT[1][:, f, 0:P], 1, 8), bc(head_on[:], 2, P), ALU.mult)\
                        .then_inc(qz_made[1], 1)

            spread_q(0)
            with pool.Fori(1, NSPAN) as i:
                spread_q(i)
                dispatch(pool, R, i - 1)
            for b in range(B):
                pool.wait_ge(R["scattered"][b], 16 * ST * TOPK * (NSPAN - 1))

        @block.scalar
        def _(act):
            act.wait_ge(attn_loaded, 16 * 15)
            act.dma_start(g["shg"][:], g["sh_gate_w"].rearrange("(k p) m -> p k m", p=P)).then_inc(sh_loaded, 16)
            act.dma_start(g["shu"][:], g["sh_up_w"].rearrange("(k p) m -> p k m", p=P)).then_inc(sh_loaded, 16)
            act.dma_start(g["shd"][:, 0:2, :], g["sh_down_w"][0:2 * P, :].rearrange("(k p) d -> p k d", p=P))\
               .then_inc(sh_loaded, 16)
            act.dma_start(g["shd"][0:MS - 2 * P, 2, :], g["sh_down_w"][2 * P:MS, :]).then_inc(sh_loaded, 16)
            act.wait_ge(consts_made, 1)
            act.wait_ge(setup_dve, 1)

            def input_std(j):
                for b in range(B):
                    act.wait_ge(x_aggr[b], ST * j + ST)
                    nc.scalar.activation(std[b][:], mv[b][:, :, 1], ACT.Sqrt, bias=eps_col[:, 0:1])\
                      .then_inc(x_std[b], 1)

            def input_turned(j):
                for b in range(B):
                    act.wait_ge(xt_turned[b], FREE + j + 1)
                    nc.scalar.activation(xnT[b][:], pg[:, 2 + b, :].rearrange("p (k t) -> p k t", k=KD), ACT.Copy)\
                      .then_inc(xnT_made[b], 1)

            def first_factor(j, b, o):
                r = QK_ORDER[o]
                act.wait_ge(proj_ready[b], 4 * j + o + 1)
                if b == 1:
                    act.wait_ge(q_made[0], 4 * j + o + 1)
                elif o >= 2:
                    act.wait_ge(q_made[1], 4 * j + o - 1)
                nc.scalar.activation(a1[:, o % 2, :], pg[:, (r + 2) % 4, 0:SPAN], ACT.Identity,
                                     bias=rep[:, 64 + 2 * (r // 2):65 + 2 * (r // 2)]).then_inc(a1_made[b], 1)

            def spread_q(i, u, heads):
                b, t = u % 2, u // 2
                act.wait_ge(q_made[b], 4 * i + 4)
                if u >= 2:
                    act.wait_ge(s_ready, 2 * UNITS * i + 2 * (u - 1))
                for h in heads:
                    ins = nc.scalar.activation(qz[u % 2][:, :, h, :], qT[b][:, :, t * P:(t + 1) * P], ACT.Copy,
                                               scale=head_on[:, h:h + 1])
                    ins.then_inc(qz_made[u % 2], 1)

            def squares(i, u):
                b, t = u % 2, u // 2
                act.wait_ge(o_ready[b], ST * i + t + 1)
                if t == 0:
                    act.wait_ge(x2nT_stored[b], FREE + 16 * i)
                nc.scalar.activation(sq[b][:, :, t * P:(t + 1) * P],
                                     po[:, b, :].rearrange("p (f t) -> p f t", f=2)[:, :, t * P:(t + 1) * P],
                                     ACT.Square).then_inc(sq_made, 1)

            def head_std(i, u):
                b, t = u % 2, u // 2
                act.wait_ge(ms_ready, UNITS * i + u + 1)
                nc.scalar.activation(ostd[b][:, :, t * P:(t + 1) * P],
                                     pr[:, 0:2 * P].rearrange("p (f t) -> p f t", f=2), ACT.Sqrt,
                                     bias=eps_col[:, 0:1]).then_inc(ostd_made, 1)

            def one_span(i, last):
                for o in range(2, 4):
                    first_factor(i, 0, o)
                for o in range(2, 4):
                    first_factor(i, 1, o)
                    spread_q(i, 0, range(4 * o - 8, 4 * o - 4))
                for b in range(B):
                    act.wait_ge(v_ready[b], i + 1)
                    nc.scalar.activation(vz[b][:, :, :, 0:3:2, :].rearrange("p t g a e -> p (t g) a e"),
                                         pg[:, b, :].rearrange("p (g a e) -> p g a e", a=2, e=DK), ACT.Copy)\
                      .then_inc(vz_made[b], 1)
                for b in range(B):
                    act.wait_ge(kt_ready[b], i + 1)
                    nc.scalar.activation(ktok[b][:].rearrange("p t f e -> p (t f e)"), pg[:, 2 + b, :], ACT.Copy)\
                      .then_inc(ktok_made[b], 1)
                spread_q(i, 2, range(8))
                if not last:
                    input_std(i + 1)
                squares(i, 0)
                spread_q(i, 3, range(8))
                head_std(i, 0)
                squares(i, 1)
                head_std(i, 1)
                squares(i, 2)
                head_std(i, 2)
                squares(i, 3)
                if not last:
                    input_turned(i + 1)
                head_std(i, 3)
                if not last:
                    for o in range(2):
                        first_factor(i + 1, 0, o)
                for b in range(B):
                    act.wait_ge(x2_aggr[b], ST * i + ST)
                    nc.scalar.activation(std2[b][:], mv2[b][:, :, 1], ACT.Sqrt, bias=eps_col[:, 0:1])\
                      .then_inc(x2_std[b], 1)
                    if not last:
                        first_factor(i + 1, 1, b)
                for b in range(B):
                    act.wait_ge(x2t_turned[b], i + 1)
                    act.wait_ge(oT_made[b], FREE + i + 1)
                    nc.scalar.activation(x2nT[b][:], pg[:, 2 + b, :].rearrange("p (k t) -> p k t", k=KD), ACT.Copy)\
                      .then_inc(x2nT_made[b], 1)
                act.wait_ge(logit_ready, i + 1)
                nc.scalar.activation(score[:].rearrange("p n e -> p (n e)"), pr[:, 2 * P:2 * P + NB * E],
                                     ACT.Sigmoid).then_inc(score_made, 1)
                nc.scalar.activation(spare[:], eps_col[:], ACT.Sqrt).then_inc(passed, 1)

            input_std(0)
            input_turned(0)
            for b in range(B):
                for o in range(2):
                    first_factor(0, b, o)
            with act.Fori(0, NSPAN - 1) as i:
                one_span(i, False)
            one_span(NSPAN - 1, True)

        @block.vector
        def _(dve):
            n = 0

            def link(ins):
                nonlocal n
                n += 1
                ins.then_inc(R["route_step"], 1)
                dve.wait_ge(R["route_step"], n)

            dve.wait_ge(consts_made, 1)
            link(nc.vector.tensor_copy(rep16[:], bc(ident[0:DK, 0:DK], 1, 8)))
            link(nc.vector.tensor_scalar(kvmask[:], hblock[:].rearrange("p h d -> p (h d)"), SCALE, None, ALU.mult))
            link(nc.vector.tensor_scalar(hmean[:], hblock[:].rearrange("p h d -> p (h d)"), 1.0 / DK, None, ALU.mult))
            link(nc.vector.tensor_copy(head_on[:], hblock[:, :, 0]))
            link(nc.vector.tensor_copy(first_row[:], first_i[:]))
            link(nc.vector.tensor_copy(next_row[:], first_i[:]))
            link(nc.vector.tensor_copy(g["part_f"][:], g["part_i"][:]))
            nc.vector.memset(kT[0][:, 0, 0:1], 0.0).then_inc(setup_dve, 1)
            dve.wait_ge(setup_pe, 1)
            link(nc.vector.tensor_copy(rep[:], pg[:, 0, 0:69]))
            for m in range(4):
                link(nc.vector.tensor_tensor(gsb[:, m, :].rearrange("p (h d) -> p h d", d=DK),
                                             bc(rep[:, m * DK:(m + 1) * DK], 1, 8), hblock[:], ALU.mult))
            nc.vector.memset(kT[0][:, 0, 1:2], 0.0).then_inc(setup_dve, 1)
            dve.wait_ge(setup_pe, 2)
            link(nc.vector.tensor_copy(fmap.rearrange("p m c -> p (m c)"), pg[:, 1, :]))
            link(nc.vector.tensor_copy(wvT[:].rearrange("p k d -> p (k d)"), pg[:, 2, :]))
            link(nc.vector.tensor_scalar(woT[:].rearrange("p k d -> p (k d)"), pg[:, 3, :], rep[:, 68:69], None,
                                         ALU.mult))
            nc.vector.memset(kT[0][:, 0, 2:3], 0.0).then_inc(setup_dve, 1)
            def layer_stats(src, ready, st, m, stats, aggr, b, i):
                for t in range(ST):
                    ready(t)
                    nc.vector.bn_stats(st[b][:, t, :], src[b][:, t, :]).then_inc(stats[b], 1)
                for t in range(ST):
                    apart(dve, stats[b], ST * i + t + 1, passed)
                    nc.vector.bn_aggr(m[b][:, t, :], st[b][:, t, :]).then_inc(aggr[b], 1)

            def input_stats(j):
                for b in range(B):
                    layer_stats(xt, lambda t: dve.wait_ge(x_loaded[b], 16 * j + 16), bst, mv, x_stats, x_aggr, b, j)

            def input_normal(j):
                for b in range(B):
                    dve.wait_ge(x_std[b], j + 1)
                    nc.vector.reciprocal(rstd[b][:], std[b][:]).then_inc(x_rstd, 1)
                    dve.wait_ge(x_rstd, B * j + (b + 1))
                    for t in range(ST):
                        nc.vector.tensor_scalar(xn[b][:, t, :], xt[b][:, t, :], mv[b][:, t, 0:1], rstd[b][:, t:t + 1],
                                                ALU.subtract, ALU.mult).then_inc(xn_made[b], 1)

            def second_factor(i, b, o):
                r = QK_ORDER[o]
                f = r % 2
                dst = qT[b][:, f, :] if r < 2 else kT[b][:, f, :]
                dve.wait_ge(a1_made[b], 4 * i + o + 1)
                nc.vector.scalar_tensor_tensor(
                    out=dst, in0=pg[:, (r + 2) % 4, SPAN:2 * SPAN],
                    scalar=rep[:, 65 + 2 * (r // 2):66 + 2 * (r // 2)], in1=a1[:, o % 2, :],
                    op0=ALU.add, op1=ALU.mult).then_inc(q_made[b], 1)

            def mask_scores(i, u):
                for g in range(2):
                    dve.wait_ge(s_ready, 2 * UNITS * i + 2 * u + g + 1)
                    nc.vector.tensor_tensor(
                        sT[u % 2][:, 2 * g:2 * g + 2, :, :].rearrange("p n h m -> p (n h) m"),
                        pg[:, 2 * g:2 * g + 2, :].rearrange("p n (h m) -> p (n h) m", m=P),
                        bc(cmask[:], 1, 8), ALU.mult).then_inc(s_masked, 1)

            def mask_state(i, u):
                b = u % 2
                dve.wait_ge(kv_ready[b], ST * i + u // 2 + 1)
                nc.vector.tensor_tensor(kvm[b][:], pkv[:, b, 0:2 * P].rearrange("p (f e) -> p f e", f=2),
                                        bc(kvmask[:], 1, 2), ALU.mult).then_inc(kvm_made[b], 1)

            def invert_std(i, u):
                b, t = u % 2, u // 2
                part = ostd[b][:, :, t * P:(t + 1) * P]
                dve.wait_ge(ostd_made, UNITS * i + u + 1)
                nc.vector.reciprocal(part, part).then_inc(orstd_made, 1)
                dve.wait_ge(orstd_made, UNITS * i + u + 1)

            def one_span(i, first, last):
                parts = [lambda: None] * 4 if first else routing(nc, dve, R, pr, i - 1)
                for o in range(2):
                    second_factor(i, 1, o)
                parts[0]()
                for o in range(2, 4):
                    second_factor(i, 0, o)
                parts[1]()
                for o in range(2, 4):
                    second_factor(i, 1, o)
                parts[2]()
                mask_scores(i, 0)
                if not last:
                    input_stats(i + 1)
                parts[3]()
                mask_scores(i, 1)
                mask_state(i, 0)
                mask_scores(i, 2)
                if not last:
                    input_normal(i + 1)
                mask_state(i, 1)
                mask_scores(i, 3)
                mask_state(i, 2)
                invert_std(i, 0)
                mask_state(i, 3)
                invert_std(i, 1)
                for b in range(B):
                    invert_std(i, b + 2)
                    nc.vector.tensor_tensor(oT[b][:].rearrange("p f t -> p (f t)"), po[:, b, :],
                                            orstd[b][:].rearrange("p f t -> p (f t)"), ALU.mult).then_inc(oT_made[b], 1)
                if not last:
                    for o in range(2):
                        second_factor(i + 1, 0, o)
                for b in range(B):
                    dve.wait_ge(y_ready[b], i + 1)
                    dve.wait_ge(xr_loaded[b], 16 * i + 16)
                    dve.wait_ge(x2_stored[b], FREE + 16 * i)
                    nc.vector.tensor_tensor(x2[b][:], pg[:, 2 + b, :].rearrange("p (t d) -> p t d", t=ST), xr[b][:],
                                            ALU.add).then_inc(x2_made[b], 1)
                    dve.wait_ge(x2_made[b], FREE + i + 1)
                    layer_stats(x2, lambda t: None, bst2, mv2, x2_stats, x2_aggr, b, i)
                for b in range(B):
                    dve.wait_ge(x2_std[b], i + 1)
                    nc.vector.reciprocal(rstd2[b][:], std2[b][:]).then_inc(x2_rstd, 1)
                    dve.wait_ge(x2_rstd, B * i + (b + 1))
                    dve.wait_ge(dispatched[b], FREE + i)
                    for t in range(ST):
                        nc.vector.tensor_scalar(xp[b][:, t, 0:D], x2[b][:, t, :], mv2[b][:, t, 0:1],
                                                rstd2[b][:, t:t + 1], ALU.subtract, ALU.mult).then_inc(xp_made[b], 1)
                    nc.vector.tensor_copy(xp[b][:, :, D:ROW].bitcast(I32),
                                          ids[:, bass.ds((L // P) * b + ST * i, ST)].unsqueeze(2))\
                      .then_inc(id_made[b], 1)

            input_stats(0)
            input_normal(0)
            dve.wait_ge(setup_pe, 3)
            for m in range(4):
                link(nc.vector.tensor_copy(wqk[:, m, :, :].rearrange("p k d -> p (k d)"), pg[:, m, :]))
            nc.vector.memset(kT[0][:, 0, 3:4], 0.0).then_inc(setup_dve, 1)
            assert n == SETUP_LINKS, n
            for o in range(2):
                second_factor(0, 0, o)
            one_span(0, True, False)
            with dve.Fori(1, NSPAN - 1) as i:
                one_span(i, False, False)
            one_span(NSPAN - 1, False, True)
            dve.wait_ge(attn_loaded, 16 * 15)
            nc.vector.tensor_copy(wgu[:, :, :, M].rearrange("p e k -> p k e"), wr[:]).then_inc(router_cols, 1)

        @block.tensor
        def _(pe):
            pe.wait_ge(consts_made, 1)
            pe.wait_ge(setup_dve, 1)
            pe.wait_ge(attn_loaded, 16 * 15)
            nc.tensor.matmul(pg[:, 0, 0:69], rep16[:].rearrange("p h d -> p (h d)"), f4[:], start=True, stop=True)\
              .then_inc(setup_pe, 1)
            for n, bank in ((2, 2), (3, 3)):
                for k in range(KD):
                    for r in range(KD):
                        ins = nc.tensor.transpose(pg[:, bank, (k * KD + r) * P:(k * KD + r + 1) * P],
                                                  nat[:, n, r, k * P:(k + 1) * P], ident[:])
            pe.wait_ge(setup_dve, 2)
            for m in range(4):
                ins = nc.tensor.transpose(pg[:, 1, m * P:(m + 1) * P], gsb[:, m, :], ident[:])
            ins.then_inc(setup_pe, 1)
            pe.wait_ge(setup_dve, 3)
            for m in range(4):
                for k in range(KD):
                    for f in range(2):
                        ins = nc.tensor.matmul(pg[:, m, (k * 2 + f) * P:(k * 2 + f + 1) * P],
                                               nat[:, m // 2, f, k * P:(k + 1) * P], fmap[:, m, :],
                                               start=True, stop=True)
            ins.then_inc(setup_pe, 1)
            for b in range(B):
                nc.tensor.matmul(pkv[:, b, 0:2 * P], ident[:], zeros[:, 0:2 * P], start=True, stop=True)
            pe.wait_ge(setup_dve, 4)

            def turn(src, b, bank):
                for k in range(KD):
                    for t in range(ST):
                        ins = nc.tensor.transpose(pg[:, bank, k * SPAN + t * P:k * SPAN + (t + 1) * P],
                                                  src[b][:, t, k * P:(k + 1) * P], ident[:])
                return ins

            def turn_input(j):
                for b in range(B):
                    pe.wait_ge(xn_made[b], ST * j + ST)
                    turn(xn, b, 2 + b).then_inc(xt_turned[b], 1)

            def project(j, b, o):
                r = QK_ORDER[o]
                for m in range(2):
                    for k in range(KD):
                        ins = nc.tensor.matmul(pg[:, (r + 2) % 4, m * SPAN:(m + 1) * SPAN],
                                               wqk[:, 2 * (r // 2) + m, k, (r % 2) * P:(r % 2 + 1) * P],
                                               xnT[b][:, k, :], start=(k == 0), stop=(k == KD - 1))
                ins.then_inc(proj_ready[b], 1)

            def project_ahead(j):
                for b in range(B):
                    pe.wait_ge(xnT_made[b], j + 1)
                for o in range(2):
                    project(j, 0, o)

            def project_second(j, orders):
                for o in orders:
                    pe.wait_ge(q_made[0], 4 * j + o + 1)
                    project(j, 1, o)

            def scores(i, u):
                b, t = u % 2, u // 2
                pe.wait_ge(qz_made[b], (16 * i + 8 * t + 8, 10 * i + 8 * t + 2)[b])
                for f in range(2):
                    if u == 0:
                        for bb in range(B):
                            pe.wait_ge((vz_made, ktok_made)[f][bb], i + 1)
                    else:
                        pe.wait_ge(s_masked, 2 * UNITS * i + 2 * (u - 1) + f + 1)
                    for half in range(2):
                        ins = nc.tensor.matmul(pg[:, 2 * f + half, :], kT[b][:, f, t * P:(t + 1) * P],
                                               qz[u % 2][:, f, 4 * half:4 * half + 4, :].rearrange("p h m -> p (h m)"),
                                               start=True, stop=True)
                    ins.then_inc(s_ready, 1)

            def outputs(i, u):
                b, t = u % 2, u // 2
                if t == 0:
                    pe.wait_ge(oT_made[b], FREE + i)
                else:
                    pe.wait_ge(kvm_made[b], ST * i + t)
                    pe.wait_ge(sq_made, UNITS * i + u - 1)
                pe.wait_ge(s_masked, 2 * UNITS * i + 2 * u + 2)
                for f in range(2):
                    cols = slice(f * SPAN + t * P, f * SPAN + (t + 1) * P)
                    nc.tensor.matmul(po[:, b, cols], kvm[b][:, f, :], qT[b][:, f, t * P:(t + 1) * P],
                                     start=True, stop=False, skip_group_check=True)
                    for a in range(2):
                        for q in range(4):
                            ins = nc.tensor.matmul(
                                po[32 * q:32 * q + 32, b, cols],
                                vz[b][:, t, 4 * f + q, a:a + 2, :].rearrange("p a e -> p (a e)"),
                                sT[u % 2][:, 2 * f + q // 2, 2 * (q % 2) + a, :], start=False, stop=(a == 1 and q == 3),
                                skip_group_check=True)
                ins.then_inc(o_ready[b], 1)

            def mean_squares(i, u):
                b, t = u % 2, u // 2
                pe.wait_ge(sq_made, UNITS * i + u + 1)
                if u:
                    pe.wait_ge(ostd_made, UNITS * i + u)
                else:
                    pe.wait_ge(rank_read, FREE + i)
                nc.tensor.matmul(pr[:, 0:2 * P], hmean[:], sq[b][:, :, t * P:(t + 1) * P],
                                 start=True, stop=True).then_inc(ms_ready, 1)

            def add_state(i, u):
                b, t = u % 2, u // 2
                if u:
                    pe.wait_ge(kvm_made[1 - b], ST * i + (t + b))
                for f in range(2):
                    ins = nc.tensor.matmul(pkv[:, b, f * P:(f + 1) * P], ktok[b][:, t, f, :],
                                           vz[b][:, t, 4 * f:4 * f + 4, 0:3:2, :],
                                           start=False, stop=True, skip_group_check=True)
                ins.then_inc(kv_ready[b], 1)

            def one_span(i, first, last):
                for b in range(B):
                    pe.wait_ge(x2nT_made[b], FREE + i)
                for o in range(2, 4):
                    project(i, 0, o)
                project_second(i, range(2, 4))
                for b in range(B):
                    pe.wait_ge(q_made[1], 4 * i + b + 1)
                    for t in range(ST):
                        for k in range(KD):
                            ins = nc.tensor.matmul(pg[:, b, t * D:(t + 1) * D], xnT[b][:, k, t * P:(t + 1) * P],
                                                   wvT[:, k, :], start=(k == 0), stop=(k == KD - 1))
                    ins.then_inc(v_ready[b], 1)
                for b in range(B):
                    pe.wait_ge(q_made[1], 4 * i + b + 3)
                    for t in range(ST):
                        for f in range(2):
                            ins = nc.tensor.transpose(pg[:, 2 + b, (2 * t + f) * P:(2 * t + f + 1) * P],
                                                      kT[b][:, f, t * P:(t + 1) * P], ident[:])
                    ins.then_inc(kt_ready[b], 1)
                scores(i, 0)
                if not first:
                    rank(nc, pe, R, pr, i - 1)
                for u in range(UNITS):
                    if u + 1 < UNITS:
                        scores(i, u + 1)
                    outputs(i, u)
                    add_state(i, u)
                    if u:
                        mean_squares(i, u - 1)
                if not last:
                    turn_input(i + 1)
                mean_squares(i, UNITS - 1)
                if not last:
                    project_ahead(i + 1)
                for b in range(B):
                    pe.wait_ge(oT_made[b], FREE + i + 1)
                    if not last:
                        pe.wait_ge(xnT_made[b], i + 2)
                    for t in range(ST):
                        for f in range(2):
                            ins = nc.tensor.matmul(pg[:, 2 + b, t * D:(t + 1) * D], oT[b][:, f, t * P:(t + 1) * P],
                                                   woT[:, f, :], start=(f == 0), stop=(f == 1))
                    ins.then_inc(y_ready[b], 1)
                if not last:
                    project_second(i + 1, range(2))
                for b in range(B):
                    pe.wait_ge(xp_made[b], ST * i + ST)
                    turn(xp, b, 2 + b).then_inc(x2t_turned[b], 1)
                for b in range(B):
                    pe.wait_ge(x2nT_made[b], FREE + i + 1)
                    for t in range(ST):
                        for k in range(KD):
                            n = b * ST + t
                            ins = nc.tensor.matmul(pr[:, 2 * P + n * E:2 * P + (n + 1) * E],
                                                   x2nT[b][:, k, t * P:(t + 1) * P],
                                                   wr[:, k, :], start=(k == 0), stop=(k == KD - 1))
                ins.then_inc(logit_ready, 1)

            turn_input(0)
            project_ahead(0)
            project_second(0, range(2))
            one_span(0, True, False)
            with pe.Fori(1, NSPAN - 1) as i:
                one_span(i, False, False)
            one_span(NSPAN - 1, False, True)


def phase_b(nc, ctx, sb, sem, sems, g):
    rows_d, x2nT_d, acc_d = (g[k] for k in ("rows_d", "x2nT_d", "acc_d"))
    ident, wgu, shg, shu, shd, next_row, first_row, zeros, part_f = (
        g[k] for k in ("ident", "wgu", "shg", "shu", "shd", "next_row", "first_row", "zeros", "part_f"))
    with ExitStack() as own:
        def t1(name, shape, dt=F32):
            return sb(name, shape, dt, own)

        wd = t1("wd", [P, E, 2, D])
        pad_row = t1("pad_row", [P, ROW])
        pad_slots = t1("pad_slots", [P, E + 1], U32)
        pad_f = t1("pad_f", [P, E + 1])
        jj_i = t1("jj_i", [P, 2], I32)
        jj = t1("jj", [P, 2])
        cnt = t1("cnt", [P, E])
        cnt_i = t1("cnt_i", [P, E], I32)
        tiles_of = t1("tiles_of", [P, E])
        tile_end = t1("tile_end", [P, E])
        onesE = t1("onesE", [P, E])
        before = t1("before", [P, 2, E])
        started = t1("started", [P, 2, E])
        expert = t1("expert", [P, 2])
        tile_at = t1("tile_at", [P, 2])
        inside = t1("inside", [P, 2])
        table = t1("table", [P, 4])
        table_i = t1("table_i", [1, 4, P], I32)
        xe = [t1(f"xe{s}", [P, ROW]) for s in range(SLOTS)]
        ys = t1("ys", [P, 4, D])
        shared = ExitStack()

        def t3(name, shape):
            return sb(name, shape, F32, shared)

        xs = [g["xs0"], t3("xs1", [P, KD, SP_TOK])]
        sig = [t3(f"sig{s}", [P, SP_TOK]) for s in range(2)]
        sgu = sig
        hs_own = [t3(f"hs0_{s}", [P, SP_TOK]) for s in range(2)]
        hs_both = [t3(f"hs{n}", [P, SP_TOK]) for n in range(1, 3)]
        hs = [[hs_own[s], *hs_both] for s in range(2)]

        pb = own.enter_context(nc.psum_tensor("pb", [P, 8, 512], F32))

        down_loaded = sem("down_loaded")
        row_loaded = sems("row_loaded", SLOTS)
        pool_step = sem("pool_step")
        pad_made = sem("pad_made")
        padded = sem("padded")
        table_step = sem("table_step")
        table_made = sem("table_made")
        table_turned = sem("table_turned")
        table_ready = sem("table_ready")
        xs_loaded, sh_stored = g["xs_loaded"], sems("sh_stored")
        gate_ready, sig_made, sgu_made, hs_made, sh_y_ready, ys_made = (
            sems(n) for n in ("gate_ready", "sig_made", "sgu_made", "hs_made", "sh_y_ready", "ys_made"))

        FT = [(0, P), (P, P), (2 * P, MS - 2 * P)]
        NSH = T // SP_TOK
        STEPS = NSH // 2
        R = g["route"]

        def before_it(i, s):
            return (i, 0) if s else (i - 1, 1)

        block = shared.enter_context(nc.Block())

        @block.sync
        def _(sp):
            def load(i, s):
                at = (2 * i + s) * SP_TOK
                sp.dma_start(xs[s][:], x2nT_d[:, :, bass.ds(at, SP_TOK)]).then_inc(xs_loaded[s], 16)

            def store(i, s):
                sp.wait_ge(ys_made[s], FREE + 2 * i + 2)
                sp.dma_start(acc_d[0][bass.ds((2 * i + s) * SP_TOK, SP_TOK), :].rearrange("(t p) d -> p t d", p=P),
                             ys[:]).then_inc(sh_stored[s], 16)

            load(0, 1)
            with sp.Fori(0, STEPS - 1) as i:
                for s in range(2):
                    store(i, s)
                    load(i + 1, s)
            store(STEPS - 1, 0)
            sp.wait_ge(table_ready, 1)
            for b in range(B):
                sp.wait_ge(R["scattered"][b], 16 * ST * TOPK * NSPAN)
            sp.wait_ge(padded, 16 * (E + 1))
            for s in range(SLOTS):
                row = sp.value_load(table_i[0:1, 0, s:s + 1], min_val=0, max_val=NROWS - P)
                sp.dma_start(xe[s][:], rows_d[bass.ds(row, P), :]).then_inc(row_loaded[s], 16)
            store(STEPS - 1, 1)

        @block.scalar
        def _(act):
            act.wait_ge(g["sh_loaded"], 64)

            def one_body(i, first):
                for s in range(2):
                    for n, (f0, fn) in enumerate(FT):
                        u = (3 * s + n) // 2
                        q = (3 * s + n) % 2
                        act.wait_ge(gate_ready[q], 3 * i + u + 1)
                        nc.scalar.activation(sig[q][0:fn, :], pb[0:fn, 2 * q, :], ACT.Sigmoid).then_inc(sig_made[q], 1)
                        if first and s == 0 and n < 2:
                            act.wait_ge(xs_loaded[n], 16)
                            act.dma_start(wd[0:MH, :, n, :], g["down_w"][:, n * MH:(n + 1) * MH, :].rearrange(
                                "e p d -> p e d")).then_inc(down_loaded, 16)

            one_body(0, True)
            with act.Fori(1, STEPS) as i:
                one_body(i, False)
            act.wait_ge(down_loaded, 32)

        @block.gpsimd
        def _(pool):
            for free in (*sh_stored, *hs_made, *sh_y_ready, *ys_made):
                pool.sem_inc(free, FREE)
            n = 0

            def link(ins):
                nonlocal n
                n += 1
                ins.then_inc(pool_step, 1)
                pool.wait_ge(pool_step, n)

            link(pool.memset(pad_row[:], 0.0))
            link(pool.iota(pad_row[:, D:ROW].bitcast(I32), pattern=[[0, 1]], base=T, channel_multiplier=1))
            link(pool.iota(jj_i[:], pattern=[[P, 2]], base=0, channel_multiplier=1))
            link(pool.memset(onesE[:], 1.0))
            dispatch(pool, R, NSPAN - 1)
            pool.wait_ge(pad_made, 1)
            for e in range(E + 1):
                pool.indirect_dma_start(rows_d[:, :], bass.IndirectOffsetOnAxis(ap=pad_slots[:, e:e + 1], axis=0),
                                        pad_row[:], None).then_inc(padded, 16)
            pool.wait_ge(padded, 16 * (E + 1))
            for b in range(B):
                pool.wait_ge(R["scattered"][b], 16 * ST * TOPK * NSPAN)

        @block.vector
        def _(dve):
            n = 0

            def link(ins):
                nonlocal n
                n += 1
                ins.then_inc(table_step, 1)
                dve.wait_ge(table_step, n)

            def make_table():
                link(nc.vector.tensor_scalar(pad_f[:, 0:E], next_row[:], part_f[:, 0:1], -1.0, ALU.add, ALU.add))
                link(nc.vector.tensor_scalar(pad_f[:, E:E + 1], part_f[:], float(E * REGION), None, ALU.add))
                nc.vector.tensor_copy(pad_slots[:], pad_f[:]).then_inc(pad_made, 1)
                dve.wait_ge(pool_step, 4)
                link(nc.vector.tensor_tensor(cnt[:], next_row[:], first_row[:], ALU.subtract))
                link(nc.vector.tensor_scalar(cnt_i[:], cnt[:], float(P - 1), None, ALU.add))
                link(nc.vector.tensor_scalar(cnt_i[:], cnt_i[:], 7, None, ALU.logical_shift_right))
                link(nc.vector.tensor_copy(tiles_of[:], cnt_i[:]))
                link(nc.vector.tensor_tensor_scan(tile_end[:], onesE[:], tiles_of[:], 0.0, ALU.mult, ALU.add))
                link(nc.vector.tensor_copy(jj[:], jj_i[:]))
                link(nc.vector.tensor_tensor(before[:], bc(tile_end[:], 1, 2), bc(jj[:], 2, E), ALU.is_le))
                link(nc.vector.tensor_reduce(expert[:], before[:], AX_X, ALU.add))
                link(nc.vector.tensor_tensor(started[:], before[:], bc(tiles_of[:], 1, 2), ALU.mult))
                link(nc.vector.tensor_reduce(tile_at[:], started[:], AX_X, ALU.add))
                link(nc.vector.tensor_tensor(tile_at[:], jj[:], tile_at[:], ALU.subtract))
                link(nc.vector.tensor_scalar(inside[:], expert[:], float(E) - 0.5, float(P), ALU.is_lt, ALU.mult))
                link(nc.vector.tensor_tensor(tile_at[:], tile_at[:], inside[:], ALU.mult))
                link(nc.vector.scalar_tensor_tensor(out=table[:, 0:2], in0=expert[:], scalar=float(REGION),
                                                    in1=tile_at[:],
                                                    op0=ALU.mult, op1=ALU.add))
                link(nc.vector.tensor_scalar(table[:, 2:4], expert[:], float(E - 1), None, ALU.min))
                nc.vector.memset(cnt[:, 0:1], 0.0).then_inc(table_made, 1)

            def read_table():
                dve.wait_ge(table_turned, 1)
                nc.vector.tensor_copy(table_i[:].rearrange("p n t -> p (n t)"), pb[0:1, 7, :]).then_inc(table_ready, 1)

            def hidden(i, s, n):
                f0, fn = FT[n]
                u = (3 * s + n) // 2
                q = (3 * s + n) % 2
                dve.wait_ge(sig_made[q], 3 * i + u + 1)
                nc.vector.tensor_tensor(sgu[q][0:fn, :], pb[0:fn, 2 * q, :], sig[q][0:fn, :], ALU.mult)\
                  .then_inc(sgu_made[q], 1)
                dve.wait_ge(sgu_made[q], 3 * i + u + 1)
                if n == 0:
                    dve.wait_ge(sh_y_ready[s], FREE + i)
                else:
                    dve.wait_ge(sh_y_ready[1 - s], FREE + i + s)
                nc.vector.tensor_tensor(hs[s][n][0:fn, :], pb[0:fn, 2 * q + 1, :], sgu[q][0:fn, :], ALU.mult)\
                  .then_inc(hs_made[q], 1)

            def take_output(i, s):
                dve.wait_ge(sh_y_ready[s], FREE + i + 1)
                dve.wait_ge(sh_stored[1 - s], FREE + 16 * (i + s))
                for half in range(2):
                    nc.vector.tensor_copy(ys[:, 2 * half:2 * half + 2, :],
                                          pb[:, 4 + half, :].rearrange("p (t d) -> p t d", t=2)).then_inc(ys_made[s], 1)

            group_scores, pick_groups, pick_experts, find_rows = routing(nc, dve, R, pb[:, 6, :], NSPAN - 1)
            hidden(0, 0, 0)
            group_scores()
            hidden(0, 0, 1)
            pick_groups()
            hidden(0, 0, 2)
            pick_experts()
            hidden(0, 1, 0)
            find_rows()
            take_output(0, 0)
            hidden(0, 1, 1)
            make_table()
            hidden(0, 1, 2)
            read_table()
            with dve.Fori(1, STEPS) as i:
                for s in range(2):
                    hidden(i, s, 0)
                    take_output(*before_it(i, s))
                    for n in range(1, 3):
                        hidden(i, s, n)
            take_output(STEPS - 1, 1)

        @block.tensor
        def _(pe):
            def gate_up(i, s, n):
                f0, fn = FT[n]
                u = (3 * s + n) // 2
                q = (3 * s + n) % 2
                pe.wait_ge(hs_made[q], FREE + 3 * i + u)
                for w, bank in ((shg, 2 * q), (shu, 2 * q + 1)):
                    for k in range(KD):
                        ins = nc.tensor.matmul(pb[0:fn, bank, :], w[:, k, f0:f0 + fn], xs[s][:, k, :],
                                               start=(k == 0), stop=(k == KD - 1))
                ins.then_inc(gate_ready[q], 1)

            def down(i, s):
                for q in range(2):
                    pe.wait_ge(hs_made[q], FREE + 3 * i + (3 * s + 3 + 1 - q) // 2)
                if s == 0:
                    pe.wait_ge(ys_made[1], FREE + 2 * i)
                else:
                    pe.wait_ge(ys_made[0], FREE + 2 * i + 2)
                for t in range(4):
                    for n, (f0, fn) in enumerate(FT):
                        ins = nc.tensor.matmul(pb[:, 4 + t // 2, (t % 2) * D:(t % 2 + 1) * D],
                                               hs[s][n][0:fn, t * P:(t + 1) * P], shd[0:fn, n, :],
                                               start=(n == 0), stop=(n == 2))
                ins.then_inc(sh_y_ready[s], 1)

            pe.wait_ge(g["sh_loaded"], 64)
            pe.wait_ge(xs_loaded[0], 16)
            for n in range(3):
                gate_up(0, 0, n)
            pe.wait_ge(xs_loaded[1], 16)
            gate_up(0, 1, 0)
            rank(nc, pe, R, pb[:, 6, :], NSPAN - 1)
            down(0, 0)
            gate_up(0, 1, 1)
            gate_up(0, 1, 2)
            pe.wait_ge(table_made, 1)
            for n in range(4):
                ins = nc.tensor.transpose(pb[0:1, 7, n * P:(n + 1) * P], table[:, n:n + 1], ident[:])
            ins.then_inc(table_turned, 1)
            with pe.Fori(1, STEPS) as i:
                for s in range(2):
                    pe.wait_ge(xs_loaded[s], 16 * i + 16)
                    gate_up(i, s, 0)
                    down(*before_it(i, s))
                    gate_up(i, s, 1)
                    gate_up(i, s, 2)
            down(STEPS - 1, 1)

        shared.close()
        phase_c(nc, sb, sem, sems, g, wd, table_i, xe, row_loaded, pb, sh_stored, FREE + 16 * STEPS)


def phase_c(nc, sb, sem, sems, g, wd, table_i, xe, row_loaded, pb, sh_stored, all_stored):
    rows_d, acc_d, ident, wgu = (g[k] for k in ("rows_d", "acc_d", "ident", "wgu"))
    passed = g["passed"]
    out = g["out"].rearrange("b l d -> (b l) d")
    with ExitStack() as own:
        def ring(name, n, shape):
            return [sb(f"{name}{s}", shape, F32, own) for s in range(n)]

        xeT = ring("xeT", 2, [P, KD, P])
        sg = ring("sg", 2, [P, M + 1])
        hg = ring("hg", 2, [P, M])
        h = ring("h", 2, [P, M])
        hT = ring("hT", 2, [MH, 2, P])
        ye = ring("ye", SLOTS, [P, D])
        token = [sb(f"token{s}", [P, 1], U32, own) for s in range(SLOTS)]
        room = wgu[:].rearrange("p e k c -> p (e k c)")[:, 0:2 * SUMS * 4 * D].rearrange(
            "p (n s t d) -> p n s t d", n=2, s=SUMS, t=4)
        s0, s1 = ([room[:, n, s, :, :] for s in range(SUMS)] for n in range(2))

        added = sems("added", SLOTS)
        x_turned, xeT_made, gu_ready, sg_made, hg_made, h_made, h_turned, hT_made, ye_ready, ye_made = (
            sems(n) for n in ("e_x_turned", "xeT_made", "gu_ready", "sg_made", "hg_made", "h_made", "h_turned",
                              "hT_made", "ye_ready", "ye_made"))
        sums_loaded, so_made, so_stored = (sems(n, SUMS) for n in ("sums_loaded", "so_made", "so_stored"))

        ROUNDS = NT // UNROLL
        flat = table_i[:].rearrange("o n t -> o (n t)")

        def use(r, s):
            return (UNROLL // 2) * r + s // 2

        def held(r, s):
            return (UNROLL // SLOTS) * r + s // SLOTS

        def off(r, s, n):
            return r + (s + n) // UNROLL, (s + n) % UNROLL

        with nc.Block() as block:

            @block.sync
            def _(sp):
                def one_round(r, first):
                    for s in range(SLOTS if first else 0, UNROLL):
                        row = sp.value_load(flat[0:1, bass.ds(UNROLL * r + s, 1)], min_val=0, max_val=NROWS - P)
                        z = s % SLOTS
                        apart(sp, h_made[s % 2], use(*off(r, s, -SLOTS)) + 1, passed)
                        sp.dma_start(xe[z][:], rows_d[bass.ds(row, P), :]).then_inc(row_loaded[z], 16)

                one_round(0, True)
                with sp.Fori(1, ROUNDS) as r:
                    one_round(r, False)
                for z in range(SLOTS):
                    sp.wait_ge(added[z], 16 * (NT // SLOTS))
                with sp.Fori(0, T // SP_TOK // SUMS) as i:
                    for s in range(SUMS):
                        sp.wait_ge(so_stored[s], FREE + 16 * i)
                        for n, dst in enumerate((s0, s1)):
                            sp.dma_start(dst[s], acc_d[n][bass.ds((SUMS * i + s) * SP_TOK, SP_TOK), :].rearrange(
                                "(t p) d -> p t d", p=P)).then_inc(sums_loaded[s], 16)

            @block.gpsimd
            def _(pool):
                for free in so_stored:
                    pool.sem_inc(free, FREE)
                for s in range(2):
                    pool.wait_ge(sh_stored[s], all_stored)

                def one_round(r, first):
                    for s in range(UNROLL):
                        z = s % SLOTS
                        if not (first and s < 2):
                            apart(pool, added[(s - 2) % SLOTS], 16 * held(*off(r, s, -2)) + 16, passed)
                        apart(pool, ye_made[s % 2], use(r, s) + 1, passed)
                        pool.indirect_dma_start(
                            acc_d[s % 2][:, :],
                            bass.IndirectOffsetOnAxis(ap=token[z][:], axis=0),
                            ye[z][:], None, compute_op=ALU.add).then_inc(added[z], 16)

                one_round(0, True)
                with pool.Fori(1, ROUNDS) as r:
                    one_round(r, False)

            @block.scalar
            def _(act):
                def turned_in(r, s):
                    p = s % 2
                    act.wait_ge(x_turned[p], use(r, s) + 1)
                    nc.scalar.activation(xeT[p][:].rearrange("p k t -> p (k t)"), pb[:, p, 0:2 * P], ACT.Copy)\
                      .then_inc(xeT_made[p], 1)

                def hidden_turned(r, s):
                    p = s % 2
                    act.wait_ge(h_turned[p], use(r, s) + 1)
                    nc.scalar.activation(hT[p][:].rearrange("p k t -> p (k t)"), pb[0:MH, 4 + p, 0:2 * P], ACT.Copy)\
                      .then_inc(hT_made[p], 1)

                def one_round(r, first, last):
                    for s in range(UNROLL):
                        p = s % 2
                        act.wait_ge(gu_ready[p], use(r, s) + 1)
                        nc.scalar.activation(sg[p][:], pb[:, 2 + p, 0:M + 1], ACT.Sigmoid).then_inc(sg_made[p], 1)
                        if not (last and s == UNROLL - 1):
                            turned_in(*off(r, s, 1))
                        if not (first and s == 0):
                            hidden_turned(*off(r, s, -1))

                turned_in(0, 0)
                one_round(0, True, False)
                with act.Fori(1, ROUNDS - 1) as r:
                    one_round(r, False, False)
                one_round(ROUNDS - 1, False, True)
                hidden_turned(ROUNDS - 1, UNROLL - 1)
                with act.Fori(0, T // SP_TOK // SUMS) as i:
                    for s in range(SUMS):
                        act.wait_ge(so_made[s], i + 1)
                        act.dma_start(out[bass.ds((SUMS * i + s) * SP_TOK, SP_TOK), :].rearrange(
                            "(t p) d -> p t d", p=P), s0[s]).then_inc(so_stored[s], 16)
                for s in range(SUMS):
                    act.wait_ge(so_stored[s], FREE + 16 * (T // SP_TOK // SUMS))

            @block.vector
            def _(dve):
                def taken(r, s):
                    z = s % SLOTS
                    dve.wait_ge(ye_ready[s % 2], use(r, s) + 1)
                    dve.wait_ge(added[z], 16 * held(r, s))
                    nc.vector.tensor_copy(ye[z][:], pb[:, 6 + s % 2, 0:D]).then_inc(ye_made[s % 2], 1)

                def one_round(r, first):
                    for s in range(UNROLL):
                        p = s % 2
                        dve.wait_ge(sg_made[p], use(r, s) + 1)
                        z = s % SLOTS
                        dve.wait_ge(row_loaded[z], 16 * held(r, s) + 16)
                        dve.wait_ge(added[z], 16 * held(r, s))
                        nc.vector.tensor_copy(token[z][:], xe[z][:, D:ROW].bitcast(U32))
                        nc.vector.tensor_tensor(hg[p][:], pb[:, 2 + p, 0:M], sg[p][:, 0:M], ALU.mult)\
                          .then_inc(hg_made[p], 1)
                        dve.wait_ge(hg_made[p], use(r, s) + 1)
                        nc.vector.scalar_tensor_tensor(out=h[p][:], in0=hg[p][:], scalar=sg[p][:, M:M + 1],
                                                       in1=pb[:, 2 + p, M + 1:WIDE], op0=ALU.mult, op1=ALU.mult)\
                          .then_inc(h_made[p], 1)
                        if not (first and s < 2):
                            taken(*off(r, s, -2))

                one_round(0, True)
                with dve.Fori(1, ROUNDS) as r:
                    one_round(r, False)
                for s in range(UNROLL - 2, UNROLL):
                    taken(ROUNDS - 1, s)
                with dve.Fori(0, T // SP_TOK // SUMS) as i:
                    for s in range(SUMS):
                        dve.wait_ge(sums_loaded[s], 32 * i + 32)
                        nc.vector.tensor_tensor(s0[s], s0[s], s1[s], ALU.add).then_inc(so_made[s], 1)

            @block.tensor
            def _(pe):
                def turn_rows(r, s):
                    p = s % 2
                    z = s % SLOTS
                    pe.wait_ge(row_loaded[z], 16 * held(r, s) + 16)
                    pe.wait_ge(xeT_made[p], use(r, s))
                    for k in range(KD):
                        ins = nc.tensor.transpose(pb[:, p, k * P:(k + 1) * P], xe[z][:, k * P:(k + 1) * P], ident[:])
                    ins.then_inc(x_turned[p], 1)

                def expert_of(r, s):
                    return pe.value_load(flat[0:1, bass.ds(2 * P + UNROLL * r + s, 1)], min_val=0, max_val=E - 1)

                def gate_up(r, s, e):
                    p = s % 2
                    pe.wait_ge(xeT_made[p], use(r, s) + 1)
                    pe.wait_ge(h_made[p], use(r, s))
                    for k in range(KD):
                        ins = nc.tensor.matmul(pb[:, 2 + p, 0:WIDE], xeT[p][:, k, :],
                                               wgu[:, bass.ds(e, 1), k, :].rearrange("p o c -> p (o c)"),
                                               start=(k == 0), stop=(k == KD - 1))
                    ins.then_inc(gu_ready[p], 1)

                def down(r, s, e):
                    p = s % 2
                    pe.wait_ge(hT_made[p], use(r, s) + 1)
                    pe.wait_ge(ye_made[p], use(r, s))
                    for k in range(2):
                        ins = nc.tensor.matmul(pb[:, 6 + p, 0:D], hT[p][:, k, :],
                                               wd[0:MH, bass.ds(e, 1), k, :].rearrange("p o d -> p (o d)"),
                                               start=(k == 0), stop=(k == 1))
                    ins.then_inc(ye_ready[p], 1)

                def turn_hidden(r, s):
                    p = s % 2
                    pe.wait_ge(h_made[p], use(r, s) + 1)
                    pe.wait_ge(hT_made[p], use(r, s))
                    for k in range(2):
                        ins = nc.tensor.transpose(pb[0:MH, 4 + p, k * P:(k + 1) * P],
                                                  h[p][:, k * MH:(k + 1) * MH], ident[:])
                    ins.then_inc(h_turned[p], 1)

                def one_round(r, first=False, last=False):
                    known = {}
                    for s in range(UNROLL + 2 * last):
                        if s < UNROLL:
                            if s == 0:
                                known[s] = expert_of(r, s)
                            gate_up(r, s, known[s])
                        if not last or s < UNROLL - 1:
                            turn_rows(*off(r, s, 1))
                        if s <= UNROLL and not (first and s == 0):
                            turn_hidden(*off(r, s, -1))
                        done = off(r, s, -2)
                        if s < 2 and not first:
                            known[s - 2] = expert_of(*done)
                        if s + 1 < UNROLL:
                            known[s + 1] = expert_of(r, s + 1)
                        if s - 2 in known:
                            down(*done, known[s - 2])

                turn_rows(0, 0)
                one_round(0, first=True)
                with pe.Fori(1, ROUNDS - 1) as r:
                    one_round(r)
                one_round(ROUNDS - 1, last=True)


_INS = ['L0_attn_x', 'L0_attn_wq', 'L0_attn_wk', 'L0_attn_wv', 'L0_attn_wo', 'L0_attn_fq1_w', 'L0_attn_fq1_b',
        'L0_attn_fq2_w', 'L0_attn_fq2_b', 'L0_attn_fk1_w', 'L0_attn_fk1_b', 'L0_attn_fk2_w', 'L0_attn_fk2_b',
        'L0_attn_norm_w', 'L0_ffn_w_router', 'L0_ffn_corr_bias', 'L0_ffn_gate_w', 'L0_ffn_up_w', 'L0_ffn_down_w',
        'L0_ffn_sh_gate_w', 'L0_ffn_sh_up_w', 'L0_ffn_sh_down_w']


def kernel(**inputs):
    import concourse.bacc as bacc
    from concourse.bass_utils import run_bass_kernel_spmd

    nc = bacc.Bacc("TRN2", target_bir_lowering=False, num_devices=1)
    arrays, args = {}, []
    for name in _INS:
        a = np.ascontiguousarray(inputs[name])
        arrays[f"in_{name}"] = a
        args.append(nc.dram_tensor(f"in_{name}", a.shape, mybir.dt.from_np(a.dtype), kind="ExternalInput").ap())
    out = nc.dram_tensor("out_0", (B, L, D), F32, kind="ExternalOutput").ap()
    moe_block_kernel(nc, *args, out)
    r = run_bass_kernel_spmd(nc, [arrays], core_ids=[0])
    return r.results[0]["out_0"]
```
